# Optimizing a Trainium2 kernel written in Bass

```python
import numpy as np
import jax
import jax.numpy as jnp

def _softmax(x, axis=-1):
    return jax.nn.softmax(x, axis=axis)

def _gelu(x):
    return jax.nn.gelu(x, approximate=True)

def _silu(x):
    return jax.nn.silu(x)

def _sigmoid(x):
    return jax.nn.sigmoid(x)

def _layernorm(x, axis=-1, eps=1e-05):
    m = jnp.mean(x, axis=axis, keepdims=True)
    v = jnp.var(x, axis=axis, keepdims=True)
    return (x - m) / jnp.sqrt(v + eps)

def _scatter_add(tgt, idx, src, axis=0):
    return tgt.at[idx].add(src)

def _segment_sum(src, seg, n):
    return jax.ops.segment_sum(src, seg, n)
kernel_name = 'mk_gnn_ffn_d1_gnn_r32_eae445'

def setup_inputs(seed: int=0):
    np.random.seed(seed)
    _w = jnp.asarray

    def _rec_inputs():
        import jax
        import jax.numpy as jnp
        _gk = jax.random.key(seed)
        x = -0.0002117 + 1 * jax.random.normal(jax.random.fold_in(_gk, 1), (3125, 256), jnp.float32)
        src = jax.random.randint(jax.random.fold_in(_gk, 2), (50000,), 0, 3125, jnp.int32)
        dst = jnp.minimum((3125 * jax.random.uniform(jax.random.fold_in(_gk, 3), (50000,)) ** 2.0).astype(jnp.int32), 99999)
        _o = jnp.argsort(dst, stable=True)
        src = src[_o]
        dst = dst[_o]
        return (x, src, dst)
    x, src, dst = _rec_inputs()

    def _L0_gnn_setup():
        import jax, jax.numpy as jnp
        import numpy as np
        N_NODES = 3125
        N_EDGES = 9375
        D_MODEL = 256
        N_HEADS = 8
        D_HEAD = D_MODEL // N_HEADS

        def _layernorm(x, w, b, eps=1e-05):
            mu = jnp.mean(x, axis=-1, keepdims=True)
            var = jnp.var(x, axis=-1, keepdims=True)
            return (x - mu) * jax.lax.rsqrt(var + eps) * w + b
        key = jax.random.key(seed)
        ks = jax.random.split(key, 16)
        d, h = (D_MODEL, D_MODEL)
        s = 1.0 / np.sqrt(d)
        inp = {'x': jax.random.normal(ks[0], (N_NODES, d), dtype=jnp.float32), 'edge_index': jax.random.randint(ks[1], (2, N_EDGES), 0, N_NODES, dtype=jnp.int64), 'Wq': jax.random.normal(ks[2], (d, d), dtype=jnp.float32) * s, 'Wk': jax.random.normal(ks[3], (d, d), dtype=jnp.float32) * s, 'Wv': jax.random.normal(ks[4], (d, d), dtype=jnp.float32) * s, 'O_w': jax.random.normal(ks[5], (d, d), dtype=jnp.float32) * s, 'O_b': jnp.zeros((d,), dtype=jnp.float32), 'ln1_w': jnp.ones((d,), dtype=jnp.float32), 'ln1_b': jnp.zeros((d,), dtype=jnp.float32), 'f1_w': jax.random.normal(ks[6], (d, 2 * d), dtype=jnp.float32) * s, 'f1_b': jnp.zeros((2 * d,), dtype=jnp.float32), 'f2_w': jax.random.normal(ks[7], (2 * d, d), dtype=jnp.float32) / np.sqrt(2 * d), 'f2_b': jnp.zeros((d,), dtype=jnp.float32), 'ln2_w': jnp.ones((d,), dtype=jnp.float32), 'ln2_b': jnp.zeros((d,), dtype=jnp.float32), 'gru_w_ih': jax.random.normal(ks[8], (d, 3 * h), dtype=jnp.float32) * s, 'gru_w_hh': jax.random.normal(ks[9], (h, 3 * h), dtype=jnp.float32) * s, 'gru_b_ih': jnp.zeros((3 * h,), dtype=jnp.float32), 'gru_b_hh': jnp.zeros((3 * h,), dtype=jnp.float32)}
        return inp
    _L0_gnn_all = _L0_gnn_setup()
    _L0_gnn_in = {k: v for k, v in _L0_gnn_all.items() if k in ('Wq', 'Wk', 'Wv', 'O_w', 'O_b', 'ln1_w', 'ln1_b', 'f1_w', 'f1_b', 'f2_w', 'f2_b', 'ln2_w', 'ln2_b', 'gru_w_ih', 'gru_w_hh', 'gru_b_ih', 'gru_b_hh')}
    del _L0_gnn_all

    def _L0_ffn_setup():
        import jax, jax.numpy as jnp
        import numpy as np
        B, S, D, H, E, K = (8, 256, 256, 1024, 8, 2)
        key = jax.random.key(seed)
        ks = jax.random.split(key, 7)
        s_in = 1.0 / np.sqrt(D)
        s_hid = 1.0 / np.sqrt(H)
        return {'x': jax.random.normal(ks[0], (B, S, D), dtype=jnp.float32), 'Wg': jax.random.uniform(ks[1], (E, D), jnp.float32, -s_in, s_in), 'bg': jax.random.uniform(ks[2], (E,), jnp.float32, -s_in, s_in), 'W1': jax.random.uniform(ks[3], (E, H, D), jnp.float32, -s_in, s_in), 'b1': jax.random.uniform(ks[4], (E, H), jnp.float32, -s_in, s_in), 'W2': jax.random.uniform(ks[5], (E, D, H), jnp.float32, -s_hid, s_hid), 'b2': jax.random.uniform(ks[6], (E, D), jnp.float32, -s_hid, s_hid)}
    _L0_ffn_all = _L0_ffn_setup()
    _L0_ffn_in = {k: v for k, v in _L0_ffn_all.items() if k in ('Wg', 'bg', 'W1', 'b1', 'W2', 'b2')}
    del _L0_ffn_all
    return {'x': x, 'src': src, 'dst': dst, 'L0_gnn_Wq': _L0_gnn_in['Wq'], 'L0_gnn_Wk': _L0_gnn_in['Wk'], 'L0_gnn_Wv': _L0_gnn_in['Wv'], 'L0_gnn_O_w': _L0_gnn_in['O_w'], 'L0_gnn_O_b': _L0_gnn_in['O_b'], 'L0_gnn_ln1_w': _L0_gnn_in['ln1_w'], 'L0_gnn_ln1_b': _L0_gnn_in['ln1_b'], 'L0_gnn_f1_w': _L0_gnn_in['f1_w'], 'L0_gnn_f1_b': _L0_gnn_in['f1_b'], 'L0_gnn_f2_w': _L0_gnn_in['f2_w'], 'L0_gnn_f2_b': _L0_gnn_in['f2_b'], 'L0_gnn_ln2_w': _L0_gnn_in['ln2_w'], 'L0_gnn_ln2_b': _L0_gnn_in['ln2_b'], 'L0_gnn_gru_w_ih': _L0_gnn_in['gru_w_ih'], 'L0_gnn_gru_w_hh': _L0_gnn_in['gru_w_hh'], 'L0_gnn_gru_b_ih': _L0_gnn_in['gru_b_ih'], 'L0_gnn_gru_b_hh': _L0_gnn_in['gru_b_hh'], 'L0_ffn_Wg': _L0_ffn_in['Wg'], 'L0_ffn_bg': _L0_ffn_in['bg'], 'L0_ffn_W1': _L0_ffn_in['W1'], 'L0_ffn_b1': _L0_ffn_in['b1'], 'L0_ffn_W2': _L0_ffn_in['W2'], 'L0_ffn_b2': _L0_ffn_in['b2']}

def reference(x, src, dst, L0_gnn_Wq, L0_gnn_Wk, L0_gnn_Wv, L0_gnn_O_w, L0_gnn_O_b, L0_gnn_ln1_w, L0_gnn_ln1_b, L0_gnn_f1_w, L0_gnn_f1_b, L0_gnn_f2_w, L0_gnn_f2_b, L0_gnn_ln2_w, L0_gnn_ln2_b, L0_gnn_gru_w_ih, L0_gnn_gru_w_hh, L0_gnn_gru_b_ih, L0_gnn_gru_b_hh, L0_ffn_Wg, L0_ffn_bg, L0_ffn_W1, L0_ffn_b1, L0_ffn_W2, L0_ffn_b2):
    import jax
    import jax.numpy as jnp

    def _L0_gnn_ref(x, edge_index, Wq, Wk, Wv, O_w, O_b, ln1_w, ln1_b, f1_w, f1_b, f2_w, f2_b, ln2_w, ln2_b, gru_w_ih, gru_w_hh, gru_b_ih, gru_b_hh):
        import jax, jax.numpy as jnp
        import numpy as np
        N_NODES = 3125
        N_EDGES = 9375
        D_MODEL = 256
        N_HEADS = 8
        D_HEAD = D_MODEL // N_HEADS

        def _layernorm(x, w, b, eps=1e-05):
            mu = jnp.mean(x, axis=-1, keepdims=True)
            var = jnp.var(x, axis=-1, keepdims=True)
            return (x - mu) * jax.lax.rsqrt(var + eps) * w + b
        N = x.shape[0]
        H, D = (N_HEADS, D_HEAD)
        Q = (x @ Wq).reshape(N, H, D)
        K = (x @ Wk).reshape(N, H, D)
        V = (x @ Wv).reshape(N, H, D)
        score = jnp.einsum('nhd,ngd->nhg', Q, K) / np.sqrt(D)
        score = jax.nn.softmax(score, axis=-1)
        x1 = jnp.einsum('nhg,ngd->nhd', score, V).reshape(N, H * D)
        src, dst = (edge_index[0], edge_index[1])
        msg = x1[dst] * x1[src]
        attn_out = jax.ops.segment_sum(msg, dst, num_segments=N)
        h = attn_out @ O_w + O_b
        h = x + h
        h = _layernorm(h, ln1_w, ln1_b)
        ffn = jax.nn.relu(h @ f1_w + f1_b) @ f2_w + f2_b
        h = _layernorm(h + ffn, ln2_w, ln2_b)
        gi = h @ gru_w_ih + gru_b_ih
        gh = h @ gru_w_hh + gru_b_hh
        gi_r, gi_z, gi_n = jnp.split(gi, 3, axis=-1)
        gh_r, gh_z, gh_n = jnp.split(gh, 3, axis=-1)
        r = jax.nn.sigmoid(gi_r + gh_r)
        z = jax.nn.sigmoid(gi_z + gh_z)
        n = jnp.tanh(gi_n + r * gh_n)
        return (1.0 - z) * n + z * h

    def _L0_ffn_ref(x, Wg, bg, W1, b1, W2, b2):
        import jax, jax.numpy as jnp
        import numpy as np
        B, S, D, H, E, K = (8, 256, 256, 1024, 8, 2)
        gate_scores = jnp.einsum('bsd,ed->bse', x, Wg) + bg
        topk_scores, topk_idx = jax.lax.top_k(gate_scores, K)
        topk_probs = jax.nn.softmax(topk_scores, axis=-1)
        combine = jnp.sum(topk_probs[..., None] * jax.nn.one_hot(topk_idx, E, dtype=x.dtype), axis=-2)
        out = jnp.zeros_like(x)
        for e in range(E):
            h = jax.nn.relu(jnp.einsum('bsd,hd->bsh', x, W1[e]) + b1[e])
            y = jnp.einsum('bsh,dh->bsd', h, W2[e]) + b2[e]
            out = out + combine[..., e:e + 1] * y
        return out
    edge_index = jnp.stack([src, dst])
    x = x + _L0_gnn_ref(_layernorm(x, axis=-1), edge_index, L0_gnn_Wq, L0_gnn_Wk, L0_gnn_Wv, L0_gnn_O_w, L0_gnn_O_b, L0_gnn_ln1_w, L0_gnn_ln1_b, L0_gnn_f1_w, L0_gnn_f1_b, L0_gnn_f2_w, L0_gnn_f2_b, L0_gnn_ln2_w, L0_gnn_ln2_b, L0_gnn_gru_w_ih, L0_gnn_gru_w_hh, L0_gnn_gru_b_ih, L0_gnn_gru_b_hh)
    x = x + _L0_ffn_ref(_layernorm(x, axis=-1)[None], L0_ffn_Wg, L0_ffn_bg, L0_ffn_W1, L0_ffn_b1, L0_ffn_W2, L0_ffn_b2)[0]
    return x

_drawn_inputs = setup_inputs


def setup_inputs(seed=0):
    import zlib

    import numpy as np

    out = dict(_drawn_inputs(seed))
    spreads = {'L0_gnn_O_b': (0.0, 0.1),
     'L0_gnn_ln1_w': (1.0, 0.2),
     'L0_gnn_ln1_b': (0.0, 0.1),
     'L0_gnn_f1_b': (0.0, 0.1),
     'L0_gnn_f2_b': (0.0, 0.1),
     'L0_gnn_ln2_w': (1.0, 0.2),
     'L0_gnn_ln2_b': (0.0, 0.1),
     'L0_gnn_gru_b_ih': (0.0, 0.1),
     'L0_gnn_gru_b_hh': (0.0, 0.292)}
    factors = {'L0_ffn_b1': 7.961, 'L0_ffn_b2': 6.282}
    for name, (base, spread) in spreads.items():
        noise = np.random.default_rng([zlib.crc32(name.encode()), seed]).standard_normal(out[name].shape)
        drawn = base * np.exp(spread * noise) if base else spread * noise
        out[name] = jnp.asarray(drawn.astype(out[name].dtype))
    for name, factor in factors.items():
        out[name] = (out[name] * factor).astype(out[name].dtype)
    return out
```

```python
import concourse.bass as bass
from concourse import mybir
from contextlib import ExitStack

F32 = mybir.dt.float32
I32 = mybir.dt.int32
U32 = mybir.dt.uint32
ALU = mybir.AluOpType
ACT = mybir.ActivationFunctionType
AX = mybir.AxisListType

P = 128
NODES, EDGES, D = 3125, 50000, 256
HEADS = 8
DH = D // HEADS
TILES = -(-NODES // P)
NPAD = TILES * P
KC = D // P
GE = 4
GROUPS = -(-EDGES // (GE * P))
COLS = GROUPS * GE
EPS = 1e-5
SLOTS = 3
WINDOW = 2 * P
TILE_BITS = TILES.bit_length()
TILE_MAX = 1 << TILE_BITS
X_LOADS = 5
X_TILES = TILES // X_LOADS


def bcast(ap, axis, shape):
    return ap.unsqueeze(axis).broadcast_to(shape)


def attention_phase(nc, X, XN, X1, S, x_in, w_in, x1_dram, xs_dram, ys_dram, ins, keep):
    with ExitStack() as ctx:
        sb = lambda name, shape, dt=F32: ctx.enter_context(nc.sbuf_tensor("attn_" + name, shape, dt))
        sem = lambda name: ctx.enter_context(nc.semaphore("attn_" + name))
        psum = lambda name, shape: ctx.enter_context(nc.psum_tensor("attn_" + name, shape, F32))
        ident = keep["ident"]
        wqkv = sb("wqkv", [P, KC, 3 * D])
        xn = sb("xn", [P, SLOTS, D])
        xnT = sb("xnT", [P, SLOTS, KC, P])
        qkv = sb("qkv", [P, SLOTS, 3 * D])
        prod = sb("prod", [P, HEADS * HEADS, DH])
        vprod = sb("vprod", [P, SLOTS, HEADS, D])
        score = sb("score", [P, SLOTS, HEADS, HEADS])
        prob = sb("prob", [P, SLOTS, HEADS, HEADS])
        row = sb("row", [P, HEADS])
        stats = sb("stats", [P, TILES, 6])
        moments = sb("moments", [P, TILES, 2])
        std = sb("std", [P, TILES])
        rstd = sb("rstd", [P, TILES])
        xnT_ps = psum("xnT_ps", [P, 512])
        x1_ps = psum("x1_ps", [P, 512])
        qkv_ps = psum("qkv_ps", [P, SLOTS, 2, 512])

        x_loaded = [sem(f"x_loaded_{n}") for n in range(X_LOADS)]
        w_loaded, id_loaded = sem("w_loaded"), sem("id_loaded")
        var_ready, std_ready = sem("var_ready"), sem("std_ready")
        norm_ready, xnT_done, xnT_copied = sem("norm_ready"), sem("xnT_done"), sem("xnT_copied")
        qkv_done, qkv_copied = sem("qkv_done"), sem("qkv_copied")
        shifted, exped, prob_ready = sem("shifted"), sem("exped"), sem("prob_ready")
        vprod_ready, x1_ready, x1_stored = sem("vprod_ready"), sem("x1_ready"), sem("x1_stored")
        x1_summed = sem("x1_summed")
        bias_loaded, xn_kept = sem("bias_loaded"), sem("xn_kept")
        s_cleared, slots_cleared = sem("s_cleared"), sem("slots_cleared")
        fills = sum(-(-dram.shape[0] // P // TILES) for dram in (xs_dram, ys_dram))
        block = ctx.enter_context(nc.Block())

        def over_tiles(eng, step):
            for t in range(SLOTS):
                step(t, t, t)
            loops = TILES // SLOTS - 2
            with eng.Fori(0, loops) as k:
                for h in range(SLOTS):
                    step(k * SLOTS + SLOTS + h, h, SLOTS + h)
            for t in range((loops + 1) * SLOTS, TILES):
                step(t, t % SLOTS, t)

        @block.sync
        def _(sp):
            for n in range(X_LOADS):
                part = slice(n * X_TILES, (n + 1) * X_TILES)
                sp.dma_start(X[:, part, :], x_in[:, part, :]).then_inc(x_loaded[n], 16)
            sp.dma_start(ident[:, :], ins["ident"]).then_inc(id_loaded, 16)
            sp.dma_start(wqkv[:, :, :], w_in).then_inc(w_loaded, 16)
            sp.dma_start(keep["O_b"][:, :], ins["O_b"]).then_inc(bias_loaded, 16)

            def store(t, slot, n):
                sp.wait_ge(x1_ready, t + 1)
                sp.dma_start(x1_dram[bass.ds(t * P, P), :], X1[:, bass.ds(t, 1), :].rearrange("p a d -> p (a d)")).then_inc(x1_stored, 16)
            over_tiles(sp, store)
            sp.wait_ge(x1_stored, 16 * TILES)
            sp.wait_ge(slots_cleared, 16 * fills)

        @block.vector
        def _(dve):
            nc.vector.memset(S[:, :, :], 0.0).then_inc(s_cleared, 1)
            nc.vector.memset(keep["eps"][:, :], EPS)
            for n in range(X_LOADS):
                dve.wait_ge(x_loaded[n], 16)
                for t in range(n * X_TILES, (n + 1) * X_TILES):
                    nc.vector.bn_stats(stats[:, t, :], X[:, t, :])
            dve.drain()
            for t in range(TILES):
                nc.vector.bn_aggr(moments[:, t, :], stats[:, t, :])
            dve.drain().then_inc(var_ready, 1)
            dve.wait_ge(std_ready, 1)
            nc.vector.reciprocal(rstd[:, :], std[:, :])
            dve.drain()

            def norm(t, slot, n):
                if n >= SLOTS:
                    dve.wait_ge(xnT_done, t - SLOTS + 1)
                    dve.wait_ge(xn_kept, t - SLOTS + 1)
                nc.vector.tensor_scalar(xn[:, slot, :], X[:, bass.ds(t, 1), :].rearrange("p a d -> p (a d)"),
                                        moments[:, bass.ds(t, 1), 0:1].rearrange("p a d -> p (a d)"), rstd[:, bass.ds(t, 1)],
                                        ALU.subtract, ALU.mult).then_inc(norm_ready, 1)

            def step(t, slot, n):
                if n + 2 < TILES:
                    norm(t + 2, (slot + 2) % SLOTS, n + 2)
                dve.wait_ge(qkv_copied, t + 1)
                q = qkv[:, slot, 0:D].rearrange("p (h d) -> p h d", h=HEADS)
                k = qkv[:, slot, D:2 * D].rearrange("p (h d) -> p h d", h=HEADS)
                shape = [P, HEADS, HEADS, DH]
                nc.vector.tensor_tensor(prod[:, :, :].rearrange("p (h g) d -> p h g d", h=HEADS),
                                        bcast(q, 2, shape), bcast(k, 1, shape), ALU.mult)
                dve.drain()
                s = score[:, slot, :, :]
                nc.vector.tensor_reduce(s.rearrange("p h g -> p (h g)"), prod[:, :, :], AX.X, ALU.add)
                dve.drain()
                nc.vector.tensor_reduce(row[:, :], s, AX.X, ALU.max)
                dve.drain()
                nc.vector.tensor_tensor(s, s, bcast(row[:, :], 2, [P, HEADS, HEADS]), ALU.subtract).then_inc(shifted, 1)
                dve.wait_ge(exped, t + 1)
                nc.vector.tensor_reduce(row[:, :], prob[:, slot, :, :], AX.X, ALU.add)
                dve.drain()
                nc.vector.reciprocal(row[:, :], row[:, :])
                dve.drain()
                nc.vector.tensor_tensor(prob[:, slot, :, :], prob[:, slot, :, :], bcast(row[:, :], 2, [P, HEADS, HEADS]),
                                        ALU.mult).then_inc(prob_ready, 1)

            norm(0, 0, 0)
            norm(1, 1, 1)
            over_tiles(dve, step)

        @block.scalar
        def _(act):
            act.wait_ge(s_cleared, 1)
            for dram in (xs_dram, ys_dram):
                per = dram.shape[0] // P
                rows = dram.rearrange("(p r) d -> p r d", p=P)
                for r in range(0, per, TILES):
                    m = min(TILES, per - r)
                    act.dma_start(rows[:, r:r + m, :], S[:, 0:m, :]).then_inc(slots_cleared, 16)

            def copy_xnT(t, slot, n):
                act.wait_ge(xnT_done, t + 1)
                nc.scalar.activation(xnT[:, slot, :, :].rearrange("p c n -> p (c n)"), xnT_ps[:, 0:D], ACT.Copy).then_inc(xnT_copied, 1)

            def copy_qkv(t, slot, n):
                act.wait_ge(qkv_done, t + 1)
                if n >= SLOTS:
                    act.wait_ge(vprod_ready, t - SLOTS + 1)
                half = 3 * D // 2
                nc.scalar.activation(qkv[:, slot, 0:D], qkv_ps[:, slot, 0, 0:D], ACT.Copy, scale=float(DH) ** -0.5)
                nc.scalar.activation(qkv[:, slot, D:half], qkv_ps[:, slot, 0, D:half], ACT.Copy)
                nc.scalar.activation(qkv[:, slot, half:], qkv_ps[:, slot, 1, 0:half], ACT.Copy)
                act.drain().then_inc(qkv_copied, 1)

            def keep_x1(t):
                act.wait_ge(x1_summed, t + 1)
                nc.scalar.activation(X1[:, bass.ds(t, 1), :].rearrange("p a d -> p (a d)"), x1_ps[:, 0:D], ACT.Copy).then_inc(x1_ready, 1)

            def step(t, slot, n):
                if n + 2 < TILES:
                    copy_xnT(t + 2, (slot + 2) % SLOTS, n + 2)
                act.wait_ge(shifted, t + 1)
                nc.scalar.activation(prob[:, slot, :, :].rearrange("p h g -> p (h g)"),
                                     score[:, slot, :, :].rearrange("p h g -> p (h g)"), ACT.Exp).then_inc(exped, 1)
                if n + 1 < TILES:
                    copy_qkv(t + 1, (slot + 1) % SLOTS, n + 1)
                if n:
                    keep_x1(t - 1)

            act.wait_ge(var_ready, 1)
            nc.scalar.activation(std[:, :], moments[:, :, 1:2].rearrange("p t a -> p (t a)"), ACT.Sqrt, bias=keep["eps"][:, 0:1]).then_inc(std_ready, 1)
            copy_xnT(0, 0, 0)
            copy_xnT(1, 1, 1)
            copy_qkv(0, 0, 0)
            over_tiles(act, step)
            keep_x1(TILES - 1)

        @block.tensor
        def _(pe):
            pe.wait_ge(id_loaded, 16)
            pe.wait_ge(w_loaded, 16)

            def transpose_xn(t, slot, n):
                pe.wait_ge(norm_ready, t + 1)
                if n:
                    pe.wait_ge(xnT_copied, t)
                for c in range(KC):
                    mm = nc.tensor.transpose(xnT_ps[:, c * P:(c + 1) * P], xn[:, slot, c * P:(c + 1) * P], ident[:, :])
                mm.then_inc(xnT_done, 1)

            def project(t, slot, n):
                pe.wait_ge(xnT_copied, t + 1)
                if n >= SLOTS:
                    pe.wait_ge(qkv_copied, t - SLOTS + 1)
                for half in range(2):
                    for c in range(KC):
                        mm = nc.tensor.matmul(qkv_ps[:, slot, half, 0:3 * D // 2], xnT[:, slot, c, :],
                                              wqkv[:, c, half * 3 * D // 2:(half + 1) * 3 * D // 2],
                                              start=(c == 0), stop=(c == KC - 1))
                mm.then_inc(qkv_done, 1)

            def sum_values(t, slot, n):
                pe.wait_ge(vprod_ready, t + 1)
                if n:
                    pe.wait_ge(x1_ready, t)
                for g in range(HEADS):
                    mm = nc.tensor.matmul(x1_ps[:, 0:D], ident[:, :], vprod[:, slot, g, :], start=(g == 0), stop=(g == HEADS - 1))
                mm.then_inc(x1_summed, 1)

            def step(t, slot, n):
                if n + 1 < TILES:
                    project(t + 1, (slot + 1) % SLOTS, n + 1)
                if n + 2 < TILES:
                    transpose_xn(t + 2, (slot + 2) % SLOTS, n + 2)
                if n:
                    sum_values(t - 1, (slot + 2) % SLOTS, n - 1)

            transpose_xn(0, 0, 0)
            transpose_xn(1, 1, 1)
            project(0, 0, 0)
            over_tiles(pe, step)
            sum_values(TILES - 1, (TILES - 1) % SLOTS, TILES - 1)

        @block.gpsimd
        def _(pool):
            def keep_xn(t, slot, n):
                pool.wait_ge(norm_ready, t + 1)
                nc.gpsimd.tensor_tensor(tile_of(XN, t), xn[:, slot, :], keep["O_b"][:, :], ALU.add).then_inc(xn_kept, 1)

            pool.wait_ge(bias_loaded, 16)
            keep_xn(0, 0, 0)
            keep_xn(1, 1, 1)

            def step(t, slot, n):
                if n + 2 < TILES:
                    keep_xn(t + 2, (slot + 2) % SLOTS, n + 2)
                pool.wait_ge(prob_ready, t + 1)
                if n >= SLOTS:
                    pool.wait_ge(x1_summed, t - SLOTS + 1)
                shape = [P, HEADS, HEADS, DH]
                v = qkv[:, slot, 2 * D:3 * D].rearrange("p (g d) -> p g d", g=HEADS)
                nc.gpsimd.tensor_tensor(vprod[:, slot, :, :].rearrange("p g (h d) -> p g h d", h=HEADS),
                                        bcast(prob[:, slot, :, :].rearrange("p h g -> p g h"), 3, shape),
                                        bcast(v, 2, shape), ALU.mult).then_inc(vprod_ready, 1)
            over_tiles(pool, step)


GNN_KEPT = dict(O_w=[P, KC, D], f1_w=[P, KC, 2 * D], f2_w=[P, 2 * KC, D], w_ih=[P, KC, 3 * D], w_hh=[P, KC, 3 * D],
                f1_b=[P, 2 * KC], b_ih=[P, 3 * KC], b_hh=[P, 3 * KC],
                ln1_w=[P, D], ln1_b=[P, D], ln2_w=[P, D], ln2_b=[P, D], f2_b=[P, D])


def load_kept(eng, names, ins, keep, loaded):
    for name, shape in names.items():
        whole = tuple(slice(None) for _ in shape)
        eng.dma_start(keep[name][whole], ins[name]).then_inc(loaded, 16)
    eng.wait_ge(loaded, 16 * len(names))


def edge_phase(nc, S, x1_dram, src_in, dst_in, ins, keep):
    with ExitStack() as ctx:
        sb = lambda name, shape, dt=F32: ctx.enter_context(nc.sbuf_tensor("edge_" + name, shape, dt))
        sem = lambda name: ctx.enter_context(nc.semaphore("edge_" + name))
        src = sb("src", [P, COLS], I32)
        dst = sb("dst", [P, COLS], I32)
        dst_f = sb("dst_f", [P, COLS])
        iota_f = sb("iota_f", [P, NPAD + P])
        ends = sb("ends", [P, 2, GROUPS])
        ends_all = sb("ends_all", [P, 2, GROUPS])
        ends_i = sb("ends_i", [P, 2, GROUPS], I32)
        extra_f = sb("extra_f", [P, GROUPS])
        extra_i = sb("extra_i", [P, GROUPS], I32)
        scan = sb("scan", [P, 2, GROUPS])
        table = sb("table", [P, GROUPS], I32)
        index = sb("index", [P, SLOTS, GE], I32)
        rows = sb("rows", [P, SLOTS, GE, D])
        onehot = sb("onehot", [P, SLOTS, GE, WINDOW])
        part_ps = ctx.enter_context(nc.psum_tensor("edge_part_ps", [P, SLOTS, 512], F32))

        src_loaded, dst_loaded = sem("src_loaded"), sem("dst_loaded")
        iota_made, ends_made, ends_reduced = sem("iota_made"), sem("ends_made"), sem("ends_reduced")
        table_made = sem("table_made")
        index_made, index_seen = sem("index_made"), sem("index_seen")
        rows_loaded = [sem(f"rows_loaded_{s}") for s in range(SLOTS)]
        first_onehot, first_summed = sem("first_onehot"), sem("first_summed")
        more_onehot, more_summed = sem("more_onehot"), sem("more_summed")
        group_summed, kept_loaded = sem("group_summed"), sem("kept_loaded")
        block = ctx.enter_context(nc.Block())

        def over_groups(eng, step):
            for g in range(SLOTS):
                step(g, g, g)
            loops = GROUPS // SLOTS - 1
            with eng.Fori(0, loops - 1) as k:
                for h in range(SLOTS):
                    step(k * SLOTS + SLOTS + h, h, SLOTS + h)
            for g in range(loops * SLOTS, GROUPS):
                step(g, g % SLOTS, g)

        def within(value, greatest, why):
            return nc.s_assert_within(value, 0, greatest, skip_runtime_bounds_check_because=why)

        def unpack(eng, g):
            packed = eng.value_load(table[0:1, bass.ds(g, 1)], min_val=0, max_val=(1 << 31) - 1)
            tile = eng.snap(within(packed & (TILE_MAX - 1), TILES - 1, "a tile of nodes"))
            more = eng.snap((packed >> TILE_BITS) & (TILE_MAX - 1), min_val=0, max_val=TILES // 2)
            before = eng.snap(packed >> (2 * TILE_BITS), min_val=0, max_val=GROUPS * TILES // 2)
            return tile, more, before

        @block.sync
        def _(sp):
            sp.dma_start(dst[:, :], dst_in).then_inc(dst_loaded, 16)
            sp.dma_start(src[:, :], src_in).then_inc(src_loaded, 16)
            load_kept(sp, GNN_KEPT, ins, keep, kept_loaded)

        @block.gpsimd
        def _(pool):
            nc.gpsimd.iota(iota_f[:, :], [[1, NPAD + P]], base=0, channel_multiplier=0, allow_small_or_imprecise_dtypes=True).then_inc(iota_made, 1)
            pool.wait_ge(ends_made, 1)
            nc.gpsimd.partition_all_reduce(ends_all[:, :, :].rearrange("p a g -> p (a g)"), ends[:, :, :].rearrange("p a g -> p (a g)"),
                                           P, bass.bass_isa.ReduceOp.max).then_inc(ends_reduced, 1)
            pool.wait_ge(src_loaded, 16)

            def step(g, slot, n):
                if n >= SLOTS:
                    pool.wait_ge(group_summed, g - SLOTS + 1)
                nc.gpsimd.tensor_copy(index[:, slot, :], src[:, bass.ds(g * GE, GE)]).then_inc(index_made, 1)
                pool.wait_ge(index_made, g + 1)
                pool.sem_inc(index_seen, 1)
                for j in range(GE):
                    nc.gpsimd.indirect_dma_start(out=rows[:, slot, j, :], out_offset=None, in_=x1_dram,
                                                 in_offset=bass.IndirectOffsetOnAxis(ap=index[:, slot, j:j + 1].bitcast(U32), axis=0)).then_inc(rows_loaded[slot], 16)
            over_groups(pool, step)

        @block.vector
        def _(dve):
            dve.wait_ge(dst_loaded, 16)
            nc.vector.tensor_copy(dst_f[:, :], dst[:, :])
            dve.drain()
            by_group = dst_f[:, :].rearrange("p (g j) -> p g j", j=GE)
            nc.vector.tensor_reduce(ends[:, 0, :], by_group, AX.X, ALU.max)
            nc.vector.tensor_reduce(ends[:, 1, :], by_group, AX.X, ALU.min)
            dve.drain()
            nc.vector.tensor_scalar(ends[:, 1, :], ends[:, 1, :], -1.0, None, ALU.mult).then_inc(ends_made, 1)
            dve.wait_ge(iota_made, 1)
            dve.wait_ge(ends_reduced, 1)
            nc.vector.tensor_scalar(ends_all[:, 1, :], ends_all[:, 1, :], -1.0, None, ALU.mult)
            dve.drain()
            nc.vector.tensor_copy(ends_i[:, :, :], ends_all[:, :, :])
            dve.drain()
            nc.vector.tensor_scalar(ends_i[:, :, :], ends_i[:, :, :], P.bit_length() - 1, None, ALU.arith_shift_right)
            dve.drain()
            nc.vector.tensor_tensor(extra_i[:, :], ends_i[:, 0, :], ends_i[:, 1, :], ALU.subtract)
            dve.drain()
            nc.vector.tensor_scalar(extra_i[:, :], extra_i[:, :], 1, None, ALU.arith_shift_right)
            dve.drain()
            nc.vector.tensor_copy(extra_f[:, :], extra_i[:, :])
            nc.vector.tensor_copy(scan[:, 0, :], extra_i[:, :])
            dve.drain()
            now, reach = 0, 1
            while reach < GROUPS:
                nc.vector.tensor_copy(scan[:, 1 - now, 0:reach], scan[:, now, 0:reach])
                nc.vector.tensor_tensor(scan[:, 1 - now, reach:], scan[:, now, reach:], scan[:, now, 0:GROUPS - reach], ALU.add)
                dve.drain()
                now, reach = 1 - now, 2 * reach
            nc.vector.tensor_tensor(scan[:, now, :], scan[:, now, :], extra_f[:, :], ALU.subtract)
            dve.drain()
            nc.vector.scalar_tensor_tensor(extra_f[:, :], scan[:, now, :], float(TILE_MAX), extra_f[:, :], ALU.mult, ALU.add)
            dve.drain()
            nc.vector.scalar_tensor_tensor(table[:, :], extra_f[:, :], float(TILE_MAX), ends_i[:, 1, :], ALU.mult, ALU.add)
            dve.drain().then_inc(table_made, 1)
            dve.wait_ge(table_made, 1)

            def make_onehot(g, slot, tile, made):
                nc.vector.tensor_tensor(onehot[:, slot, :, :],
                                        bcast(iota_f[:, bass.ds(tile * P, WINDOW)], 1, [P, GE, WINDOW]),
                                        bcast(dst_f[:, bass.ds(g * GE, GE)], 2, [P, GE, WINDOW]), ALU.is_equal).then_inc(made, 1)

            def add_part(slot, tile):
                s = S[:, bass.ds(tile, WINDOW // P), :]
                nc.vector.tensor_tensor(s, s, part_ps[:, slot, :].rearrange("p (w d) -> p w d", d=D), ALU.add)

            def first_tile(g):
                packed = dve.value_load(table[0:1, bass.ds(g, 1)], min_val=0, max_val=(1 << 31) - 1)
                return dve.snap(within(packed & (TILE_MAX - 1), TILES - 1, "a tile of nodes"))

            def step(g, slot, n):
                tile, more, before = unpack(dve, g)
                if n + 1 < GROUPS:
                    make_onehot(g + 1, (slot + 1) % SLOTS, first_tile(g + 1), first_onehot)
                dve.wait_ge(first_summed, g + 1)
                add_part(slot, tile)
                with dve.If(more > 0):
                    with dve.Fori(0, more) as j:
                        to = within(tile + 2 * j + 2, TILES - 1, "a tile of nodes up to that of the group's greatest dst")
                        make_onehot(g, slot, to, more_onehot)
                        dve.wait_ge(more_summed, before + j + 1)
                        add_part(slot, to)
                with dve.Else():
                    dve.nop()
                dve.drain().then_inc(group_summed, 1)

            make_onehot(0, 0, first_tile(0), first_onehot)
            over_groups(dve, step)

        @block.tensor
        def _(pe):
            pe.wait_ge(table_made, 1)

            def sum_window(slot, done):
                for w in range(WINDOW // P):
                    for e in range(GE):
                        mm = nc.tensor.matmul(part_ps[:, slot, w * D:(w + 1) * D], onehot[:, slot, e, w * P:(w + 1) * P],
                                              rows[:, slot, e, :], start=(e == 0), stop=(e == GE - 1))
                mm.then_inc(done, 1)

            def step(g, slot, n):
                _, more, before = unpack(pe, g)
                pe.wait_ge(rows_loaded[slot], n // SLOTS * GE * 16 + GE * 16 if isinstance(g, int) else (g - slot - SLOTS) // SLOTS * (GE * 16) + 2 * GE * 16)
                pe.wait_ge(first_onehot, g + 1)
                sum_window(slot, first_summed)
                with pe.If(more > 0):
                    with pe.Fori(0, more) as j:
                        pe.wait_ge(more_onehot, before + j + 1)
                        sum_window(slot, more_summed)
                with pe.Else():
                    pe.nop()
            over_groups(pe, step)


def pipeline(eng, count, slots, stages):
    span = max(lag for _, lag in stages)
    start = -(-(span + slots) // slots) * slots
    loops = (count - 1 - start) // slots

    def step(i, n):
        for work, lag in stages:
            if 0 <= n - lag < count:
                work(i - lag, (n - lag) % slots, n - lag)

    for i in range(start):
        step(i, i)
    with eng.Fori(0, loops) as k:
        for h in range(slots):
            step(k * slots + start + h, start + h)
    for i in range(start + loops * slots, count + span):
        step(i, i)


def tile_of(array, t):
    return array[:, bass.ds(t, 1), :].rearrange("p a d -> p (a d)")


def mix_phase(nc, XN, X1, S, h1T, keep):
    with ExitStack() as ctx:
        sb = lambda name, shape, dt=F32: ctx.enter_context(nc.sbuf_tensor("mix_" + name, shape, dt))
        sem = lambda name: ctx.enter_context(nc.semaphore("mix_" + name))
        psum = lambda name, shape: ctx.enter_context(nc.psum_tensor("mix_" + name, shape, F32))
        ident = keep["ident"]
        attn = sb("attn", [P, SLOTS, D])
        attnT = sb("attnT", [P, SLOTS, KC, P])
        h0 = sb("h0", [P, SLOTS, D])
        h1 = sb("h1", [P, SLOTS, D])
        stats = sb("stats", [P, SLOTS, 6])
        moments = sb("moments", [P, SLOTS, 2])
        std = sb("std", [P, SLOTS])
        rstd = sb("rstd", [P, SLOTS])
        attnT_ps = psum("attnT_ps", [P, 512])
        h1T_ps = psum("h1T_ps", [P, 512])
        out_ps = psum("out_ps", [P, SLOTS, 512])
        attn_made, attnT_done, attnT_copied = sem("attn_made"), sem("attnT_done"), sem("attnT_copied")
        out_done, var_made, std_made = sem("out_done"), sem("var_made"), sem("std_made")
        scaled, scaled_w, h1_made = sem("scaled"), sem("scaled_w"), sem("h1_made")
        h1T_done, h1T_copied = sem("h1T_done"), sem("h1T_copied")
        block = ctx.enter_context(nc.Block())

        @block.vector
        def _(dve):
            def gate(t, slot, n):
                if n >= SLOTS:
                    dve.wait_ge(attnT_done, t - SLOTS + 1)
                nc.vector.tensor_tensor(attn[:, slot, :], tile_of(X1, t), tile_of(S, t), ALU.mult).then_inc(attn_made, 1)

            def add(t, slot, n):
                dve.wait_ge(out_done, t + 1)
                if n >= SLOTS:
                    dve.wait_ge(h1_made, t - SLOTS + 1)
                nc.vector.tensor_tensor(h0[:, slot, :], out_ps[:, slot, 0:D], tile_of(XN, t), ALU.add)
                dve.drain()
                nc.vector.bn_stats(stats[:, slot, :], h0[:, slot, :])
                dve.drain()
                nc.vector.bn_aggr(moments[:, slot, :], stats[:, slot, :]).then_inc(var_made, 1)

            def scale(t, slot, n):
                dve.wait_ge(std_made, t + 1)
                nc.vector.reciprocal(rstd[:, slot:slot + 1], std[:, slot:slot + 1])
                dve.drain()
                nc.vector.tensor_scalar(h0[:, slot, :], h0[:, slot, :], moments[:, slot, 0:1], rstd[:, slot:slot + 1],
                                        ALU.subtract, ALU.mult).then_inc(scaled, 1)
            pipeline(dve, TILES, SLOTS, [(scale, 3), (gate, 0), (add, 2)])

        @block.gpsimd
        def _(pool):
            def affine(t, slot, n):
                pool.wait_ge(scaled, t + 1)
                if n >= SLOTS:
                    pool.wait_ge(h1T_done, t - SLOTS + 1)
                nc.gpsimd.tensor_tensor(h0[:, slot, :], h0[:, slot, :], keep["ln1_w"][:, :], ALU.mult).then_inc(scaled_w, 1)
                pool.wait_ge(scaled_w, t + 1)
                nc.gpsimd.tensor_tensor(h1[:, slot, :], h0[:, slot, :], keep["ln1_b"][:, :], ALU.add).then_inc(h1_made, 1)
                pool.wait_ge(h1_made, t + 1)
                nc.gpsimd.tensor_tensor(tile_of(XN, t), h1[:, slot, :], keep["f2_b"][:, :], ALU.add)
            pipeline(pool, TILES, SLOTS, [(affine, 0)])

        @block.scalar
        def _(act):
            def copy_attnT(t, slot, n):
                act.wait_ge(attnT_done, t + 1)
                if n >= SLOTS:
                    act.wait_ge(out_done, t - SLOTS + 1)
                nc.scalar.activation(attnT[:, slot, :, :].rearrange("p c n -> p (c n)"), attnT_ps[:, 0:D], ACT.Copy).then_inc(attnT_copied, 1)

            def root(t, slot, n):
                act.wait_ge(var_made, t + 1)
                nc.scalar.activation(std[:, slot:slot + 1], moments[:, slot, 1:2], ACT.Sqrt, bias=keep["eps"][:, 0:1]).then_inc(std_made, 1)

            def copy_h1T(t, slot, n):
                act.wait_ge(h1T_done, t + 1)
                nc.scalar.activation(h1T[:, :, bass.ds(t * P, P)], h1T_ps[:, 0:D].rearrange("p (c n) -> p c n", c=KC), ACT.Copy).then_inc(h1T_copied, 1)
            pipeline(act, TILES, SLOTS, [(copy_attnT, 0), (root, 2), (copy_h1T, 4)])

        @block.tensor
        def _(pe):
            def transpose_attn(t, slot, n):
                pe.wait_ge(attn_made, t + 1)
                if n:
                    pe.wait_ge(attnT_copied, t)
                for c in range(KC):
                    mm = nc.tensor.transpose(attnT_ps[:, c * P:(c + 1) * P], attn[:, slot, c * P:(c + 1) * P], ident[:, :])
                mm.then_inc(attnT_done, 1)

            def project(t, slot, n):
                pe.wait_ge(attnT_copied, t + 1)
                if n >= SLOTS:
                    pe.wait_ge(var_made, t - SLOTS + 1)
                for c in range(KC):
                    mm = nc.tensor.matmul(out_ps[:, slot, 0:D], attnT[:, slot, c, :], keep["O_w"][:, c, :], start=(c == 0), stop=(c == KC - 1))
                mm.then_inc(out_done, 1)

            def transpose_h1(t, slot, n):
                pe.wait_ge(h1_made, t + 1)
                if n:
                    pe.wait_ge(h1T_copied, t)
                for c in range(KC):
                    mm = nc.tensor.transpose(h1T_ps[:, c * P:(c + 1) * P], h1[:, slot, c * P:(c + 1) * P], ident[:, :])
                mm.then_inc(h1T_done, 1)
            pipeline(pe, TILES, SLOTS, [(transpose_attn, 0), (project, 1), (transpose_h1, 4)])


GT = 2
NGT = -(-TILES // GT)
W2 = GT * P
GSLOTS = 2


def tiles_in(n):
    return min(GT, TILES - n * GT) if n >= NGT - 1 else GT


def ffn_phase(nc, XN, h1T, h2T, keep):
    FC = 2 * D // P
    with ExitStack() as ctx:
        sb = lambda name, shape, dt=F32: ctx.enter_context(nc.sbuf_tensor("ffn_" + name, shape, dt))
        sem = lambda name: ctx.enter_context(nc.semaphore("ffn_" + name))
        psum = lambda name, shape: ctx.enter_context(nc.psum_tensor("ffn_" + name, shape, F32))
        ident = keep["ident"]
        fT = sb("fT", [P, GSLOTS, FC, W2])
        r = sb("r", [P, GSLOTS, GT, D])
        h2 = sb("h2", [P, GSLOTS, GT, D])
        stats = sb("stats", [P, GSLOTS, GT, 6])
        moments = sb("moments", [P, GSLOTS, GT, 2])
        std = sb("std", [P, GSLOTS, GT])
        rstd = sb("rstd", [P, GSLOTS, GT])
        f_ps = psum("f_ps", [P, 2, FC, W2])
        f_ps = f_ps[:, :, :, :]
        out_ps = psum("out_ps", [P, GSLOTS, GT * D])
        hT_ps = psum("hT_ps", [P, KC, W2])
        f_done, f_read, fT_made, out_done = sem("f_done"), sem("f_read"), sem("fT_made"), sem("out_done")
        var_made, std_made, scaled = sem("var_made"), sem("std_made"), sem("scaled")
        scaled_w, h2_made, hT_done, hT_copied = sem("scaled_w"), sem("h2_made"), sem("hT_done"), sem("hT_copied")
        block = ctx.enter_context(nc.Block())

        def group_of(array, g, n):
            return array[:, bass.ds(g * GT, tiles_in(n)), :]

        @block.tensor
        def _(pe):
            def up(g, slot, n):
                w = tiles_in(n) * P
                if n >= 2:
                    pe.wait_ge(fT_made, g - 1)
                for k in range(FC):
                    for c in range(KC):
                        mm = nc.tensor.matmul(f_ps[:, n % 2, k, 0:w], keep["f1_w"][:, c, k * P:(k + 1) * P], h1T[:, c, bass.ds(g * W2, w)],
                                              start=(c == 0), stop=(c == KC - 1))
                mm.then_inc(f_done, 1)

            def down(g, slot, n):
                pe.wait_ge(fT_made, g + 1)
                if n >= 1:
                    pe.wait_ge(var_made, g)
                for i in range(tiles_in(n)):
                    for k in range(FC):
                        mm = nc.tensor.matmul(out_ps[:, 0, i * D:(i + 1) * D], fT[:, slot, k, i * P:(i + 1) * P], keep["f2_w"][:, k, :],
                                              start=(k == 0), stop=(k == FC - 1))
                mm.then_inc(out_done, 1)

            def transpose(g, slot, n):
                pe.wait_ge(h2_made, g + 1)
                if n:
                    pe.wait_ge(hT_copied, g)
                for i in range(tiles_in(n)):
                    for c in range(KC):
                        mm = nc.tensor.transpose(hT_ps[:, c, i * P:(i + 1) * P], h2[:, slot, i, c * P:(c + 1) * P], ident[:, :])
                mm.then_inc(hT_done, 1)
            pipeline(pe, NGT, GSLOTS, [(up, 0), (down, 1), (transpose, 3)])

        @block.scalar
        def _(act):
            def relu(g, slot, n):
                w = tiles_in(n) * P
                act.wait_ge(f_done, g + 1)
                if n >= GSLOTS:
                    act.wait_ge(out_done, g - GSLOTS + 1)
                for k in range(FC):
                    nc.scalar.activation(fT[:, slot, k, 0:w], f_ps[:, n % 2, k, 0:w], ACT.Relu, bias=keep["f1_b"][:, k:k + 1])
                act.drain().then_inc(fT_made, 1)

            def root(g, slot, n):
                act.wait_ge(var_made, g + 1)
                m = tiles_in(n)
                nc.scalar.activation(std[:, slot, 0:m], moments[:, slot, 0:m, 1:2].rearrange("p m a -> p (m a)"), ACT.Sqrt, bias=keep["eps"][:, 0:1]).then_inc(std_made, 1)

            def copy_hT(g, slot, n):
                w = tiles_in(n) * P
                act.wait_ge(hT_done, g + 1)
                nc.scalar.activation(h2T[:, :, bass.ds(g * W2, w)], hT_ps[:, :, 0:w], ACT.Copy).then_inc(hT_copied, 1)
            pipeline(act, NGT, GSLOTS, [(relu, 0), (root, 1), (copy_hT, 3)])

        @block.vector
        def _(dve):
            def add(g, slot, n):
                m = tiles_in(n)
                dve.wait_ge(out_done, g + 1)
                if n >= GSLOTS:
                    dve.wait_ge(h2_made, g - GSLOTS + 1)
                nc.vector.tensor_tensor(r[:, slot, 0:m, :], out_ps[:, 0, 0:m * D].rearrange("p (m d) -> p m d", d=D), group_of(XN, g, n), ALU.add)
                dve.drain()
                for i in range(m):
                    nc.vector.bn_stats(stats[:, slot, i, :], r[:, slot, i, :])
                dve.drain()
                for i in range(m):
                    nc.vector.bn_aggr(moments[:, slot, i, :], stats[:, slot, i, :])
                dve.drain().then_inc(var_made, 1)

            def scale(g, slot, n):
                m = tiles_in(n)
                dve.wait_ge(std_made, g + 1)
                nc.vector.reciprocal(rstd[:, slot, 0:m], std[:, slot, 0:m])
                dve.drain()
                for i in range(m):
                    nc.vector.tensor_scalar(r[:, slot, i, :], r[:, slot, i, :], moments[:, slot, i, 0:1], rstd[:, slot, i:i + 1], ALU.subtract, ALU.mult)
                dve.drain().then_inc(scaled, 1)
            pipeline(dve, NGT, GSLOTS, [(scale, 2), (add, 1)])

        @block.gpsimd
        def _(pool):
            def affine(g, slot, n):
                m = tiles_in(n)
                pool.wait_ge(scaled, g + 1)
                if n >= GSLOTS:
                    pool.wait_ge(hT_done, g - GSLOTS + 1)
                nc.gpsimd.tensor_tensor(r[:, slot, 0:m, :], r[:, slot, 0:m, :], bcast(keep["ln2_w"][:, :], 1, [P, m, D]), ALU.mult).then_inc(scaled_w, 1)
                pool.wait_ge(scaled_w, g + 1)
                nc.gpsimd.tensor_tensor(h2[:, slot, 0:m, :], r[:, slot, 0:m, :], bcast(keep["ln2_b"][:, :], 1, [P, m, D]), ALU.add).then_inc(h2_made, 1)
            pipeline(pool, NGT, GSLOTS, [(affine, 0)])


def gru_phase(nc, X, h2T, keep):
    with ExitStack() as ctx:
        sb = lambda name, shape, dt=F32: ctx.enter_context(nc.sbuf_tensor("gru_" + name, shape, dt))
        sem = lambda name: ctx.enter_context(nc.semaphore("gru_" + name))
        psum = lambda name, shape: ctx.enter_context(nc.psum_tensor("gru_" + name, shape, F32))
        ident = keep["ident"]
        w_rz = sb("w_rz", [P, KC, 2 * D])
        b_rz = sb("b_rz", [P, 2 * KC])
        rz = sb("rz", [P, GSLOTS, 2 * KC, W2])
        rn = sb("rn", [P, GSLOTS, KC, W2])
        new = rn
        diff = sb("diff", [P, GSLOTS, KC, W2])
        yT = diff
        rz_ps = psum("rz_ps", [P, 2 * KC, W2])
        ni_ps = psum("ni_ps", [P, 2, KC, W2])
        nh_ps = psum("nh_ps", [P, 2, KC, W2])
        y_ps = psum("y_ps", [P, GT, D])
        w_made, rz_done, n_done = sem("w_made"), sem("rz_done"), sem("n_done")
        rz_made, rn_made, n_made, diff_made = sem("rz_made"), sem("rn_made"), sem("n_made"), sem("diff_made")
        zd_made, yT_made, y_done, y_added = sem("zd_made"), sem("yT_made"), sem("y_done"), sem("y_added")
        block = ctx.enter_context(nc.Block())
        w_ih, w_hh, b_ih, b_hh = keep["w_ih"], keep["w_hh"], keep["b_ih"], keep["b_hh"]

        @block.gpsimd
        def _(pool):
            nc.gpsimd.tensor_tensor(w_rz[:, :, :], w_ih[:, :, 0:2 * D], w_hh[:, :, 0:2 * D], ALU.add)
            nc.gpsimd.tensor_tensor(b_rz[:, :], b_ih[:, 0:2 * KC], b_hh[:, 0:2 * KC], ALU.add).then_inc(w_made, 1)

            def blend(g, slot, n):
                w = tiles_in(n) * P
                pool.wait_ge(diff_made, g + 1)
                if n >= GSLOTS:
                    pool.wait_ge(y_done, g - GSLOTS + 1)
                nc.gpsimd.tensor_tensor(diff[:, slot, :, 0:w], diff[:, slot, :, 0:w], rz[:, slot, KC:2 * KC, 0:w], ALU.mult).then_inc(zd_made, 1)
                pool.wait_ge(zd_made, g + 1)
                nc.gpsimd.tensor_tensor(yT[:, slot, :, 0:w], diff[:, slot, :, 0:w], new[:, slot, :, 0:w], ALU.add).then_inc(yT_made, 1)
            pipeline(pool, NGT, GSLOTS, [(blend, 0)])

        @block.tensor
        def _(pe):
            def products(ps, weights, chunks, first, g, n):
                w = tiles_in(n) * P
                for k in range(chunks):
                    for c in range(KC):
                        mm = nc.tensor.matmul(ps[:, k, 0:w], weights[:, c, first + k * P:first + (k + 1) * P], h2T[:, c, bass.ds(g * W2, w)],
                                              start=(c == 0), stop=(c == KC - 1))
                return mm

            def gates(g, slot, n):
                if n:
                    pe.wait_ge(rz_made, g)
                products(rz_ps, w_rz, 2 * KC, 0, g, n).then_inc(rz_done, 1)
                if n >= 2:
                    pe.wait_ge(rn_made, g - 1)
                products(nh_ps[:, n % 2], w_hh, KC, 2 * D, g, n)
                products(ni_ps[:, n % 2], w_ih, KC, 2 * D, g, n).then_inc(n_done, 1)

            def transpose(g, slot, n):
                pe.wait_ge(yT_made, g + 1)
                if n:
                    pe.wait_ge(y_added, g)
                for i in range(tiles_in(n)):
                    for c in range(KC):
                        mm = nc.tensor.transpose(y_ps[:, i, c * P:(c + 1) * P], yT[:, slot, c, i * P:(i + 1) * P], ident[:, :])
                mm.then_inc(y_done, 1)
            pe.wait_ge(w_made, 1)
            pipeline(pe, NGT, GSLOTS, [(gates, 0), (transpose, 2)])

        @block.scalar
        def _(act):
            def sigmoid(g, slot, n):
                w = tiles_in(n) * P
                act.wait_ge(rz_done, g + 1)
                if n >= GSLOTS:
                    act.wait_ge(yT_made, g - GSLOTS + 1)
                for k in range(2 * KC):
                    nc.scalar.activation(rz[:, slot, k, 0:w], rz_ps[:, k, 0:w], ACT.Sigmoid, bias=b_rz[:, k:k + 1])
                act.drain().then_inc(rz_made, 1)

            def tanh(g, slot, n):
                w = tiles_in(n) * P
                act.wait_ge(rn_made, g + 1)
                for k in range(KC):
                    nc.scalar.activation(new[:, slot, k, 0:w], rn[:, slot, k, 0:w], ACT.Tanh, bias=b_ih[:, 2 * KC + k:2 * KC + k + 1])
                act.drain().then_inc(n_made, 1)
            act.wait_ge(w_made, 1)
            pipeline(act, NGT, GSLOTS, [(sigmoid, 0), (tanh, 1)])

        @block.vector
        def _(dve):
            def reset(g, slot, n):
                w = tiles_in(n) * P
                dve.wait_ge(n_done, g + 1)
                dve.wait_ge(rz_made, g + 1)
                for k in range(KC):
                    nc.vector.scalar_tensor_tensor(rn[:, slot, k, 0:w], nh_ps[:, n % 2, k, 0:w], b_hh[:, 2 * KC + k:2 * KC + k + 1],
                                                   rz[:, slot, k, 0:w], ALU.add, ALU.mult)
                dve.drain()
                nc.vector.tensor_tensor(rn[:, slot, :, 0:w], rn[:, slot, :, 0:w], ni_ps[:, n % 2, :, 0:w], ALU.add).then_inc(rn_made, 1)

            def difference(g, slot, n):
                w = tiles_in(n) * P
                dve.wait_ge(n_made, g + 1)
                nc.vector.tensor_tensor(diff[:, slot, :, 0:w], h2T[:, :, bass.ds(g * W2, w)], new[:, slot, :, 0:w], ALU.subtract).then_inc(diff_made, 1)

            def add(g, slot, n):
                m = tiles_in(n)
                dve.wait_ge(y_done, g + 1)
                x = X[:, bass.ds(g * GT, m), :]
                nc.vector.tensor_tensor(x, x, y_ps[:, 0:m, :], ALU.add).then_inc(y_added, 1)
            pipeline(dve, NGT, GSLOTS, [(reset, 0), (difference, 1), (add, 2)])


EXPERTS, HIDDEN, TOP = 8, 1024, 2
HC = HIDDEN // P
SG = 2
SROWS = SG * P
MAX_SG = (TOP * NODES + EXPERTS * SROWS) // SROWS
SLOT_ROWS = MAX_SG * SROWS
FAR = -3e38
MOE_KEPT = dict(wg=[P, KC, EXPERTS], bg=[P, EXPERTS], b1=[P, EXPERTS * HC], b2=[P, EXPERTS, D])


def route_phase(nc, X, XN, xs_dram, prob, place, groups, ins, keep):
    with ExitStack() as ctx:
        sb = lambda name, shape, dt=F32: ctx.enter_context(nc.sbuf_tensor("route_" + name, shape, dt))
        sem = lambda name: ctx.enter_context(nc.semaphore("route_" + name))
        psum = lambda name, shape: ctx.enter_context(nc.psum_tensor("route_" + name, shape, F32))
        ident, wg, bg = keep["ident"], keep["wg"], keep["bg"]
        stats = sb("stats", [P, TILES, 6])
        moments = sb("moments", [P, TILES, 2])
        std = sb("std", [P, TILES])
        rstd = sb("rstd", [P, TILES])
        xn = sb("xn", [P, SLOTS, D])
        xnT = sb("xnT", [P, SLOTS, KC, P])
        gate = sb("gate", [P, TILES, EXPERTS])
        cand = sb("cand", [P, TILES, EXPERTS])
        chosen = sb("chosen", [P, TOP, TILES, EXPERTS])
        either = sb("either", [P, TILES, EXPERTS])
        best = sb("best", [P, TOP, TILES])
        top = sb("top", [P, TILES])
        ratio = sb("ratio", [P, TILES])
        scan = sb("scan", [P, 2, TILES, EXPERTS])
        rank = sb("rank", [P, TILES, EXPERTS])
        node = sb("node", [P, TILES])
        valid = sb("valid", [P, TILES])
        spare = sb("spare", [P, TOP])
        order = sb("order", [P, EXPERTS])
        below = sb("below", [P, P])
        ones = sb("ones", [P, P])
        number = sb("number", [P, EXPERTS])
        number_i = sb("number_i", [P, EXPERTS], I32)
        starts = sb("starts", [P, 2, EXPERTS])
        place_f = sb("place_f", [P, TOP, TILES])
        scatter_to = sb("scatter_to", [P, TILES, TOP], I32)
        index = sb("index", [P, SLOTS, TOP], I32)
        row = sb("row", [P, SLOTS, D])
        xnT_ps = psum("xnT_ps", [P, 512])
        gate_ps = psum("gate_ps", [P, 512])
        prefix_ps = psum("prefix_ps", [P, 512])
        count_ps = psum("count_ps", [P, 512])
        var_made, std_made, norm_made = sem("var_made"), sem("std_made"), sem("norm_made")
        xnT_done, xnT_copied, gate_done = sem("xnT_done"), sem("xnT_copied"), sem("gate_done")
        iotas_made, either_made, counted = sem("iotas_made"), sem("either_made"), sem("counted")
        margin_made, ratio_made, place_made = sem("margin_made"), sem("ratio_made"), sem("place_made")
        index_made, index_seen, row_made = sem("index_made"), sem("index_seen"), sem("row_made")
        scattered = [sem(f"scattered_{s}") for s in range(SLOTS)]
        kept_loaded = sem("kept_loaded")
        block = ctx.enter_context(nc.Block())

        @block.sync
        def _(sp):
            load_kept(sp, MOE_KEPT, ins, keep, kept_loaded)

        @block.vector
        def _(dve):
            for t in range(TILES):
                nc.vector.bn_stats(stats[:, t, :], X[:, t, :])
            dve.drain()
            for t in range(TILES):
                nc.vector.bn_aggr(moments[:, t, :], stats[:, t, :])
            dve.drain().then_inc(var_made, 1)
            dve.wait_ge(std_made, 1)
            nc.vector.reciprocal(rstd[:, :], std[:, :])
            dve.drain()

            def norm(t, slot, n):
                if n >= SLOTS:
                    dve.wait_ge(xnT_copied, t - SLOTS + 1)
                nc.vector.tensor_scalar(xn[:, slot, :], tile_of(X, t), moments[:, bass.ds(t, 1), 0:1].rearrange("p a d -> p (a d)"),
                                        rstd[:, bass.ds(t, 1)], ALU.subtract, ALU.mult).then_inc(norm_made, 1)
            pipeline(dve, TILES, SLOTS, [(norm, 0)])

            full = [P, TILES, EXPERTS]
            dve.wait_ge(gate_done, TILES)
            dve.wait_ge(iotas_made, 1)
            nc.vector.tensor_tensor(gate[:, :, :], gate_ps[:, 0:TILES * EXPERTS].rearrange("p (t e) -> p t e", e=EXPERTS), bcast(bg[:, :], 1, full), ALU.add)
            nc.vector.tensor_scalar(valid[:, :], node[:, :], float(NODES), None, ALU.is_lt)
            nc.vector.tensor_scalar(below[:, :], below[:, :], 0.0, None, ALU.is_gt)
            nc.vector.memset(ones[:, :], 1.0)
            dve.drain()
            for c in range(TOP):
                nc.vector.tensor_reduce(best[:, c, :], gate[:, :, :], AX.X, ALU.max)
                dve.drain()
                nc.vector.tensor_tensor(cand[:, :, :], gate[:, :, :], bcast(best[:, c, :], 2, full), ALU.is_equal)
                dve.drain()
                nc.vector.tensor_tensor(cand[:, :, :], cand[:, :, :], bcast(order[:, :], 1, full), ALU.mult)
                dve.drain()
                nc.vector.tensor_reduce(top[:, :], cand[:, :, :], AX.X, ALU.max)
                dve.drain()
                nc.vector.tensor_tensor(chosen[:, c, :, :], cand[:, :, :], bcast(top[:, :], 2, full), ALU.is_equal)
                dve.drain()
                if c + 1 < TOP:
                    nc.vector.scalar_tensor_tensor(gate[:, :, :], chosen[:, c, :, :], FAR, gate[:, :, :], ALU.mult, ALU.add)
                nc.vector.tensor_tensor(chosen[:, c, :, :], chosen[:, c, :, :], bcast(valid[:, :], 2, full), ALU.mult)
                dve.drain()
            nc.vector.tensor_tensor(either[:, :, :], chosen[:, 0, :, :], chosen[:, 1, :, :], ALU.add).then_inc(either_made, 1)
            nc.vector.tensor_tensor(ratio[:, :], best[:, 1, :], best[:, 0, :], ALU.subtract).then_inc(margin_made, 1)

            dve.wait_ge(counted, 1)
            tile_counts = count_ps[:, 0:TILES * EXPERTS].rearrange("p (t e) -> p t e", e=EXPERTS)
            nc.vector.tensor_copy(scan[:, 0, :, :], tile_counts)
            dve.drain()
            now, reach = 0, 1
            while reach < TILES:
                nc.vector.tensor_copy(scan[:, 1 - now, 0:reach, :], scan[:, now, 0:reach, :])
                nc.vector.tensor_tensor(scan[:, 1 - now, reach:, :], scan[:, now, reach:, :], scan[:, now, 0:TILES - reach, :], ALU.add)
                dve.drain()
                now, reach = 1 - now, 2 * reach
            nc.vector.tensor_tensor(rank[:, :, :], scan[:, now, :, :], tile_counts, ALU.subtract)
            nc.vector.tensor_scalar(number[:, :], scan[:, now, TILES - 1, :], float(SROWS - 1), None, ALU.add)
            dve.drain()
            nc.vector.tensor_tensor(rank[:, :, :], rank[:, :, :], prefix_ps[:, 0:TILES * EXPERTS].rearrange("p (t e) -> p t e", e=EXPERTS), ALU.add)
            nc.vector.tensor_copy(number_i[:, :], number[:, :])
            dve.drain()
            nc.vector.tensor_scalar(number_i[:, :], number_i[:, :], SROWS.bit_length() - 1, None, ALU.arith_shift_right)
            dve.drain()
            nc.vector.tensor_scalar(number[:, :], number_i[:, :], 1.0, None, ALU.max)
            dve.drain()
            nc.vector.tensor_copy(starts[:, 0, :], number[:, :])
            dve.drain()
            now, reach = 0, 1
            while reach < EXPERTS:
                nc.vector.tensor_copy(starts[:, 1 - now, 0:reach], starts[:, now, 0:reach])
                nc.vector.tensor_tensor(starts[:, 1 - now, reach:], starts[:, now, reach:], starts[:, now, 0:EXPERTS - reach], ALU.add)
                dve.drain()
                now, reach = 1 - now, 2 * reach
            nc.vector.tensor_tensor(starts[:, now, :], starts[:, now, :], number[:, :], ALU.subtract)
            dve.drain()
            nc.vector.tensor_copy(groups[:, 0:EXPERTS], number[:, :])
            nc.vector.tensor_copy(groups[:, EXPERTS:2 * EXPERTS], starts[:, now, :])
            nc.vector.tensor_scalar(starts[:, now, :], starts[:, now, :], float(SROWS), None, ALU.mult)
            dve.drain()
            nc.vector.tensor_tensor(rank[:, :, :], rank[:, :, :], bcast(starts[:, now, :], 1, full), ALU.add)
            dve.drain()
            for c in range(TOP):
                nc.vector.tensor_tensor(cand[:, :, :], rank[:, :, :], chosen[:, c, :, :], ALU.mult)
                dve.drain()
                nc.vector.tensor_reduce(place_f[:, c, :], cand[:, :, :], AX.X, ALU.add)
                dve.drain()
            nc.vector.tensor_copy(place[:, :, :], place_f[:, :, :].rearrange("p c t -> p t c"))
            nc.vector.tensor_scalar(valid[:, :], valid[:, :], -1.0, 1.0, ALU.mult, ALU.add)
            dve.drain()
            for c in range(TOP):
                nc.vector.scalar_tensor_tensor(place_f[:, c, :], valid[:, :], spare[:, c:c + 1], place_f[:, c, :], ALU.mult, ALU.add)
            dve.drain()
            nc.vector.tensor_copy(scatter_to[:, :, :], place_f[:, :, :].rearrange("p c t -> p t c"))
            dve.wait_ge(ratio_made, 1)
            nc.vector.tensor_scalar(top[:, :], ratio[:, :], 1.0, None, ALU.add)
            dve.drain().then_inc(place_made, 1)
            nc.vector.reciprocal(top[:, :], top[:, :])
            dve.drain()
            nc.vector.tensor_copy(prob[:, :, 0], top[:, :])
            nc.vector.tensor_tensor(prob[:, :, 1], top[:, :], ratio[:, :], ALU.mult)

            def copy_row(t, slot, n):
                if n >= SLOTS:
                    dve.wait_ge(scattered[slot], 2 * 16 * (n // SLOTS) if isinstance(t, int) else (t - slot) // SLOTS * (2 * 16))
                nc.vector.tensor_copy(row[:, slot, :], tile_of(XN, t)).then_inc(row_made, 1)
            pipeline(dve, TILES, SLOTS, [(copy_row, 0)])

        @block.scalar
        def _(act):
            act.wait_ge(var_made, 1)
            nc.scalar.activation(std[:, :], moments[:, :, 1:2].rearrange("p t a -> p (t a)"), ACT.Sqrt, bias=keep["eps"][:, 0:1]).then_inc(std_made, 1)

            def copy(t, slot, n):
                act.wait_ge(xnT_done, t + 1)
                if n >= SLOTS:
                    act.wait_ge(gate_done, t - SLOTS + 1)
                nc.scalar.activation(tile_of(XN, t), xn[:, slot, :], ACT.Copy)
                nc.scalar.activation(xnT[:, slot, :, :].rearrange("p c n -> p (c n)"), xnT_ps[:, 0:D], ACT.Copy).then_inc(xnT_copied, 1)
            pipeline(act, TILES, SLOTS, [(copy, 0)])
            act.wait_ge(margin_made, 1)
            nc.scalar.activation(ratio[:, :], ratio[:, :], ACT.Exp).then_inc(ratio_made, 1)

        @block.tensor
        def _(pe):
            def transpose(t, slot, n):
                pe.wait_ge(norm_made, t + 1)
                if n:
                    pe.wait_ge(xnT_copied, t)
                for c in range(KC):
                    mm = nc.tensor.transpose(xnT_ps[:, c * P:(c + 1) * P], xn[:, slot, c * P:(c + 1) * P], ident[:, :])
                mm.then_inc(xnT_done, 1)

            def score(t, slot, n):
                pe.wait_ge(xnT_copied, t + 1)
                for c in range(KC):
                    mm = nc.tensor.matmul(gate_ps[:, bass.ds(t * EXPERTS, EXPERTS)], xnT[:, slot, c, :], wg[:, c, :], start=(c == 0), stop=(c == KC - 1))
                mm.then_inc(gate_done, 1)
            pe.wait_ge(kept_loaded, 16 * len(MOE_KEPT))
            pipeline(pe, TILES, SLOTS, [(transpose, 0), (score, 1)])
            pe.wait_ge(either_made, 1)
            flat = either[:, :, :].rearrange("p t e -> p (t e)")
            nc.tensor.matmul(prefix_ps[:, 0:TILES * EXPERTS], below[:, :], flat, start=True, stop=True)
            nc.tensor.matmul(count_ps[:, 0:TILES * EXPERTS], ones[:, :], flat, start=True, stop=True).then_inc(counted, 1)

        @block.gpsimd
        def _(pool):
            f = dict(allow_small_or_imprecise_dtypes=True)
            nc.gpsimd.iota(node[:, :], [[P, TILES]], base=0, channel_multiplier=1, **f)
            nc.gpsimd.iota(spare[:, :], [[P, TOP]], base=SLOT_ROWS, channel_multiplier=1, **f)
            nc.gpsimd.iota(order[:, :], [[-1, EXPERTS]], base=EXPERTS, channel_multiplier=0, **f)
            nc.gpsimd.iota(below[:, :], [[1, P]], base=0, channel_multiplier=-1, **f).then_inc(iotas_made, 1)
            pool.wait_ge(place_made, 1)

            def scatter(t, slot, n):
                if n >= SLOTS:
                    pool.wait_ge(scattered[slot], 2 * 16 * (n // SLOTS) if isinstance(t, int) else (t - slot) // SLOTS * (2 * 16))
                nc.gpsimd.tensor_copy(index[:, slot, :], scatter_to[:, bass.ds(t, 1), :].rearrange("p a c -> p (a c)")).then_inc(index_made, 1)
                pool.wait_ge(index_made, t + 1)
                pool.wait_ge(row_made, t + 1)
                pool.sem_inc(index_seen, 1)
                for c in range(TOP):
                    nc.gpsimd.indirect_dma_start(out=xs_dram, out_offset=bass.IndirectOffsetOnAxis(ap=index[:, slot, c:c + 1].bitcast(U32), axis=0),
                                                 in_=row[:, slot, :], in_offset=None).then_inc(scattered[slot], 16)
            pipeline(pool, TILES, SLOTS, [(scatter, 0)])
            for s in range(SLOTS):
                pool.wait_ge(scattered[s], 2 * 16 * len(range(s, TILES, SLOTS)))


def expert_phase(nc, xs_dram, ys_dram, w1_in, w2_in, groups, keep):
    with ExitStack() as ctx:
        sb = lambda name, shape, dt=F32: ctx.enter_context(nc.sbuf_tensor("moe_" + name, shape, dt))
        sem = lambda name: ctx.enter_context(nc.semaphore("moe_" + name))
        psum = lambda name, shape: ctx.enter_context(nc.psum_tensor("moe_" + name, shape, F32))
        ident, b1, b2 = keep["ident"], keep["b1"], keep["b2"]
        w1 = sb("w1", [P, 2, KC, HIDDEN])
        w2 = sb("w2", [P, 2, HC, D])
        x = sb("x", [P, SG, D])
        xT = sb("xT", [P, KC, SROWS])
        hT = sb("hT", [P, HC, SROWS])
        y = sb("y", [P, SG, D])
        HB = 4
        h_ps = psum("h_ps", [P, HB, 512])
        xT_ps = psum("xT_ps", [P, KC, SROWS])
        y_ps = psum("y_ps", [P, SG, D])
        w_loaded = [sem("w_loaded_0"), sem("w_loaded_1")]
        x_loaded, xT_done, xT_copied = sem("x_loaded"), sem("xT_done"), sem("xT_copied")
        h_done, h_made, y_done, y_made, y_stored = sem("h_done"), sem("h_made"), sem("y_done"), sem("y_made"), sem("y_stored")
        expert_done, weights_free = sem("expert_done"), sem("weights_free")
        weights_seen, ends_seen = sem("weights_seen"), sem("ends_seen")
        block = ctx.enter_context(nc.Block())

        def span(eng, e):
            count = eng.value_load(groups[0:1, bass.ds(e, 1)], min_val=1, max_val=MAX_SG)
            before = eng.value_load(groups[0:1, bass.ds(e + EXPERTS, 1)], min_val=0, max_val=MAX_SG - 1)
            return count, before

        def over_experts(eng, body):
            with eng.Fori(0, EXPERTS // 2) as k:
                body(2 * k, 0)
                body(2 * k + 1, 1)

        @block.gpsimd
        def _(pool):
            def load(e, slot):
                pool.dma_start(w1[:, slot, :, :], w1_in[bass.ds(e, 1), :, :, :].rearrange("a p c h -> p (a c) h")).then_inc(w_loaded[slot], 16)
                pool.dma_start(w2[:, slot, :, :], w2_in[bass.ds(e, 1), :, :, :].rearrange("a p c h -> p (a c) h")).then_inc(w_loaded[slot], 16)
            load(0, 0)
            load(1, 1)
            with pool.Fori(1, EXPERTS // 2) as k:
                for slot in range(2):
                    pool.wait_ge(expert_done, 2 * k + slot - 1)
                    pool.sem_inc(weights_free, 1)
                    load(2 * k + slot, slot)

        @block.sync
        def _(sp):
            rows = lambda dram, q: dram[bass.ds(q * SROWS, SROWS), :].rearrange("(i p) d -> p i d", p=P)
            last = EXPERTS - 1
            count, before = span(sp, last)
            sp.dma_start(x[:, :, :], rows(xs_dram, 0)).then_inc(x_loaded, 16)
            with sp.Fori(0, before + count) as i:
                q = nc.s_assert_within(i, 0, MAX_SG - 1, skip_runtime_bounds_check_because="no routing fills more groups")
                sp.wait_ge(xT_done, q + 1)
                sp.dma_start(x[:, :, :], rows(xs_dram, q + 1)).then_inc(x_loaded, 16)
                sp.wait_ge(y_made, q + 1)
                sp.dma_start(rows(ys_dram, q), y[:, :, :]).then_inc(y_stored, 16)
            sp.wait_ge(y_stored, (before + count) * 16)
            sp.sem_inc(ends_seen, 1)
            sp.wait_ge(x_loaded, (before + count) * 16 + 16)
            sp.sem_inc(ends_seen, 1)

        @block.tensor
        def _(pe):
            def transpose(q):
                pe.wait_ge(x_loaded, q * 16 + 16)
                for c in range(KC):
                    for i in range(SG):
                        mm = nc.tensor.transpose(xT_ps[:, c, i * P:(i + 1) * P], x[:, i, c * P:(c + 1) * P], ident[:, :])
                mm.then_inc(xT_done, 1)

            def expert(e, slot):
                count, before = span(pe, e)
                pe.wait_ge(w_loaded[slot], (e - slot) * 16 + 32)
                pe.sem_inc(weights_seen, 1)
                with pe.Fori(0, count) as j:
                    q = before + j
                    pe.wait_ge(xT_copied, q + 1)
                    for k in range(HC):
                        if k >= HB:
                            pe.wait_ge(h_made, q * HC + k - HB + 1)
                        for c in range(KC):
                            mm = nc.tensor.matmul(h_ps[:, k % HB, 0:SROWS], w1[:, slot, c, k * P:(k + 1) * P], xT[:, c, :], start=(c == 0), stop=(c == KC - 1))
                        mm.then_inc(h_done, 1)
                    transpose(q + 1)
                    for i in range(SG):
                        for k in range(HC):
                            if i == 0:
                                pe.wait_ge(h_made, q * HC + k + 1)
                            mm = nc.tensor.matmul(y_ps[:, i, :], hT[:, k, i * P:(i + 1) * P], w2[:, slot, k, :], start=(k == 0), stop=(k == HC - 1))
                    mm.then_inc(y_done, 1)
                pe.drain().then_inc(expert_done, 1)
            transpose(0)
            over_experts(pe, expert)

        @block.scalar
        def _(act):
            def copy_xT(q):
                act.wait_ge(xT_done, q + 1)
                nc.scalar.activation(xT[:, :, :], xT_ps[:, :, :], ACT.Copy).then_inc(xT_copied, 1)

            def expert(e, slot):
                count, before = span(act, e)
                with act.Fori(0, count) as j:
                    q = before + j
                    for k in range(HC):
                        act.wait_ge(h_done, q * HC + k + 1)
                        nc.scalar.activation(hT[:, k, :], h_ps[:, k % HB, 0:SROWS], ACT.Relu, bias=b1[:, bass.ds(e * HC + k, 1)]).then_inc(h_made, 1)
                    copy_xT(q + 1)
            copy_xT(0)
            over_experts(act, expert)

        @block.vector
        def _(dve):
            def expert(e, slot):
                count, before = span(dve, e)
                with dve.Fori(0, count) as j:
                    q = before + j
                    dve.wait_ge(y_done, q + 1)
                    dve.wait_ge(y_stored, q * 16)
                    nc.vector.tensor_tensor(y[:, :, :], y_ps[:, :, :],
                                            b2[:, bass.ds(e, 1), :].broadcast_to([P, SG, D]), ALU.add).then_inc(y_made, 1)
            over_experts(dve, expert)


def combine_phase(nc, X, ys_dram, prob, place, out):
    with ExitStack() as ctx:
        sb = lambda name, shape, dt=F32: ctx.enter_context(nc.sbuf_tensor("sum_" + name, shape, dt))
        sem = lambda name: ctx.enter_context(nc.semaphore("sum_" + name))
        index = sb("index", [P, SLOTS, TOP], I32)
        y = sb("y", [P, SLOTS, TOP, D])
        result = sb("result", [P, SLOTS, D])
        index_made, index_seen = sem("index_made"), sem("index_seen")
        y_loaded = [sem(f"y_loaded_{s}") for s in range(SLOTS)]
        result_made, stored = sem("result_made"), [sem(f"stored_{s}") for s in range(SLOTS)]
        block = ctx.enter_context(nc.Block())

        @block.gpsimd
        def _(pool):
            def gather(t, slot, n):
                if n >= SLOTS:
                    pool.wait_ge(result_made, t - SLOTS + 1)
                nc.gpsimd.tensor_copy(index[:, slot, :], place[:, bass.ds(t, 1), :].rearrange("p a c -> p (a c)")).then_inc(index_made, 1)
                pool.wait_ge(index_made, t + 1)
                pool.sem_inc(index_seen, 1)
                for c in range(TOP):
                    nc.gpsimd.indirect_dma_start(out=y[:, slot, c, :], out_offset=None, in_=ys_dram,
                                                 in_offset=bass.IndirectOffsetOnAxis(ap=index[:, slot, c:c + 1].bitcast(U32), axis=0)).then_inc(y_loaded[slot], 16)
            pipeline(pool, TILES, SLOTS, [(gather, 0)])

        @block.vector
        def _(dve):
            def add(t, slot, n):
                dve.wait_ge(y_loaded[slot], 2 * 16 * (n // SLOTS + 1) if isinstance(t, int) else (t - slot) // SLOTS * 32 + 32)
                if n >= SLOTS:
                    dve.wait_ge(stored[slot], 16 * (n // SLOTS) if isinstance(t, int) else (t - slot) // SLOTS * 16)
                nc.vector.scalar_tensor_tensor(result[:, slot, :], y[:, slot, 0, :], prob[:, bass.ds(t, 1), 0:1].rearrange("p a c -> p (a c)"), tile_of(X, t), ALU.mult, ALU.add)
                dve.drain()
                nc.vector.scalar_tensor_tensor(result[:, slot, :], y[:, slot, 1, :], prob[:, bass.ds(t, 1), 1:2].rearrange("p a c -> p (a c)"), result[:, slot, :], ALU.mult, ALU.add).then_inc(result_made, 1)
            pipeline(dve, TILES, SLOTS, [(add, 0)])

        @block.sync
        def _(sp):
            def store(t, slot, n):
                sp.wait_ge(result_made, t + 1)
                sp.dma_start(out[bass.ds(t * P, P), :], result[:, slot, :]).then_inc(stored[slot], 16)
            pipeline(sp, TILES, SLOTS, [(store, 0)])
            for s in range(SLOTS):
                sp.wait_ge(stored[s], 16 * len(range(s, TILES, SLOTS)))


def build_program(nc, ins, out):
    x1_dram = nc.dram_tensor("x1_rows", [NPAD, D], F32).ap()
    xs_dram = nc.dram_tensor("slot_inputs", [SLOT_ROWS + TOP * P, D], F32).ap()
    ys_dram = nc.dram_tensor("slot_outputs", [SLOT_ROWS, D], F32).ap()
    with ExitStack() as ctx:
        sb = lambda name, shape, dt=F32: ctx.enter_context(nc.sbuf_tensor(name, shape, dt))
        X, XN, X1 = sb("X", [P, TILES, D]), sb("XN", [P, TILES, D]), sb("X1", [P, TILES, D])
        S = sb("S", [P, TILES + 1, D])
        prob = sb("prob", [P, TILES, TOP])
        place = sb("place", [P, TILES, TOP], I32)
        groups = sb("groups", [P, 2 * EXPERTS], I32)
        keep = dict(ident=sb("ident", [P, P]), eps=sb("eps", [P, 1]), O_b=sb("O_b", [P, D]))
        attention_phase(nc, X, XN, X1, S, ins["x"], ins["w_qkv"], x1_dram, xs_dram, ys_dram, ins, keep)
        with ExitStack() as gnn:
            for name, shape in GNN_KEPT.items():
                keep[name] = gnn.enter_context(nc.sbuf_tensor(name, shape, F32))
            edge_phase(nc, S, x1_dram, ins["src"], ins["dst"], ins, keep)
            h1T = gnn.enter_context(nc.sbuf_tensor("h1T", [P, KC, NPAD], F32))
            h2T = X1[:, :, :].rearrange("p t d -> p (t d)").rearrange("p (c n) -> p c n", c=KC)
            mix_phase(nc, XN, X1, S, h1T, keep)
            ffn_phase(nc, XN, h1T, h2T, keep)
            gru_phase(nc, X, h2T, keep)
        for name, shape in MOE_KEPT.items():
            keep[name] = sb(name, shape)
        route_phase(nc, X, XN, xs_dram, prob, place, groups, ins, keep)
        expert_phase(nc, xs_dram, ys_dram, ins["w1"], ins["w2"], groups, keep)
        combine_phase(nc, X, ys_dram, prob, place, out)


def kernel(x, src, dst, L0_gnn_Wq, L0_gnn_Wk, L0_gnn_Wv, L0_gnn_O_w, L0_gnn_O_b, L0_gnn_ln1_w, L0_gnn_ln1_b,
           L0_gnn_f1_w, L0_gnn_f1_b, L0_gnn_f2_w, L0_gnn_f2_b, L0_gnn_ln2_w, L0_gnn_ln2_b, L0_gnn_gru_w_ih,
           L0_gnn_gru_w_hh, L0_gnn_gru_b_ih, L0_gnn_gru_b_hh, L0_ffn_Wg, L0_ffn_bg, L0_ffn_W1, L0_ffn_b1,
           L0_ffn_W2, L0_ffn_b2):
    import numpy as np
    import concourse.bacc as bacc
    from concourse.bass_utils import run_bass_kernel_spmd as run

    def by_tile(a):
        return np.asarray(a).reshape(-1, P, a.shape[-1]).transpose(1, 0, 2)

    def by_chunk(a):
        return np.asarray(a).reshape(-1, P).T

    def repeated(a):
        return np.broadcast_to(np.asarray(a), (P,) + a.shape)

    def edges(a, fill):
        return np.concatenate([np.asarray(a), np.full(COLS * P - EDGES, fill, np.int32)]).reshape(COLS, P).T

    x_padded = np.concatenate([np.asarray(x), np.zeros((NPAD - NODES, D), np.float32)])
    qkv = np.concatenate([np.asarray(L0_gnn_Wq), np.asarray(L0_gnn_Wk), np.asarray(L0_gnn_Wv)], 1)
    arrays = dict(
        x=by_tile(x_padded), w_qkv=by_tile(qkv), ident=np.eye(P, dtype=np.float32),
        src=edges(src, 0), dst=edges(dst, NPAD - 1),
        O_w=by_tile(L0_gnn_O_w), O_b=repeated(L0_gnn_O_b), f1_w=by_tile(L0_gnn_f1_w), f1_b=by_chunk(L0_gnn_f1_b),
        f2_w=by_tile(L0_gnn_f2_w), f2_b=repeated(L0_gnn_f2_b),
        ln1_w=repeated(L0_gnn_ln1_w), ln1_b=repeated(L0_gnn_ln1_b), ln2_w=repeated(L0_gnn_ln2_w), ln2_b=repeated(L0_gnn_ln2_b),
        w_ih=by_tile(L0_gnn_gru_w_ih), w_hh=by_tile(L0_gnn_gru_w_hh), b_ih=by_chunk(L0_gnn_gru_b_ih), b_hh=by_chunk(L0_gnn_gru_b_hh),
        wg=by_tile(np.asarray(L0_ffn_Wg).T), bg=repeated(L0_ffn_bg),
        b1=by_chunk(np.asarray(L0_ffn_b1).reshape(-1)), b2=repeated(L0_ffn_b2),
        w1=np.asarray(L0_ffn_W1).transpose(0, 2, 1).reshape(EXPERTS, KC, P, HIDDEN).transpose(0, 2, 1, 3),
        w2=np.asarray(L0_ffn_W2).transpose(0, 2, 1).reshape(EXPERTS, HC, P, D).transpose(0, 2, 1, 3),
    )
    arrays = {f"in_{name}": np.ascontiguousarray(a) for name, a in arrays.items()}
    nc = bacc.Bacc("TRN2", target_bir_lowering=False, num_devices=1)
    ins = {name[3:]: nc.dram_tensor(name, a.shape, mybir.dt.from_np(a.dtype), kind="ExternalInput").ap() for name, a in arrays.items()}
    out = nc.dram_tensor("out", [NPAD, D], F32, kind="ExternalOutput").ap()
    build_program(nc, ins, out)
    result = run(nc, [arrays], core_ids=[0])
    return result.results[0]["out"][:NODES]
```

```python
import concourse.bass as bass
from concourse import mybir
from contextlib import ExitStack

F32 = mybir.dt.float32
I32 = mybir.dt.int32
U32 = mybir.dt.uint32
F32R = mybir.dt.float32r
ALU = mybir.AluOpType
ACT = mybir.ActivationFunctionType
AX = mybir.AxisListType

P = 128
NODES, EDGES, D = 3125, 50000, 256
HEADS = 8
DH = D // HEADS
TILES = -(-NODES // P)
NPAD = TILES * P
KC = D // P
SLOTS = 3
GE = 4
BATCHES = -(-EDGES // (SLOTS * GE * P))
GROUPS = BATCHES * SLOTS
COLS = GROUPS * GE
EPS = 1e-5
TILE_BITS = TILES.bit_length()
TILE_MAX = 1 << TILE_BITS
WINDOW = 2 * P
AT_MORE = SLOTS * TILE_BITS
BATCH_BITS = BATCHES.bit_length()
AHEAD = 2
X_LOADS = 5
PARTS = 2
PRODUCTS = ((0, 1), (1, 0), (0, 0))
X_TILES = TILES // X_LOADS


def bcast(ap, axis, shape):
    return ap.unsqueeze(axis).broadcast_to(shape)


def attention_phase(nc, X, XN, X1, S, x_in, w_in, x1_dram, xs_dram, ys_dram, ins, keep):
    with ExitStack() as ctx:
        sb = lambda name, shape, dt=F32: ctx.enter_context(nc.sbuf_tensor("attn_" + name, shape, dt))
        sem = lambda name: ctx.enter_context(nc.semaphore("attn_" + name))
        psum = lambda name, shape: ctx.enter_context(nc.psum_tensor("attn_" + name, shape, F32))
        ident = keep["ident"]
        wqkv = sb("wqkv", [P, KC, 3 * D])
        xn = sb("xn", [P, SLOTS, D])
        xnT = sb("xnT", [P, SLOTS, KC, P])
        qkv = sb("qkv", [P, SLOTS, 3 * D])
        prod = sb("prod", [P, HEADS * HEADS, DH])
        vprod = sb("vprod", [P, SLOTS, HEADS, D])
        score = sb("score", [P, SLOTS, HEADS, HEADS])
        prob = sb("prob", [P, SLOTS, HEADS, HEADS])
        row = sb("row", [P, HEADS])
        stats = sb("stats", [P, TILES, 6])
        moments = sb("moments", [P, TILES, 2])
        std = sb("std", [P, TILES])
        rstd = sb("rstd", [P, TILES])
        xnT_ps = psum("xnT_ps", [P, 512])
        x1_ps = psum("x1_ps", [P, 512])
        qkv_ps = psum("qkv_ps", [P, SLOTS, 2, 512])

        x_loaded = [sem(f"x_loaded_{n}") for n in range(X_LOADS)]
        w_loaded, id_loaded = sem("w_loaded"), sem("id_loaded")
        var_ready, std_ready = sem("var_ready"), sem("std_ready")
        norm_ready, xnT_done, xnT_copied = sem("norm_ready"), sem("xnT_done"), sem("xnT_copied")
        qkv_done, qkv_copied = sem("qkv_done"), sem("qkv_copied")
        shifted, exped, prob_ready = sem("shifted"), sem("exped"), sem("prob_ready")
        vprod_ready, x1_ready, x1_stored = sem("vprod_ready"), sem("x1_ready"), sem("x1_stored")
        x1_summed = sem("x1_summed")
        bias_loaded, xn_kept = sem("bias_loaded"), sem("xn_kept")
        s_cleared, slots_cleared = sem("s_cleared"), sem("slots_cleared")
        fills = sum(-(-dram.shape[0] // P // TILES) for dram in (xs_dram, ys_dram))
        block = ctx.enter_context(nc.Block())

        def over_tiles(eng, step):
            for t in range(SLOTS):
                step(t, t, t)
            loops = TILES // SLOTS - 2
            with eng.Fori(0, loops) as k:
                for h in range(SLOTS):
                    step(k * SLOTS + SLOTS + h, h, SLOTS + h)
            for t in range((loops + 1) * SLOTS, TILES):
                step(t, t % SLOTS, t)

        @block.sync
        def _(sp):
            for n in range(X_LOADS):
                part = slice(n * X_TILES, (n + 1) * X_TILES)
                sp.dma_start(X[:, part, :], x_in[:, part, :]).then_inc(x_loaded[n], 16)
            sp.dma_start(ident[:, :], ins["ident"]).then_inc(id_loaded, 16)
            sp.dma_start(wqkv[:, :, :], w_in).then_inc(w_loaded, 16)
            sp.dma_start(keep["O_b"][:, :], ins["O_b"]).then_inc(bias_loaded, 16)

            def store(t, slot, n):
                sp.wait_ge(x1_ready, t + 1)
                sp.dma_start(x1_dram[bass.ds(t * P, P), :], X1[:, bass.ds(t, 1), :].rearrange("p a d -> p (a d)")).then_inc(x1_stored, 16)
            over_tiles(sp, store)
            sp.wait_ge(x1_stored, 16 * TILES)
            sp.wait_ge(slots_cleared, 16 * fills)

        @block.vector
        def _(dve):
            nc.vector.memset(S[:, :, :], 0.0).then_inc(s_cleared, 1)
            nc.vector.memset(keep["eps"][:, :], EPS)
            for n in range(X_LOADS):
                dve.wait_ge(x_loaded[n], 16)
                for t in range(n * X_TILES, (n + 1) * X_TILES):
                    nc.vector.bn_stats(stats[:, t, :], X[:, t, :])
            dve.drain()
            for t in range(TILES):
                nc.vector.bn_aggr(moments[:, t, :], stats[:, t, :])
            dve.drain().then_inc(var_ready, 1)
            dve.wait_ge(std_ready, 1)
            nc.vector.reciprocal(rstd[:, :], std[:, :])
            dve.drain()

            def norm(t, slot, n):
                if n >= SLOTS:
                    dve.wait_ge(xnT_done, t - SLOTS + 1)
                    dve.wait_ge(xn_kept, t - SLOTS + 1)
                nc.vector.tensor_scalar(xn[:, slot, :], X[:, bass.ds(t, 1), :].rearrange("p a d -> p (a d)"),
                                        moments[:, bass.ds(t, 1), 0:1].rearrange("p a d -> p (a d)"), rstd[:, bass.ds(t, 1)],
                                        ALU.subtract, ALU.mult).then_inc(norm_ready, 1)

            def step(t, slot, n):
                if n + 2 < TILES:
                    norm(t + 2, (slot + 2) % SLOTS, n + 2)
                dve.wait_ge(qkv_copied, t + 1)
                q = qkv[:, slot, 0:D].rearrange("p (h d) -> p h d", h=HEADS)
                k = qkv[:, slot, D:2 * D].rearrange("p (h d) -> p h d", h=HEADS)
                shape = [P, HEADS, HEADS, DH]
                nc.vector.tensor_tensor(prod[:, :, :].rearrange("p (h g) d -> p h g d", h=HEADS),
                                        bcast(q, 2, shape), bcast(k, 1, shape), ALU.mult)
                dve.drain()
                s = score[:, slot, :, :]
                nc.vector.tensor_reduce(s.rearrange("p h g -> p (h g)"), prod[:, :, :], AX.X, ALU.add)
                dve.drain()
                nc.vector.tensor_reduce(row[:, :], s, AX.X, ALU.max)
                dve.drain()
                nc.vector.tensor_tensor(s, s, bcast(row[:, :], 2, [P, HEADS, HEADS]), ALU.subtract).then_inc(shifted, 1)
                dve.wait_ge(exped, t + 1)
                nc.vector.tensor_reduce(row[:, :], prob[:, slot, :, :], AX.X, ALU.add)
                dve.drain()
                nc.vector.reciprocal(row[:, :], row[:, :])
                dve.drain()
                nc.vector.tensor_tensor(prob[:, slot, :, :], prob[:, slot, :, :], bcast(row[:, :], 2, [P, HEADS, HEADS]),
                                        ALU.mult).then_inc(prob_ready, 1)

            norm(0, 0, 0)
            norm(1, 1, 1)
            over_tiles(dve, step)

        @block.scalar
        def _(act):
            act.wait_ge(s_cleared, 1)
            for dram in (xs_dram, ys_dram):
                per = dram.shape[0] // P
                rows = dram.rearrange("(p r) d -> p r d", p=P)
                for r in range(0, per, TILES):
                    m = min(TILES, per - r)
                    act.dma_start(rows[:, r:r + m, :], S[:, 0:m, :]).then_inc(slots_cleared, 16)

            def copy_xnT(t, slot, n):
                act.wait_ge(xnT_done, t + 1)
                nc.scalar.activation(xnT[:, slot, :, :].rearrange("p c n -> p (c n)"), xnT_ps[:, 0:D], ACT.Copy).then_inc(xnT_copied, 1)

            def copy_qkv(t, slot, n):
                act.wait_ge(qkv_done, t + 1)
                if n >= SLOTS:
                    act.wait_ge(vprod_ready, t - SLOTS + 1)
                half = 3 * D // 2
                nc.scalar.activation(qkv[:, slot, 0:D], qkv_ps[:, slot, 0, 0:D], ACT.Copy, scale=float(DH) ** -0.5)
                nc.scalar.activation(qkv[:, slot, D:half], qkv_ps[:, slot, 0, D:half], ACT.Copy)
                nc.scalar.activation(qkv[:, slot, half:], qkv_ps[:, slot, 1, 0:half], ACT.Copy)
                act.drain().then_inc(qkv_copied, 1)

            def keep_x1(t):
                act.wait_ge(x1_summed, t + 1)
                nc.scalar.activation(X1[:, bass.ds(t, 1), :].rearrange("p a d -> p (a d)"), x1_ps[:, 0:D], ACT.Copy).then_inc(x1_ready, 1)

            def step(t, slot, n):
                if n + 2 < TILES:
                    copy_xnT(t + 2, (slot + 2) % SLOTS, n + 2)
                act.wait_ge(shifted, t + 1)
                nc.scalar.activation(prob[:, slot, :, :].rearrange("p h g -> p (h g)"),
                                     score[:, slot, :, :].rearrange("p h g -> p (h g)"), ACT.Exp).then_inc(exped, 1)
                if n + 1 < TILES:
                    copy_qkv(t + 1, (slot + 1) % SLOTS, n + 1)
                if n:
                    keep_x1(t - 1)

            act.wait_ge(var_ready, 1)
            nc.scalar.activation(std[:, :], moments[:, :, 1:2].rearrange("p t a -> p (t a)"), ACT.Sqrt, bias=keep["eps"][:, 0:1]).then_inc(std_ready, 1)
            copy_xnT(0, 0, 0)
            copy_xnT(1, 1, 1)
            copy_qkv(0, 0, 0)
            over_tiles(act, step)
            keep_x1(TILES - 1)

        @block.tensor
        def _(pe):
            pe.wait_ge(id_loaded, 16)
            pe.wait_ge(w_loaded, 16)

            def transpose_xn(t, slot, n):
                pe.wait_ge(norm_ready, t + 1)
                if n:
                    pe.wait_ge(xnT_copied, t)
                for c in range(KC):
                    mm = nc.tensor.transpose(xnT_ps[:, c * P:(c + 1) * P], xn[:, slot, c * P:(c + 1) * P], ident[:, :])
                mm.then_inc(xnT_done, 1)

            def project(t, slot, n):
                pe.wait_ge(xnT_copied, t + 1)
                if n >= SLOTS:
                    pe.wait_ge(qkv_copied, t - SLOTS + 1)
                for half in range(2):
                    for c in range(KC):
                        mm = nc.tensor.matmul(qkv_ps[:, slot, half, 0:3 * D // 2], xnT[:, slot, c, :],
                                              wqkv[:, c, half * 3 * D // 2:(half + 1) * 3 * D // 2],
                                              start=(c == 0), stop=(c == KC - 1))
                mm.then_inc(qkv_done, 1)

            def sum_values(t, slot, n):
                pe.wait_ge(vprod_ready, t + 1)
                if n:
                    pe.wait_ge(x1_ready, t)
                for g in range(HEADS):
                    mm = nc.tensor.matmul(x1_ps[:, 0:D], ident[:, :], vprod[:, slot, g, :], start=(g == 0), stop=(g == HEADS - 1))
                mm.then_inc(x1_summed, 1)

            def step(t, slot, n):
                if n + 1 < TILES:
                    project(t + 1, (slot + 1) % SLOTS, n + 1)
                if n + 2 < TILES:
                    transpose_xn(t + 2, (slot + 2) % SLOTS, n + 2)
                if n:
                    sum_values(t - 1, (slot + 2) % SLOTS, n - 1)

            transpose_xn(0, 0, 0)
            transpose_xn(1, 1, 1)
            project(0, 0, 0)
            over_tiles(pe, step)
            sum_values(TILES - 1, (TILES - 1) % SLOTS, TILES - 1)

        @block.gpsimd
        def _(pool):
            def keep_xn(t, slot, n):
                pool.wait_ge(norm_ready, t + 1)
                nc.gpsimd.tensor_tensor(tile_of(XN, t), xn[:, slot, :], keep["O_b"][:, :], ALU.add).then_inc(xn_kept, 1)

            pool.wait_ge(bias_loaded, 16)
            keep_xn(0, 0, 0)
            keep_xn(1, 1, 1)

            def step(t, slot, n):
                if n + 2 < TILES:
                    keep_xn(t + 2, (slot + 2) % SLOTS, n + 2)
                pool.wait_ge(prob_ready, t + 1)
                if n >= SLOTS:
                    pool.wait_ge(x1_summed, t - SLOTS + 1)
                shape = [P, HEADS, HEADS, DH]
                v = qkv[:, slot, 2 * D:3 * D].rearrange("p (g d) -> p g d", g=HEADS)
                nc.gpsimd.tensor_tensor(vprod[:, slot, :, :].rearrange("p g (h d) -> p g h d", h=HEADS),
                                        bcast(prob[:, slot, :, :].rearrange("p h g -> p g h"), 3, shape),
                                        bcast(v, 2, shape), ALU.mult).then_inc(vprod_ready, 1)
            over_tiles(pool, step)


GNN_KEPT = dict(O_w=[P, KC, D], f1_w=[P, KC, 2 * D], f2_w=[P, 2 * KC, D], w_ih=[P, KC, 3 * D], w_hh=[P, KC, 3 * D],
                f1_b=[P, 2 * KC], b_ih=[P, 3 * KC], b_hh=[P, 3 * KC],
                ln1_w=[P, D], ln1_b=[P, D], ln2_w=[P, D], ln2_b=[P, D], f2_b=[P, D])


def load_kept(eng, names, ins, keep, loaded):
    for name, shape in names.items():
        whole = tuple(slice(None) for _ in shape)
        eng.dma_start(keep[name][whole], ins[name]).then_inc(loaded, 16)
    eng.wait_ge(loaded, 16 * len(names))


def pipeline(eng, count, slots, stages, warmup=0):
    span = max(lag for _, lag in stages)
    start = -(-(span + warmup + slots) // slots) * slots
    loops = (count - 1 - warmup - start) // slots

    def step(i, n):
        for work, lag in stages:
            if 0 <= n - lag < count:
                work(i - lag, (n - lag) % slots, n - lag)

    for i in range(start):
        step(i, i)
    with eng.Fori(0, loops) as k:
        for h in range(slots):
            step(k * slots + start + h, start + h)
    for i in range(start + loops * slots, count + span):
        step(i, i)


def tile_of(array, t):
    return array[:, bass.ds(t, 1), :].rearrange("p a d -> p (a d)")


def graph_phase(nc, X, XN, X1, S, x1_dram, ins, keep):
    FC = 2 * D // P
    with ExitStack() as ctx:
        sb = lambda name, shape, dt=F32: ctx.enter_context(nc.sbuf_tensor("graph_" + name, shape, dt))
        sem = lambda name: ctx.enter_context(nc.semaphore("graph_" + name))
        psum = lambda name, shape: ctx.enter_context(nc.psum_tensor("graph_" + name, shape, F32))
        ident = keep["ident"]
        src = sb("src", [P, COLS], I32)
        dst_f = sb("dst_f", [P, COLS + AHEAD * GE])
        dst_more = sb("dst_more", [P, GE])
        iota_w = sb("iota_w", [P, WINDOW])
        iota_more = sb("iota_more", [P, 1 + TILES // 2])
        ends = sb("ends", [P, 2, GROUPS])
        ends_all = sb("ends_all", [P, 2, GROUPS])
        ends_i = sb("ends_i", [P, 2, GROUPS], I32)
        least = sb("least", [P, GROUPS])
        extra_f = sb("extra_f", [P, GROUPS])
        extra_i = sb("extra_i", [P, GROUPS], I32)
        scan = sb("scan", [P, 2, GROUPS])
        table = sb("table", [P, GROUPS + 1], I32)
        words = sb("words", [P, BATCHES], I32)
        word = sb("word", [P, BATCHES])
        has_more = sb("has_more", [P, BATCHES])
        batch_least = sb("batch_least", [P, BATCHES])
        upto = sb("upto", [P, 1 + TILES])
        turns = sb("turns", [P, TILES], I32)
        number = sb("number", [P, TILES])
        last = sb("last", [P, TILES])
        index = sb("index", [P, SLOTS, GE], I32)
        rows = sb("rows", [P, SLOTS, GE, D])
        onehot = sb("onehot", [P, SLOTS, GE, WINDOW])
        part_ps = psum("part_ps", [P, SLOTS, 512])
        attn = sb("attn", [P, SLOTS, D])
        attnT = sb("attnT", [P, KC, P])
        h0 = sb("h0", [P, SLOTS, D])
        h1 = sb("h1", [P, D])
        h1T = sb("h1T", [P, SLOTS, KC, P])
        fT = sb("fT", [P, SLOTS, FC, P])
        scratch = fT[:, :, :, :].rearrange("p s k n -> p (s k n)")
        dst = scratch[:, 0:COLS].bitcast(I32)
        reaches = scratch[:, COLS:COLS + TILES * BATCHES].rearrange("p (t b) -> p t b", b=BATCHES)
        r = sb("r", [P, SLOTS, D])
        h2 = sb("h2", [P, D])
        h2T = sb("h2T", [P, SLOTS, KC, P])
        rz = sb("rz", [P, SLOTS, 2 * KC, P])
        rn = sb("rn", [P, KC, P])
        new = rn
        diff = sb("diff", [P, SLOTS, KC, P])
        yT = diff
        stats = sb("stats", [P, 2, SLOTS, 6])
        moments = sb("moments", [P, 2, SLOTS, 2])
        std = sb("std", [P, 2, SLOTS])
        rstd = sb("rstd", [P, 2, SLOTS])
        w_rz = sb("w_rz", [P, KC, 2 * D])
        b_rz = sb("b_rz", [P, 2 * KC])
        ln1_b_f2_b = sb("ln1_b_f2_b", [P, D])
        turned_ps = psum("turned_ps", [P, 512])
        out_ps = psum("out_ps", [P, 2, D])
        f_ps = psum("f_ps", [P, FC, P])
        rz_ps = psum("rz_ps", [P, 2 * KC, P])
        n_ps = psum("n_ps", [P, 2, KC, P])

        src_loaded, dst_loaded, kept_loaded = sem("src_loaded"), sem("dst_loaded"), sem("kept_loaded")
        iota_made, ends_made, ends_reduced = sem("iota_made"), sem("ends_made"), sem("ends_reduced")
        table_made, sums_made = sem("table_made"), sem("sums_made")
        index_made, index_seen = sem("index_made"), sem("index_seen")
        rows_loaded = [sem(f"rows_loaded_{s}") for s in range(SLOTS)]
        first_onehot, first_summed = sem("first_onehot"), sem("first_summed")
        more_onehot, more_summed = sem("more_onehot"), sem("more_summed")
        group_summed = sem("group_summed")
        attn_made, attnT_done, attnT_copied = sem("attn_made"), sem("attnT_done"), sem("attnT_copied")
        attn_out_done, var1_made, std1_made = sem("attn_out_done"), sem("var1_made"), sem("std1_made")
        h1_made, h1T_done, h1T_copied = sem("h1_made"), sem("h1T_done"), sem("h1T_copied")
        f_done, fT_made, f_out_done = sem("f_done"), sem("fT_made"), sem("f_out_done")
        var2_made, std2_made = sem("var2_made"), sem("std2_made")
        h2_made, h2T_done, h2T_copied = sem("h2_made"), sem("h2T_done"), sem("h2T_copied")
        rz_done, n_done, rz_made, rn_made, n_made = sem("rz_done"), sem("n_done"), sem("rz_made"), sem("rn_made"), sem("n_made")
        yT_made, y_done, y_added = sem("yT_made"), sem("y_done"), sem("y_added")
        block = ctx.enter_context(nc.Block())

        def within(value, greatest, why):
            return nc.s_assert_within(value, 0, greatest, skip_runtime_bounds_check_because=why)

        def unpack(eng, g):
            packed = eng.value_load(table[0:1, bass.ds(g, 1)], min_val=0, max_val=(1 << 31) - 1)
            tile = eng.snap(within(packed & (TILE_MAX - 1), TILES - 1, "a tile of nodes"))
            more = eng.snap((packed >> TILE_BITS) & (TILE_MAX - 1), min_val=0, max_val=TILES // 2)
            before = eng.snap(packed >> (2 * TILE_BITS), min_val=0, max_val=GROUPS * TILES)
            return tile, more, before

        def tile_in(eng, packed, at):
            return eng.snap(within((packed >> at) & (TILE_MAX - 1), TILES - 1, "a tile of nodes"))

        def over_steps(eng, plain, general, parts):
            def batch(b, after):
                packed = eng.value_load(words[0:1, bass.ds(b, 1)], min_val=0, max_val=(2 << AT_MORE) - 1)
                with eng.If(packed < (1 << AT_MORE)):
                    for slot in range(SLOTS):
                        plain(b * SLOTS + slot, slot, b, packed)
                        after(slot)
                with eng.Else():
                    for slot in range(SLOTS):
                        general(b * SLOTS + slot, slot, b)
                        after(slot)

            def step(i, slot, n):
                def part(k):
                    for work, lag in parts[k]:
                        if 0 <= n - lag < TILES:
                            work(i - lag, (n - lag) % SLOTS, n - lag)
                if n >= TILES:
                    for k in range(SLOTS):
                        part(k)
                    return
                turn = eng.value_load(turns[0:1, bass.ds(i, 1)], min_val=0, max_val=(1 << 3 * BATCH_BITS) - 1)
                mask = (1 << BATCH_BITS) - 1
                first = eng.snap(turn & mask, min_val=0, max_val=BATCHES)
                count = eng.snap((turn >> BATCH_BITS) & mask, min_val=0, max_val=BATCHES)
                last = eng.snap(within(turn >> (2 * BATCH_BITS), BATCHES - 1, "a batch"))
                with eng.If(count > 1):
                    with eng.Fori(0, count - 1) as k:
                        batch(eng.snap(within(first + k, BATCHES - 1, "a batch of the step")), lambda slot: None)
                with eng.Else():
                    eng.nop()
                with eng.If(count > 0):
                    batch(last, part)
                with eng.Else():
                    for k in range(SLOTS):
                        part(k)
            span = max(lag for stages in parts for _, lag in stages)
            pipeline(eng, TILES + span, SLOTS, [(step, 0)], span)

        @block.sync
        def _(sp):
            sp.dma_start(dst[:, :], ins["dst"]).then_inc(dst_loaded, 16)
            sp.dma_start(src[:, :], ins["src"]).then_inc(src_loaded, 16)
            load_kept(sp, GNN_KEPT, ins, keep, kept_loaded)

        @block.gpsimd
        def _(pool):
            nc.gpsimd.iota(iota_w[:, :], [[1, WINDOW]], base=0, channel_multiplier=0, allow_small_or_imprecise_dtypes=True)
            nc.gpsimd.iota(iota_more[:, :], [[WINDOW, 1 + TILES // 2]], base=0, channel_multiplier=0, allow_small_or_imprecise_dtypes=True)
            pool.drain().then_inc(iota_made, 1)
            pool.wait_ge(ends_made, 1)
            nc.gpsimd.partition_all_reduce(ends_all[:, :, :].rearrange("p a g -> p (a g)"), ends[:, :, :].rearrange("p a g -> p (a g)"),
                                           P, bass.bass_isa.ReduceOp.max).then_inc(ends_reduced, 1)
            pool.wait_ge(src_loaded, 16)

            def gather(g, slot, n):
                if n >= SLOTS:
                    pool.wait_ge(group_summed, g - SLOTS + 1)
                nc.gpsimd.tensor_copy(index[:, slot, :], src[:, bass.ds(g * GE, GE)]).then_inc(index_made, 1)
                pool.wait_ge(index_made, g + 1)
                pool.sem_inc(index_seen, 1)
                for j in range(GE):
                    nc.gpsimd.indirect_dma_start(out=rows[:, slot, j, :], out_offset=None, in_=x1_dram,
                                                 in_offset=bass.IndirectOffsetOnAxis(ap=index[:, slot, j:j + 1].bitcast(U32), axis=0)).then_inc(rows_loaded[slot], 16)
            pipeline(pool, GROUPS, SLOTS, [(gather, 0)])

        @block.vector
        def _(dve):
            dve.wait_ge(dst_loaded, 16)
            nc.vector.memset(dst_f[:, COLS:], 0.0)
            nc.vector.tensor_copy(dst_f[:, 0:COLS], dst[:, :])
            dve.drain()
            by_group = dst_f[:, 0:COLS].rearrange("p (g j) -> p g j", j=GE)
            nc.vector.tensor_reduce(ends[:, 0, :], by_group, AX.X, ALU.max)
            nc.vector.tensor_reduce(ends[:, 1, :], by_group, AX.X, ALU.min)
            dve.drain()
            nc.vector.tensor_scalar(ends[:, 1, :], ends[:, 1, :], -1.0, None, ALU.mult).then_inc(ends_made, 1)
            dve.wait_ge(iota_made, 1)
            dve.wait_ge(ends_reduced, 1)
            nc.vector.tensor_scalar(ends_all[:, 1, :], ends_all[:, 1, :], -1.0, None, ALU.mult)
            dve.drain()
            nc.vector.tensor_copy(ends_i[:, :, :], ends_all[:, :, :])
            dve.drain()
            nc.vector.tensor_scalar(ends_i[:, :, :], ends_i[:, :, :], P.bit_length() - 1, None, ALU.arith_shift_right)
            nc.vector.memset(table[:, :], 0)
            nc.vector.memset(upto[:, 0:1], 0.0)
            dve.drain()
            nc.vector.tensor_tensor(extra_i[:, :], ends_i[:, 0, :], ends_i[:, 1, :], ALU.subtract)
            nc.vector.tensor_copy(least[:, :], ends_i[:, 1, :])
            dve.drain()
            nc.vector.tensor_scalar(extra_i[:, :], extra_i[:, :], 1, None, ALU.arith_shift_right)
            dve.drain()
            nc.vector.tensor_copy(extra_f[:, :], extra_i[:, :])
            nc.vector.tensor_copy(scan[:, 0, :], extra_i[:, :])
            nc.vector.tensor_reduce(batch_least[:, :], least[:, :].rearrange("p (b s) -> p b s", s=SLOTS), AX.X, ALU.min)
            dve.drain()
            shape = [P, TILES, BATCHES]
            nc.vector.tensor_tensor(reaches[:, :, :], bcast(iota_w[:, 0:TILES], 2, shape), bcast(batch_least[:, :], 1, shape), ALU.is_ge)
            dve.drain()
            nc.vector.tensor_tensor(reaches[:, :, :], reaches[:, :, :], bcast(iota_w[:, 1:1 + BATCHES], 1, shape), ALU.mult)
            dve.drain()
            nc.vector.tensor_reduce(upto[:, 1:], reaches[:, :, :], AX.X, ALU.max)
            dve.drain()
            nc.vector.tensor_tensor(number[:, :], upto[:, 1:], upto[:, 0:TILES], ALU.subtract)
            nc.vector.tensor_scalar(last[:, :], upto[:, 1:], -1.0, 0.0, ALU.add, ALU.max)
            dve.drain()
            nc.vector.scalar_tensor_tensor(number[:, :], last[:, :], float(1 << BATCH_BITS), number[:, :], ALU.mult, ALU.add)
            dve.drain()
            nc.vector.scalar_tensor_tensor(turns[:, :], number[:, :], float(1 << BATCH_BITS), upto[:, 0:TILES], ALU.mult, ALU.add)
            by_batch = least[:, :].rearrange("p (b s) -> p b s", s=SLOTS)
            nc.vector.tensor_reduce(has_more[:, :], extra_f[:, :].rearrange("p (b s) -> p b s", s=SLOTS), AX.X, ALU.max)
            dve.drain()
            nc.vector.tensor_scalar(word[:, :], has_more[:, :], 0.0, None, ALU.is_gt)
            nc.vector.scalar_tensor_tensor(by_group, bcast(least[:, :], 2, [P, GROUPS, GE]), -float(P), by_group, ALU.mult, ALU.add)
            dve.drain()
            for slot in reversed(range(SLOTS)):
                nc.vector.scalar_tensor_tensor(word[:, :], word[:, :], float(TILE_MAX), by_batch[:, :, slot], ALU.mult, ALU.add)
                dve.drain()
            nc.vector.tensor_copy(words[:, :], word[:, :])
            now, reach = 0, 1
            while reach < GROUPS:
                nc.vector.tensor_copy(scan[:, 1 - now, 0:reach], scan[:, now, 0:reach])
                nc.vector.tensor_tensor(scan[:, 1 - now, reach:], scan[:, now, reach:], scan[:, now, 0:GROUPS - reach], ALU.add)
                dve.drain()
                now, reach = 1 - now, 2 * reach
            nc.vector.tensor_tensor(scan[:, now, :], scan[:, now, :], extra_f[:, :], ALU.subtract)
            dve.drain()
            nc.vector.scalar_tensor_tensor(extra_f[:, :], scan[:, now, :], float(TILE_MAX), extra_f[:, :], ALU.mult, ALU.add)
            dve.drain()
            nc.vector.scalar_tensor_tensor(table[:, 0:GROUPS], extra_f[:, :], float(TILE_MAX), ends_i[:, 1, :], ALU.mult, ALU.add)
            dve.drain().then_inc(table_made, 1)
            dve.wait_ge(table_made, 1)

            def make_onehot(slot, nodes, made):
                nc.vector.tensor_tensor(onehot[:, slot, :, :], bcast(iota_w[:, :], 1, [P, GE, WINDOW]),
                                        bcast(nodes, 2, [P, GE, WINDOW]), ALU.is_equal).then_inc(made, 1)

            def make_first(g, slot):
                make_onehot(slot, dst_f[:, bass.ds(g * GE, GE)], first_onehot)

            def add_part(tile, slot):
                s = S[:, bass.ds(tile, WINDOW // P), :]
                return nc.vector.tensor_tensor(s, s, part_ps[:, slot, :].rearrange("p (w d) -> p w d", d=D), ALU.add)

            def general(g, slot, b):
                tile, more, before = unpack(dve, g)
                make_first(g + AHEAD, (slot + AHEAD) % SLOTS)
                dve.wait_ge(first_summed, g + 1)
                add_part(tile, slot)
                with dve.If(more > 0):
                    with dve.Fori(0, more) as j:
                        to = within(tile + 2 * j + 2, TILES - 1, "a tile of nodes up to that of the group's greatest dst")
                        nc.vector.tensor_scalar(dst_more[:, :], dst_f[:, bass.ds(g * GE, GE)], iota_more[:, bass.ds(within(j + 1, TILES // 2, "a window"), 1)], None, ALU.subtract)
                        dve.drain()
                        make_onehot(slot, dst_more[:, :], more_onehot)
                        dve.wait_ge(more_summed, before + j + 1)
                        add_part(to, slot)
                with dve.Else():
                    dve.nop()
                dve.drain().then_inc(group_summed, 1)

            def plain(g, slot, b, packed):
                make_first(g + AHEAD, (slot + AHEAD) % SLOTS)
                dve.wait_ge(first_summed, g + 1)
                add_part(tile_in(dve, packed, TILE_BITS * slot), slot)
                dve.drain().then_inc(group_summed, 1)

            def gate(t, slot, n):
                if n >= SLOTS:
                    dve.wait_ge(attnT_done, t - SLOTS + 1)
                nc.vector.tensor_tensor(attn[:, slot, :], tile_of(X1, t), tile_of(S, t), ALU.mult).then_inc(attn_made, 1)

            def variance(which, values, slot, made):
                dve.drain()
                nc.vector.bn_stats(stats[:, which, slot, :], values[:, slot, :])
                dve.drain()
                nc.vector.bn_aggr(moments[:, which, slot, :], stats[:, which, slot, :]).then_inc(made, 1)

            def center(which, values, w, slot):
                nc.vector.reciprocal(rstd[:, which, slot:slot + 1], std[:, which, slot:slot + 1])
                nc.vector.scalar_tensor_tensor(values[:, slot, :], values[:, slot, :], moments[:, which, slot, 0:1], w[:, :], ALU.subtract, ALU.mult)
                dve.drain()

            def add_attn(t, slot, n):
                dve.wait_ge(attn_out_done, t + 1)
                nc.vector.tensor_tensor(h0[:, slot, :], out_ps[:, 0, :], tile_of(XN, t), ALU.add)
                variance(0, h0, slot, var1_made)

            def norm1(t, slot, n):
                dve.wait_ge(std1_made, t + 1)
                if n:
                    dve.wait_ge(h1T_done, t)
                center(0, h0, keep["ln1_w"], slot)
                nc.vector.scalar_tensor_tensor(h1[:, :], h0[:, slot, :], rstd[:, 0, slot:slot + 1], keep["ln1_b"][:, :], ALU.mult, ALU.add).then_inc(h1_made, 1)
                nc.vector.scalar_tensor_tensor(tile_of(XN, t), h0[:, slot, :], rstd[:, 0, slot:slot + 1], ln1_b_f2_b[:, :], ALU.mult, ALU.add)

            def add_ffn(t, slot, n):
                dve.wait_ge(f_out_done, t + 1)
                nc.vector.tensor_tensor(r[:, slot, :], out_ps[:, 1, :], tile_of(XN, t), ALU.add)
                variance(1, r, slot, var2_made)

            def norm2(t, slot, n):
                dve.wait_ge(std2_made, t + 1)
                if n:
                    dve.wait_ge(h2T_done, t)
                center(1, r, keep["ln2_w"], slot)
                nc.vector.scalar_tensor_tensor(h2[:, :], r[:, slot, :], rstd[:, 1, slot:slot + 1], keep["ln2_b"][:, :], ALU.mult, ALU.add).then_inc(h2_made, 1)

            def reset(t, slot, n):
                dve.wait_ge(n_done, t + 1)
                dve.wait_ge(rz_made, t + 1)
                if n:
                    dve.wait_ge(yT_made, t)
                for k in range(KC):
                    nc.vector.scalar_tensor_tensor(rn[:, k, :], n_ps[:, 1, k, :], keep["b_hh"][:, 2 * KC + k:2 * KC + k + 1],
                                                   rz[:, slot, k, :], ALU.add, ALU.mult)
                dve.drain()
                nc.vector.tensor_tensor(rn[:, :, :], rn[:, :, :], n_ps[:, 0, :, :], ALU.add).then_inc(rn_made, 1)

            def blend(t, slot, n):
                dve.wait_ge(n_made, t + 1)
                if n >= SLOTS:
                    dve.wait_ge(y_done, t - SLOTS + 1)
                nc.vector.tensor_tensor(diff[:, slot, :, :], h2T[:, slot, :, :], new[:, :, :], ALU.subtract)
                dve.drain()
                nc.vector.tensor_tensor(diff[:, slot, :, :], diff[:, slot, :, :], rz[:, slot, KC:2 * KC, :], ALU.mult)
                dve.drain()
                nc.vector.tensor_tensor(yT[:, slot, :, :], diff[:, slot, :, :], new[:, :, :], ALU.add).then_inc(yT_made, 1)

            def add_y(t, slot, n):
                dve.wait_ge(y_done, t + 1)
                nc.vector.tensor_tensor(tile_of(X, t), tile_of(X, t), turned_ps[:, 0:D], ALU.add).then_inc(y_added, 1)

            dve.wait_ge(kept_loaded, 16 * len(GNN_KEPT))
            nc.vector.tensor_tensor(w_rz[:, :, :], keep["w_ih"][:, :, 0:2 * D], keep["w_hh"][:, :, 0:2 * D], ALU.add)
            nc.vector.tensor_tensor(b_rz[:, :], keep["b_ih"][:, 0:2 * KC], keep["b_hh"][:, 0:2 * KC], ALU.add)
            nc.vector.tensor_tensor(ln1_b_f2_b[:, :], keep["ln1_b"][:, :], keep["f2_b"][:, :], ALU.add)
            dve.drain().then_inc(sums_made, 1)
            for g in range(AHEAD):
                make_first(g, g)
            over_steps(dve, plain, general, [[(norm1, 2), (reset, 7)], [(add_y, 8), (add_attn, 1), (norm2, 5), (blend, 7)], [(gate, 0), (add_ffn, 4)]])

        @block.scalar
        def _(act):
            def copy_attnT(t, slot, n):
                act.wait_ge(attnT_done, t + 1)
                if n:
                    act.wait_ge(attn_out_done, t)
                nc.scalar.activation(attnT[:, :, :].rearrange("p c n -> p (c n)"), turned_ps[:, 0:D], ACT.Copy).then_inc(attnT_copied, 1)

            def root1(t, slot, n):
                act.wait_ge(var1_made, t + 1)
                nc.scalar.activation(std[:, 0, slot:slot + 1], moments[:, 0, slot, 1:2], ACT.Sqrt, bias=keep["eps"][:, 0:1]).then_inc(std1_made, 1)

            def copy_h1T(t, slot, n):
                act.wait_ge(h1T_done, t + 1)
                if n >= SLOTS:
                    act.wait_ge(f_done, t - SLOTS + 1)
                nc.scalar.activation(h1T[:, slot, :, :].rearrange("p c n -> p (c n)"), turned_ps[:, 0:D], ACT.Copy).then_inc(h1T_copied, 1)

            def relu(t, slot, n):
                act.wait_ge(f_done, t + 1)
                if n >= SLOTS:
                    act.wait_ge(f_out_done, t - SLOTS + 1)
                for k in range(FC):
                    nc.scalar.activation(fT[:, slot, k, :], f_ps[:, k, :], ACT.Relu, bias=keep["f1_b"][:, k:k + 1])
                act.drain().then_inc(fT_made, 1)

            def root2(t, slot, n):
                act.wait_ge(var2_made, t + 1)
                nc.scalar.activation(std[:, 1, slot:slot + 1], moments[:, 1, slot, 1:2], ACT.Sqrt, bias=keep["eps"][:, 0:1]).then_inc(std2_made, 1)

            def copy_h2T(t, slot, n):
                act.wait_ge(h2T_done, t + 1)
                if n >= SLOTS:
                    act.wait_ge(yT_made, t - SLOTS + 1)
                nc.scalar.activation(h2T[:, slot, :, :].rearrange("p c n -> p (c n)"), turned_ps[:, 0:D], ACT.Copy).then_inc(h2T_copied, 1)

            def sigmoid(t, slot, n):
                act.wait_ge(rz_done, t + 1)
                if n >= SLOTS:
                    act.wait_ge(yT_made, t - SLOTS + 1)
                for k in range(2 * KC):
                    nc.scalar.activation(rz[:, slot, k, :], rz_ps[:, k, :], ACT.Sigmoid, bias=b_rz[:, k:k + 1])
                act.drain().then_inc(rz_made, 1)

            def tanh(t, slot, n):
                act.wait_ge(rn_made, t + 1)
                for k in range(KC):
                    nc.scalar.activation(new[:, k, :], rn[:, k, :], ACT.Tanh, bias=keep["b_ih"][:, 2 * KC + k:2 * KC + k + 1])
                act.drain().then_inc(n_made, 1)

            act.wait_ge(sums_made, 1)
            pipeline(act, TILES, SLOTS, [(copy_attnT, 1), (relu, 3), (copy_h1T, 2), (tanh, 7), (copy_h2T, 5), (root1, 1), (root2, 4), (sigmoid, 6)])

        @block.tensor
        def _(pe):
            def sum_window(slot, done):
                for w in range(WINDOW // P):
                    for e in range(GE):
                        mm = nc.tensor.matmul(part_ps[:, slot, w * D:(w + 1) * D], onehot[:, slot, e, w * P:(w + 1) * P],
                                              rows[:, slot, e, :], start=(e == 0), stop=(e == GE - 1))
                mm.then_inc(done, 1)

            def first_window(g, slot, b):
                pe.wait_ge(rows_loaded[slot], b * (GE * 16) + GE * 16)
                pe.wait_ge(first_onehot, g + 1)
                sum_window(slot, first_summed)

            def general(g, slot, b):
                _, more, before = unpack(pe, g)
                first_window(g, slot, b)
                with pe.If(more > 0):
                    with pe.Fori(0, more) as j:
                        pe.wait_ge(more_onehot, before + j + 1)
                        sum_window(slot, more_summed)
                with pe.Else():
                    pe.nop()

            def plain(g, slot, b, packed):
                first_window(g, slot, b)

            TURNED = ((attnT_copied, 1), (y_added, 8), (h1T_copied, 2), (h2T_copied, 5))

            def turned_free(t, n, user):
                lag = TURNED[user][1]
                for back in range(1, len(TURNED) + 1):
                    emptied, other = TURNED[(user - back) % len(TURNED)]
                    behind = other - lag + (1 if back > user else 0)
                    if 0 <= n - behind < TILES:
                        pe.wait_ge(emptied, t - behind + 1)
                        return

            def transpose(source, made, done, user):
                def stage(t, slot, n):
                    whole = source[:, slot, :] if len(source.shape) == 3 else source
                    pe.wait_ge(made, t + 1)
                    turned_free(t, n, user)
                    for c in range(KC):
                        mm = nc.tensor.transpose(turned_ps[:, c * P:(c + 1) * P], whole[:, c * P:(c + 1) * P], ident[:, :])
                    mm.then_inc(done, 1)
                return stage
            transpose_attn = transpose(attn, attn_made, attnT_done, 0)
            transpose_h1 = transpose(h1, h1_made, h1T_done, 2)
            transpose_h2 = transpose(h2, h2_made, h2T_done, 3)
            by_row = yT[:, :, :, :].rearrange("p s c n -> p s (c n)")
            transpose_y = transpose(by_row, yT_made, y_done, 1)

            def project(t, slot, n):
                pe.wait_ge(attnT_copied, t + 1)
                if n:
                    pe.wait_ge(var1_made, t)
                if n >= 4:
                    pe.wait_ge(var2_made, t - 3)
                for c in range(KC):
                    mm = nc.tensor.matmul(out_ps[:, 0, :], attnT[:, c, :], keep["O_w"][:, c, :], start=(c == 0), stop=(c == KC - 1))
                mm.then_inc(attn_out_done, 1)

            def by_feature(ps, weights, chunks, first, hT, slot):
                for k in range(chunks):
                    for c in range(KC):
                        mm = nc.tensor.matmul(ps[:, k, :], weights[:, c, first + k * P:first + (k + 1) * P], hT[:, slot, c, :],
                                              start=(c == 0), stop=(c == KC - 1))
                return mm

            def up(t, slot, n):
                pe.wait_ge(h1T_copied, t + 1)
                if n:
                    pe.wait_ge(fT_made, t)
                by_feature(f_ps, keep["f1_w"], FC, 0, h1T, slot).then_inc(f_done, 1)

            def down(t, slot, n):
                pe.wait_ge(fT_made, t + 1)
                if n:
                    pe.wait_ge(var2_made, t)
                if n + 3 < TILES:
                    pe.wait_ge(var1_made, t + 4)
                for k in range(FC):
                    mm = nc.tensor.matmul(out_ps[:, 1, :], fT[:, slot, k, :], keep["f2_w"][:, k, :], start=(k == 0), stop=(k == FC - 1))
                mm.then_inc(f_out_done, 1)

            def gates(t, slot, n):
                pe.wait_ge(h2T_copied, t + 1)
                if n:
                    pe.wait_ge(rz_made, t)
                by_feature(rz_ps, w_rz, 2 * KC, 0, h2T, slot).then_inc(rz_done, 1)
                if n:
                    pe.wait_ge(rn_made, t)
                by_feature(n_ps[:, 1], keep["w_hh"], KC, 2 * D, h2T, slot)
                by_feature(n_ps[:, 0], keep["w_ih"], KC, 2 * D, h2T, slot).then_inc(n_done, 1)

            pe.wait_ge(table_made, 1)
            pe.wait_ge(sums_made, 1)
            over_steps(pe, plain, general, [[(transpose_attn, 1), (up, 3)], [(transpose_y, 8), (project, 1), (transpose_h1, 2)],
                                            [(transpose_h2, 5), (down, 4), (gates, 6)]])


EXPERTS, HIDDEN, TOP = 8, 1024, 2
HC = HIDDEN // P
SG = 2
SROWS = SG * P
MAX_SG = (TOP * NODES + EXPERTS * SROWS) // SROWS
SLOT_ROWS = MAX_SG * SROWS
FAR = -3e38
MOE_KEPT = dict(wg=[P, KC, EXPERTS], bg=[P, EXPERTS], b1=[P, EXPERTS * HC], b2=[P, EXPERTS, D])


class Weights:
    def __init__(self, nc, ctx, w1_in, w2_in):
        sb = lambda name, shape: ctx.enter_context(nc.sbuf_tensor(name, shape, F32))
        self.nc, self.w1_in, self.w2_in = nc, w1_in, w2_in
        self.w1_whole, self.w2_whole = sb("w1_whole", [P, KC, HIDDEN]), sb("w2_whole", [P, HC, D])
        self.w1, self.w2 = sb("w1", [P, 2, PARTS, KC, HIDDEN]), sb("w2", [P, 2, PARTS, HC, D])
        self.loaded, self.high_made, self.split_made, self.seen = [
            ctx.enter_context(nc.semaphore(f"weights_{name}")) for name in ("loaded", "high_made", "split_made", "seen")]

    def load(self, pool, e):
        pool.dma_start(self.w1_whole[:, :, :], self.w1_in[bass.ds(e, 1), :, :, :].rearrange("a p c h -> p (a c) h")).then_inc(self.loaded, 16)
        pool.dma_start(self.w2_whole[:, :, :], self.w2_in[bass.ds(e, 1), :, :, :].rearrange("a p c h -> p (a c) h")).then_inc(self.loaded, 16)

    def split(self, pool, e, slot):
        nc = self.nc
        pool.wait_ge(self.loaded, e * 32 + 32)
        pool.sem_inc(self.seen, 1)
        for whole, parts in ((self.w1_whole, self.w1), (self.w2_whole, self.w2)):
            nc.gpsimd.tensor_copy(parts[:, slot, 0, :, :].bitcast(F32R), whole[:, :, :])
        pool.drain().then_inc(self.high_made, 1)
        pool.wait_ge(self.high_made, e + 1)
        pool.sem_inc(self.seen, 1)
        for whole, parts in ((self.w1_whole, self.w1), (self.w2_whole, self.w2)):
            nc.gpsimd.tensor_tensor(parts[:, slot, 1, :, :].bitcast(F32R), whole[:, :, :], parts[:, slot, 0, :, :], ALU.subtract)
        pool.drain().then_inc(self.split_made, 1)
        pool.wait_ge(self.split_made, e + 1)
        pool.sem_inc(self.seen, 1)


def route_phase(nc, X, XN, xs_dram, prob, place, groups, weights, ins, keep):
    with ExitStack() as ctx:
        sb = lambda name, shape, dt=F32: ctx.enter_context(nc.sbuf_tensor("route_" + name, shape, dt))
        sem = lambda name: ctx.enter_context(nc.semaphore("route_" + name))
        psum = lambda name, shape: ctx.enter_context(nc.psum_tensor("route_" + name, shape, F32))
        ident, wg, bg = keep["ident"], keep["wg"], keep["bg"]
        stats = sb("stats", [P, TILES, 6])
        moments = sb("moments", [P, TILES, 2])
        std = sb("std", [P, TILES])
        rstd = sb("rstd", [P, TILES])
        xn = sb("xn", [P, SLOTS, D])
        xnT = sb("xnT", [P, SLOTS, KC, P])
        gate = sb("gate", [P, TILES, EXPERTS])
        cand = sb("cand", [P, TILES, EXPERTS])
        chosen = sb("chosen", [P, TOP, TILES, EXPERTS])
        either = sb("either", [P, TILES, EXPERTS])
        best = sb("best", [P, TOP, TILES])
        top = sb("top", [P, TILES])
        ratio = sb("ratio", [P, TILES])
        scan = sb("scan", [P, 2, TILES, EXPERTS])
        rank = sb("rank", [P, TILES, EXPERTS])
        node = sb("node", [P, TILES])
        valid = sb("valid", [P, TILES])
        spare = sb("spare", [P, TOP])
        order = sb("order", [P, EXPERTS])
        below = sb("below", [P, P])
        ones = sb("ones", [P, P])
        number = sb("number", [P, EXPERTS])
        number_i = sb("number_i", [P, EXPERTS], I32)
        starts = sb("starts", [P, 2, EXPERTS])
        place_f = sb("place_f", [P, TOP, TILES])
        scatter_to = sb("scatter_to", [P, TILES, TOP], I32)
        index = sb("index", [P, SLOTS, TOP], I32)
        row = sb("row", [P, SLOTS, D])
        xnT_ps = psum("xnT_ps", [P, 512])
        gate_ps = psum("gate_ps", [P, 512])
        prefix_ps = psum("prefix_ps", [P, 512])
        count_ps = psum("count_ps", [P, 512])
        var_made, std_made, norm_made = sem("var_made"), sem("std_made"), sem("norm_made")
        xnT_done, xnT_copied, gate_done = sem("xnT_done"), sem("xnT_copied"), sem("gate_done")
        iotas_made, either_made, counted = sem("iotas_made"), sem("either_made"), sem("counted")
        margin_made, ratio_made, place_made = sem("margin_made"), sem("ratio_made"), sem("place_made")
        index_made, index_seen, row_made = sem("index_made"), sem("index_seen"), sem("row_made")
        scattered = [sem(f"scattered_{s}") for s in range(SLOTS)]
        kept_loaded = sem("kept_loaded")
        block = ctx.enter_context(nc.Block())

        @block.sync
        def _(sp):
            load_kept(sp, MOE_KEPT, ins, keep, kept_loaded)

        @block.vector
        def _(dve):
            for t in range(TILES):
                nc.vector.bn_stats(stats[:, t, :], X[:, t, :])
            dve.drain()
            for t in range(TILES):
                nc.vector.bn_aggr(moments[:, t, :], stats[:, t, :])
            dve.drain().then_inc(var_made, 1)
            dve.wait_ge(std_made, 1)
            nc.vector.reciprocal(rstd[:, :], std[:, :])
            dve.drain()

            def norm(t, slot, n):
                if n >= SLOTS:
                    dve.wait_ge(xnT_copied, t - SLOTS + 1)
                nc.vector.tensor_scalar(xn[:, slot, :], tile_of(X, t), moments[:, bass.ds(t, 1), 0:1].rearrange("p a d -> p (a d)"),
                                        rstd[:, bass.ds(t, 1)], ALU.subtract, ALU.mult).then_inc(norm_made, 1)
            pipeline(dve, TILES, SLOTS, [(norm, 0)])

            full = [P, TILES, EXPERTS]
            dve.wait_ge(gate_done, TILES)
            dve.wait_ge(iotas_made, 1)
            nc.vector.tensor_tensor(gate[:, :, :], gate_ps[:, 0:TILES * EXPERTS].rearrange("p (t e) -> p t e", e=EXPERTS), bcast(bg[:, :], 1, full), ALU.add)
            nc.vector.tensor_scalar(valid[:, :], node[:, :], float(NODES), None, ALU.is_lt)
            nc.vector.tensor_scalar(below[:, :], below[:, :], 0.0, None, ALU.is_gt)
            nc.vector.memset(ones[:, :], 1.0)
            dve.drain()
            for c in range(TOP):
                nc.vector.tensor_reduce(best[:, c, :], gate[:, :, :], AX.X, ALU.max)
                dve.drain()
                nc.vector.tensor_tensor(cand[:, :, :], gate[:, :, :], bcast(best[:, c, :], 2, full), ALU.is_equal)
                dve.drain()
                nc.vector.tensor_tensor(cand[:, :, :], cand[:, :, :], bcast(order[:, :], 1, full), ALU.mult)
                dve.drain()
                nc.vector.tensor_reduce(top[:, :], cand[:, :, :], AX.X, ALU.max)
                dve.drain()
                nc.vector.tensor_tensor(chosen[:, c, :, :], cand[:, :, :], bcast(top[:, :], 2, full), ALU.is_equal)
                dve.drain()
                if c + 1 < TOP:
                    nc.vector.scalar_tensor_tensor(gate[:, :, :], chosen[:, c, :, :], FAR, gate[:, :, :], ALU.mult, ALU.add)
                nc.vector.tensor_tensor(chosen[:, c, :, :], chosen[:, c, :, :], bcast(valid[:, :], 2, full), ALU.mult)
                dve.drain()
            nc.vector.tensor_tensor(either[:, :, :], chosen[:, 0, :, :], chosen[:, 1, :, :], ALU.add).then_inc(either_made, 1)
            nc.vector.tensor_tensor(ratio[:, :], best[:, 1, :], best[:, 0, :], ALU.subtract).then_inc(margin_made, 1)

            dve.wait_ge(counted, 1)
            tile_counts = count_ps[:, 0:TILES * EXPERTS].rearrange("p (t e) -> p t e", e=EXPERTS)
            nc.vector.tensor_copy(scan[:, 0, :, :], tile_counts)
            dve.drain()
            now, reach = 0, 1
            while reach < TILES:
                nc.vector.tensor_copy(scan[:, 1 - now, 0:reach, :], scan[:, now, 0:reach, :])
                nc.vector.tensor_tensor(scan[:, 1 - now, reach:, :], scan[:, now, reach:, :], scan[:, now, 0:TILES - reach, :], ALU.add)
                dve.drain()
                now, reach = 1 - now, 2 * reach
            nc.vector.tensor_tensor(rank[:, :, :], scan[:, now, :, :], tile_counts, ALU.subtract)
            nc.vector.tensor_scalar(number[:, :], scan[:, now, TILES - 1, :], float(SROWS - 1), None, ALU.add)
            dve.drain()
            nc.vector.tensor_tensor(rank[:, :, :], rank[:, :, :], prefix_ps[:, 0:TILES * EXPERTS].rearrange("p (t e) -> p t e", e=EXPERTS), ALU.add)
            nc.vector.tensor_copy(number_i[:, :], number[:, :])
            dve.drain()
            nc.vector.tensor_scalar(number_i[:, :], number_i[:, :], SROWS.bit_length() - 1, None, ALU.arith_shift_right)
            dve.drain()
            nc.vector.tensor_scalar(number[:, :], number_i[:, :], 1.0, None, ALU.max)
            dve.drain()
            nc.vector.tensor_copy(starts[:, 0, :], number[:, :])
            dve.drain()
            now, reach = 0, 1
            while reach < EXPERTS:
                nc.vector.tensor_copy(starts[:, 1 - now, 0:reach], starts[:, now, 0:reach])
                nc.vector.tensor_tensor(starts[:, 1 - now, reach:], starts[:, now, reach:], starts[:, now, 0:EXPERTS - reach], ALU.add)
                dve.drain()
                now, reach = 1 - now, 2 * reach
            nc.vector.tensor_tensor(starts[:, now, :], starts[:, now, :], number[:, :], ALU.subtract)
            dve.drain()
            nc.vector.tensor_copy(groups[:, 0:EXPERTS], number[:, :])
            nc.vector.tensor_copy(groups[:, EXPERTS:2 * EXPERTS], starts[:, now, :])
            nc.vector.tensor_scalar(starts[:, now, :], starts[:, now, :], float(SROWS), None, ALU.mult)
            dve.drain()
            nc.vector.tensor_tensor(rank[:, :, :], rank[:, :, :], bcast(starts[:, now, :], 1, full), ALU.add)
            dve.drain()
            for c in range(TOP):
                nc.vector.tensor_tensor(cand[:, :, :], rank[:, :, :], chosen[:, c, :, :], ALU.mult)
                dve.drain()
                nc.vector.tensor_reduce(place_f[:, c, :], cand[:, :, :], AX.X, ALU.add)
                dve.drain()
            nc.vector.tensor_copy(place[:, :, :], place_f[:, :, :].rearrange("p c t -> p t c"))
            nc.vector.tensor_scalar(valid[:, :], valid[:, :], -1.0, 1.0, ALU.mult, ALU.add)
            dve.drain()
            for c in range(TOP):
                nc.vector.scalar_tensor_tensor(place_f[:, c, :], valid[:, :], spare[:, c:c + 1], place_f[:, c, :], ALU.mult, ALU.add)
            dve.drain()
            nc.vector.tensor_copy(scatter_to[:, :, :], place_f[:, :, :].rearrange("p c t -> p t c"))
            dve.wait_ge(ratio_made, 1)
            nc.vector.tensor_scalar(top[:, :], ratio[:, :], 1.0, None, ALU.add)
            dve.drain().then_inc(place_made, 1)
            nc.vector.reciprocal(top[:, :], top[:, :])
            dve.drain()
            nc.vector.tensor_copy(prob[:, :, 0], top[:, :])
            nc.vector.tensor_tensor(prob[:, :, 1], top[:, :], ratio[:, :], ALU.mult)

            def copy_row(t, slot, n):
                if n >= SLOTS:
                    dve.wait_ge(scattered[slot], 2 * 16 * (n // SLOTS) if isinstance(t, int) else (t - slot) // SLOTS * (2 * 16))
                nc.vector.tensor_copy(row[:, slot, :], tile_of(XN, t)).then_inc(row_made, 1)
            pipeline(dve, TILES, SLOTS, [(copy_row, 0)])

        @block.scalar
        def _(act):
            act.wait_ge(var_made, 1)
            nc.scalar.activation(std[:, :], moments[:, :, 1:2].rearrange("p t a -> p (t a)"), ACT.Sqrt, bias=keep["eps"][:, 0:1]).then_inc(std_made, 1)

            def copy(t, slot, n):
                act.wait_ge(xnT_done, t + 1)
                if n >= SLOTS:
                    act.wait_ge(gate_done, t - SLOTS + 1)
                nc.scalar.activation(tile_of(XN, t), xn[:, slot, :], ACT.Copy)
                nc.scalar.activation(xnT[:, slot, :, :].rearrange("p c n -> p (c n)"), xnT_ps[:, 0:D], ACT.Copy).then_inc(xnT_copied, 1)
            pipeline(act, TILES, SLOTS, [(copy, 0)])
            act.wait_ge(margin_made, 1)
            nc.scalar.activation(ratio[:, :], ratio[:, :], ACT.Exp).then_inc(ratio_made, 1)

        @block.tensor
        def _(pe):
            def transpose(t, slot, n):
                pe.wait_ge(norm_made, t + 1)
                if n:
                    pe.wait_ge(xnT_copied, t)
                for c in range(KC):
                    mm = nc.tensor.transpose(xnT_ps[:, c * P:(c + 1) * P], xn[:, slot, c * P:(c + 1) * P], ident[:, :])
                mm.then_inc(xnT_done, 1)

            def score(t, slot, n):
                pe.wait_ge(xnT_copied, t + 1)
                for c in range(KC):
                    mm = nc.tensor.matmul(gate_ps[:, bass.ds(t * EXPERTS, EXPERTS)], xnT[:, slot, c, :], wg[:, c, :], start=(c == 0), stop=(c == KC - 1))
                mm.then_inc(gate_done, 1)
            pe.wait_ge(kept_loaded, 16 * len(MOE_KEPT))
            pipeline(pe, TILES, SLOTS, [(transpose, 0), (score, 1)])
            pe.wait_ge(either_made, 1)
            flat = either[:, :, :].rearrange("p t e -> p (t e)")
            nc.tensor.matmul(prefix_ps[:, 0:TILES * EXPERTS], below[:, :], flat, start=True, stop=True)
            nc.tensor.matmul(count_ps[:, 0:TILES * EXPERTS], ones[:, :], flat, start=True, stop=True).then_inc(counted, 1)

        @block.gpsimd
        def _(pool):
            f = dict(allow_small_or_imprecise_dtypes=True)
            nc.gpsimd.iota(node[:, :], [[P, TILES]], base=0, channel_multiplier=1, **f)
            nc.gpsimd.iota(spare[:, :], [[P, TOP]], base=SLOT_ROWS, channel_multiplier=1, **f)
            nc.gpsimd.iota(order[:, :], [[-1, EXPERTS]], base=EXPERTS, channel_multiplier=0, **f)
            nc.gpsimd.iota(below[:, :], [[1, P]], base=0, channel_multiplier=-1, **f).then_inc(iotas_made, 1)
            weights.load(pool, 0)
            weights.split(pool, 0, 0)
            weights.load(pool, 1)
            pool.wait_ge(place_made, 1)

            def scatter(t, slot, n):
                if n >= SLOTS:
                    pool.wait_ge(scattered[slot], 2 * 16 * (n // SLOTS) if isinstance(t, int) else (t - slot) // SLOTS * (2 * 16))
                nc.gpsimd.tensor_copy(index[:, slot, :], scatter_to[:, bass.ds(t, 1), :].rearrange("p a c -> p (a c)")).then_inc(index_made, 1)
                pool.wait_ge(index_made, t + 1)
                pool.wait_ge(row_made, t + 1)
                pool.sem_inc(index_seen, 1)
                for c in range(TOP):
                    nc.gpsimd.indirect_dma_start(out=xs_dram, out_offset=bass.IndirectOffsetOnAxis(ap=index[:, slot, c:c + 1].bitcast(U32), axis=0),
                                                 in_=row[:, slot, :], in_offset=None).then_inc(scattered[slot], 16)
            pipeline(pool, TILES, SLOTS, [(scatter, 0)])
            for s in range(SLOTS):
                pool.wait_ge(scattered[s], 2 * 16 * len(range(s, TILES, SLOTS)))


def expert_phase(nc, xs_dram, ys_dram, weights, groups, keep):
    with ExitStack() as ctx:
        sb = lambda name, shape, dt=F32: ctx.enter_context(nc.sbuf_tensor("moe_" + name, shape, dt))
        sem = lambda name: ctx.enter_context(nc.semaphore("moe_" + name))
        psum = lambda name, shape: ctx.enter_context(nc.psum_tensor("moe_" + name, shape, F32))
        ident, b1, b2 = keep["ident"], keep["b1"], keep["b2"]
        w1, w2 = weights.w1, weights.w2
        x = sb("x", [P, SG, D])
        xT = sb("xT", [P, PARTS, KC, SROWS])
        hT_whole = sb("hT_whole", [P, HC, SROWS])
        hT = sb("hT", [P, PARTS, HC, SROWS])
        y = sb("y", [P, SG, D])
        HB = 4
        h_ps = psum("h_ps", [P, HB, 512])
        xT_ps = psum("xT_ps", [P, KC, SROWS])
        y_ps = psum("y_ps", [P, SG, D])
        h_split, xT_high = sem("h_split"), sem("xT_high")
        x_loaded, xT_done, xT_copied = sem("x_loaded"), sem("xT_done"), sem("xT_copied")
        h_done, h_made, y_done, y_made, y_stored = sem("h_done"), sem("h_made"), sem("y_done"), sem("y_made"), sem("y_stored")
        expert_done, weights_free = sem("expert_done"), sem("weights_free")
        weights_seen, ends_seen = sem("weights_seen"), sem("ends_seen")
        block = ctx.enter_context(nc.Block())

        def span(eng, e):
            count = eng.value_load(groups[0:1, bass.ds(e, 1)], min_val=1, max_val=MAX_SG)
            before = eng.value_load(groups[0:1, bass.ds(e + EXPERTS, 1)], min_val=0, max_val=MAX_SG - 1)
            return count, before

        def over_experts(eng, body):
            with eng.Fori(0, EXPERTS // 2) as k:
                body(2 * k, 0)
                body(2 * k + 1, 1)

        @block.gpsimd
        def _(pool):
            weights.split(pool, 1, 1)
            weights.load(pool, 2)

            def turn(e, slot):
                pool.wait_ge(expert_done, e - 1)
                pool.sem_inc(weights_free, 1)
                weights.split(pool, e, slot)
            with pool.Fori(1, EXPERTS // 2 - 1) as k:
                for slot in range(2):
                    turn(2 * k + slot, slot)
                    weights.load(pool, 2 * k + slot + 1)
            turn(EXPERTS - 2, 0)
            weights.load(pool, EXPERTS - 1)
            turn(EXPERTS - 1, 1)

        @block.sync
        def _(sp):
            rows = lambda dram, q: dram[bass.ds(q * SROWS, SROWS), :].rearrange("(i p) d -> p i d", p=P)
            last = EXPERTS - 1
            count, before = span(sp, last)
            sp.sem_inc(y_stored, 1)
            sp.dma_start(x[:, :, :], rows(xs_dram, 0)).then_inc(x_loaded, 16)
            with sp.Fori(0, before + count) as i:
                q = nc.s_assert_within(i, 0, MAX_SG - 1, skip_runtime_bounds_check_because="no routing fills more groups")
                sp.wait_ge(xT_done, q + 1)
                sp.dma_start(x[:, :, :], rows(xs_dram, q + 1)).then_inc(x_loaded, 16)
                sp.wait_ge(y_made, q + 1)
                sp.dma_start(rows(ys_dram, q), y[:, :, :]).then_inc(y_stored, 16)
            sp.wait_ge(y_stored, (before + count) * 16 + 1)
            sp.sem_inc(ends_seen, 1)
            sp.wait_ge(x_loaded, (before + count) * 16 + 16)
            sp.sem_inc(ends_seen, 1)

        @block.tensor
        def _(pe):
            def transpose(q):
                pe.wait_ge(x_loaded, q * 16 + 16)
                for c in range(KC):
                    for i in range(SG):
                        mm = nc.tensor.transpose(xT_ps[:, c, i * P:(i + 1) * P], x[:, i, c * P:(c + 1) * P], ident[:, :])
                mm.then_inc(xT_done, 1)

            def expert(e, slot):
                count, before = span(pe, e)
                pe.wait_ge(weights.split_made, e + 1)
                pe.sem_inc(weights_seen, 1)
                with pe.Fori(0, count) as j:
                    q = before + j
                    pe.wait_ge(xT_copied, q + 1)
                    for k in range(HC):
                        if k >= HB:
                            pe.wait_ge(h_made, q * HC + k - HB + 1)
                        for c in range(KC):
                            for a, b in PRODUCTS:
                                mm = nc.tensor.matmul(h_ps[:, k % HB, 0:SROWS], w1[:, slot, a, c, k * P:(k + 1) * P].bitcast(F32R), xT[:, b, c, :].bitcast(F32R),
                                                      start=(c == 0 and (a, b) == PRODUCTS[0]), stop=(c == KC - 1 and (a, b) == PRODUCTS[-1]))
                        mm.then_inc(h_done, 1)
                    transpose(q + 1)
                    for i in range(SG):
                        for k in range(HC):
                            if i == 0:
                                pe.wait_ge(h_split, q * HC + k + 1)
                            for a, b in PRODUCTS:
                                mm = nc.tensor.matmul(y_ps[:, i, :], hT[:, a, k, i * P:(i + 1) * P].bitcast(F32R), w2[:, slot, b, k, :].bitcast(F32R),
                                                      start=(k == 0 and (a, b) == PRODUCTS[0]), stop=(k == HC - 1 and (a, b) == PRODUCTS[-1]))
                    mm.then_inc(y_done, 1)
                pe.drain().then_inc(expert_done, 1)
            transpose(0)
            over_experts(pe, expert)

        @block.scalar
        def _(act):
            def copy_xT(q):
                act.wait_ge(xT_done, q + 1)
                nc.scalar.activation(xT[:, 0, :, :].bitcast(F32R), xT_ps[:, :, :], ACT.Copy).then_inc(xT_high, 1)

            def expert(e, slot):
                count, before = span(act, e)
                with act.Fori(0, count) as j:
                    q = before + j
                    for k in range(HC):
                        act.wait_ge(h_done, q * HC + k + 1)
                        nc.scalar.activation(hT_whole[:, k, :], h_ps[:, k % HB, 0:SROWS], ACT.Relu, bias=b1[:, bass.ds(e * HC + k, 1)]).then_inc(h_made, 1)
                    copy_xT(q + 1)
                    act.wait_ge(h_split, q * HC + HC)
            copy_xT(0)
            over_experts(act, expert)

        @block.vector
        def _(dve):
            def split_xT(q):
                dve.wait_ge(xT_high, q + 1)
                nc.vector.tensor_tensor(xT[:, 1, :, :].bitcast(F32R), xT_ps[:, :, :], xT[:, 0, :, :], ALU.subtract).then_inc(xT_copied, 1)

            def expert(e, slot):
                count, before = span(dve, e)
                with dve.Fori(0, count) as j:
                    q = before + j
                    for k in range(HC):
                        dve.wait_ge(h_made, q * HC + k + 1)
                        nc.vector.tensor_copy(hT[:, 0, k, :].bitcast(F32R), hT_whole[:, k, :])
                        dve.drain()
                        nc.vector.tensor_tensor(hT[:, 1, k, :].bitcast(F32R), hT_whole[:, k, :], hT[:, 0, k, :], ALU.subtract).then_inc(h_split, 1)
                    split_xT(q + 1)
                    dve.wait_ge(y_done, q + 1)
                    dve.wait_ge(y_stored, q * 16 + 1)
                    nc.vector.tensor_tensor(y[:, :, :], y_ps[:, :, :],
                                            b2[:, bass.ds(e, 1), :].broadcast_to([P, SG, D]), ALU.add).then_inc(y_made, 1)
            split_xT(0)
            over_experts(dve, expert)


def combine_phase(nc, X, ys_dram, prob, place, out):
    with ExitStack() as ctx:
        sb = lambda name, shape, dt=F32: ctx.enter_context(nc.sbuf_tensor("sum_" + name, shape, dt))
        sem = lambda name: ctx.enter_context(nc.semaphore("sum_" + name))
        index = sb("index", [P, SLOTS, TOP], I32)
        y = sb("y", [P, SLOTS, TOP, D])
        result = sb("result", [P, SLOTS, D])
        index_made, index_seen = sem("index_made"), sem("index_seen")
        y_loaded = [sem(f"y_loaded_{s}") for s in range(SLOTS)]
        result_made, stored = sem("result_made"), [sem(f"stored_{s}") for s in range(SLOTS)]
        block = ctx.enter_context(nc.Block())

        @block.gpsimd
        def _(pool):
            def gather(t, slot, n):
                if n >= SLOTS:
                    pool.wait_ge(result_made, t - SLOTS + 1)
                nc.gpsimd.tensor_copy(index[:, slot, :], place[:, bass.ds(t, 1), :].rearrange("p a c -> p (a c)")).then_inc(index_made, 1)
                pool.wait_ge(index_made, t + 1)
                pool.sem_inc(index_seen, 1)
                for c in range(TOP):
                    nc.gpsimd.indirect_dma_start(out=y[:, slot, c, :], out_offset=None, in_=ys_dram,
                                                 in_offset=bass.IndirectOffsetOnAxis(ap=index[:, slot, c:c + 1].bitcast(U32), axis=0)).then_inc(y_loaded[slot], 16)
            pipeline(pool, TILES, SLOTS, [(gather, 0)])

        @block.vector
        def _(dve):
            def add(t, slot, n):
                dve.wait_ge(y_loaded[slot], 2 * 16 * (n // SLOTS + 1) if isinstance(t, int) else (t - slot) // SLOTS * 32 + 32)
                if n >= SLOTS:
                    dve.wait_ge(stored[slot], 16 * (n // SLOTS) if isinstance(t, int) else (t - slot) // SLOTS * 16)
                nc.vector.scalar_tensor_tensor(result[:, slot, :], y[:, slot, 0, :], prob[:, bass.ds(t, 1), 0:1].rearrange("p a c -> p (a c)"), tile_of(X, t), ALU.mult, ALU.add)
                dve.drain()
                nc.vector.scalar_tensor_tensor(result[:, slot, :], y[:, slot, 1, :], prob[:, bass.ds(t, 1), 1:2].rearrange("p a c -> p (a c)"), result[:, slot, :], ALU.mult, ALU.add).then_inc(result_made, 1)
            pipeline(dve, TILES, SLOTS, [(add, 0)])

        @block.sync
        def _(sp):
            def store(t, slot, n):
                sp.wait_ge(result_made, t + 1)
                sp.dma_start(out[bass.ds(t * P, P), :], result[:, slot, :]).then_inc(stored[slot], 16)
            pipeline(sp, TILES, SLOTS, [(store, 0)])
            for s in range(SLOTS):
                sp.wait_ge(stored[s], 16 * len(range(s, TILES, SLOTS)))


def build_program(nc, ins, out):
    x1_dram = nc.dram_tensor("x1_rows", [NPAD, D], F32).ap()
    xs_dram = nc.dram_tensor("slot_inputs", [SLOT_ROWS + TOP * P, D], F32).ap()
    ys_dram = nc.dram_tensor("slot_outputs", [SLOT_ROWS, D], F32).ap()
    with ExitStack() as ctx:
        sb = lambda name, shape, dt=F32: ctx.enter_context(nc.sbuf_tensor(name, shape, dt))
        X, XN = sb("X", [P, TILES, D]), sb("XN", [P, TILES, D])
        prob = sb("prob", [P, TILES, TOP])
        place = sb("place", [P, TILES, TOP], I32)
        groups = sb("groups", [P, 2 * EXPERTS], I32)
        keep = dict(ident=sb("ident", [P, P]), eps=sb("eps", [P, 1]), O_b=sb("O_b", [P, D]))
        with ExitStack() as gnn:
            X1 = gnn.enter_context(nc.sbuf_tensor("X1", [P, TILES, D], F32))
            S = gnn.enter_context(nc.sbuf_tensor("S", [P, TILES + 1, D], F32))
            attention_phase(nc, X, XN, X1, S, ins["x"], ins["w_qkv"], x1_dram, xs_dram, ys_dram, ins, keep)
            for name, shape in GNN_KEPT.items():
                keep[name] = gnn.enter_context(nc.sbuf_tensor(name, shape, F32))
            graph_phase(nc, X, XN, X1, S, x1_dram, ins, keep)
        for name, shape in MOE_KEPT.items():
            keep[name] = sb(name, shape)
        with ExitStack() as moe:
            weights = Weights(nc, moe, ins["w1"], ins["w2"])
            route_phase(nc, X, XN, xs_dram, prob, place, groups, weights, ins, keep)
            expert_phase(nc, xs_dram, ys_dram, weights, groups, keep)
        combine_phase(nc, X, ys_dram, prob, place, out)


def kernel(x, src, dst, L0_gnn_Wq, L0_gnn_Wk, L0_gnn_Wv, L0_gnn_O_w, L0_gnn_O_b, L0_gnn_ln1_w, L0_gnn_ln1_b,
           L0_gnn_f1_w, L0_gnn_f1_b, L0_gnn_f2_w, L0_gnn_f2_b, L0_gnn_ln2_w, L0_gnn_ln2_b, L0_gnn_gru_w_ih,
           L0_gnn_gru_w_hh, L0_gnn_gru_b_ih, L0_gnn_gru_b_hh, L0_ffn_Wg, L0_ffn_bg, L0_ffn_W1, L0_ffn_b1,
           L0_ffn_W2, L0_ffn_b2):
    import numpy as np
    import concourse.bacc as bacc
    from concourse.bass_utils import run_bass_kernel_spmd as run

    def by_tile(a):
        return np.asarray(a).reshape(-1, P, a.shape[-1]).transpose(1, 0, 2)

    def by_chunk(a):
        return np.asarray(a).reshape(-1, P).T

    def repeated(a):
        return np.broadcast_to(np.asarray(a), (P,) + a.shape)

    def edges(a, fill):
        return np.concatenate([np.asarray(a), np.full(COLS * P - EDGES, fill, np.int32)]).reshape(COLS, P).T

    x_padded = np.concatenate([np.asarray(x), np.zeros((NPAD - NODES, D), np.float32)])
    qkv = np.concatenate([np.asarray(L0_gnn_Wq), np.asarray(L0_gnn_Wk), np.asarray(L0_gnn_Wv)], 1)
    arrays = dict(
        x=by_tile(x_padded), w_qkv=by_tile(qkv), ident=np.eye(P, dtype=np.float32),
        src=edges(src, 0), dst=edges(dst, NPAD - 1),
        O_w=by_tile(L0_gnn_O_w), O_b=repeated(L0_gnn_O_b), f1_w=by_tile(L0_gnn_f1_w), f1_b=by_chunk(L0_gnn_f1_b),
        f2_w=by_tile(L0_gnn_f2_w), f2_b=repeated(L0_gnn_f2_b),
        ln1_w=repeated(L0_gnn_ln1_w), ln1_b=repeated(L0_gnn_ln1_b), ln2_w=repeated(L0_gnn_ln2_w), ln2_b=repeated(L0_gnn_ln2_b),
        w_ih=by_tile(L0_gnn_gru_w_ih), w_hh=by_tile(L0_gnn_gru_w_hh), b_ih=by_chunk(L0_gnn_gru_b_ih), b_hh=by_chunk(L0_gnn_gru_b_hh),
        wg=by_tile(np.asarray(L0_ffn_Wg).T), bg=repeated(L0_ffn_bg),
        b1=by_chunk(np.asarray(L0_ffn_b1).reshape(-1)), b2=repeated(L0_ffn_b2),
        w1=np.asarray(L0_ffn_W1).transpose(0, 2, 1).reshape(EXPERTS, KC, P, HIDDEN).transpose(0, 2, 1, 3),
        w2=np.asarray(L0_ffn_W2).transpose(0, 2, 1).reshape(EXPERTS, HC, P, D).transpose(0, 2, 1, 3),
    )
    arrays = {f"in_{name}": np.ascontiguousarray(a) for name, a in arrays.items()}
    nc = bacc.Bacc("TRN2", target_bir_lowering=False, num_devices=1)
    ins = {name[3:]: nc.dram_tensor(name, a.shape, mybir.dt.from_np(a.dtype), kind="ExternalInput").ap() for name, a in arrays.items()}
    out = nc.dram_tensor("out", [NPAD, D], F32, kind="ExternalOutput").ap()
    build_program(nc, ins, out)
    result = run(nc, [arrays], core_ids=[0])
    return result.results[0]["out"][:NODES]
```

```python
import concourse.bass as bass
from concourse import mybir
from contextlib import ExitStack

F32 = mybir.dt.float32
I32 = mybir.dt.int32
U32 = mybir.dt.uint32
F32R = mybir.dt.float32r
ALU = mybir.AluOpType
ACT = mybir.ActivationFunctionType
AX = mybir.AxisListType

P = 128
NODES, EDGES, D = 3125, 50000, 256
HEADS = 8
DH = D // HEADS
TILES = -(-NODES // P)
NPAD = TILES * P
KC = D // P
SLOTS = 3
GE = 4
BATCHES = -(-EDGES // (SLOTS * GE * P))
GROUPS = BATCHES * SLOTS
COLS = GROUPS * GE
EPS = 1e-5
TILE_BITS = TILES.bit_length()
TILE_MAX = 1 << TILE_BITS
WINDOW = 2 * P
AT_MORE = SLOTS * TILE_BITS
BATCH_BITS = BATCHES.bit_length()
AHEAD = 2
X_LOADS = 5
PARTS = 2
PRODUCTS = ((0, 1), (1, 0), (0, 0))
X_TILES = TILES // X_LOADS


def bcast(ap, axis, shape):
    return ap.unsqueeze(axis).broadcast_to(shape)


def attention_phase(nc, X, XN, X1, S, x_in, w_in, x1_dram, y_dram, edge, ins, keep):
    with ExitStack() as ctx:
        sb = lambda name, shape, dt=F32: ctx.enter_context(nc.sbuf_tensor("attn_" + name, shape, dt))
        sem = lambda name: ctx.enter_context(nc.semaphore("attn_" + name))
        psum = lambda name, shape: ctx.enter_context(nc.psum_tensor("attn_" + name, shape, F32))
        ident = keep["ident"]
        wqkv = sb("wqkv", [P, KC, 3 * D])
        xn = sb("xn", [P, SLOTS, D])
        xnT = sb("xnT", [P, SLOTS, KC, P])
        qkv = sb("qkv", [P, SLOTS, 3 * D])
        prod = sb("prod", [P, HEADS * HEADS, DH])
        vprod = sb("vprod", [P, SLOTS, HEADS, D])
        score = sb("score", [P, SLOTS, HEADS, HEADS])
        prob = sb("prob", [P, SLOTS, HEADS, HEADS])
        greatest = sb("greatest", [P, HEADS])
        total = sb("total", [P, HEADS])
        stats = sb("stats", [P, TILES, 6])
        moments = sb("moments", [P, TILES, 2])
        std = sb("std", [P, TILES])
        rstd = sb("rstd", [P, TILES])
        xnT_ps = psum("xnT_ps", [P, 512])
        x1_ps = psum("x1_ps", [P, 512])
        qkv_ps = psum("qkv_ps", [P, SLOTS, 2, 512])

        x_loaded = [sem(f"x_loaded_{n}") for n in range(X_LOADS)]
        w_loaded, id_loaded = sem("w_loaded"), sem("id_loaded")
        var_ready, std_ready = sem("var_ready"), sem("std_ready")
        norm_ready, xnT_done, xnT_copied = sem("norm_ready"), sem("xnT_done"), sem("xnT_copied")
        qkv_done, qkv_copied = sem("qkv_done"), sem("qkv_copied")
        shifted, exped, prob_ready = sem("shifted"), sem("exped"), sem("prob_ready")
        vprod_ready, x1_ready, x1_stored = sem("vprod_ready"), sem("x1_ready"), sem("x1_stored")
        x1_summed = sem("x1_summed")
        bias_loaded, xn_kept = sem("bias_loaded"), sem("xn_kept")
        dst = sb("dst", [P, COLS], I32)
        ends = sb("ends", [P, 2, GROUPS])
        dst_loaded, ends_made = sem("dst_loaded"), sem("ends_made")
        s_cleared, padding_cleared = sem("s_cleared"), sem("padding_cleared")
        block = ctx.enter_context(nc.Block())

        def over_tiles(eng, step):
            for t in range(SLOTS):
                step(t, t, t)
            loops = TILES // SLOTS - 2
            with eng.Fori(0, loops) as k:
                for h in range(SLOTS):
                    step(k * SLOTS + SLOTS + h, h, SLOTS + h)
            for t in range((loops + 1) * SLOTS, TILES):
                step(t, t % SLOTS, t)

        @block.sync
        def _(sp):
            for n in range(X_LOADS):
                part = slice(n * X_TILES, (n + 1) * X_TILES)
                sp.dma_start(X[:, part, :], x_in[:, part, :]).then_inc(x_loaded[n], 16)
            sp.dma_start(ident[:, :], ins["ident"]).then_inc(id_loaded, 16)
            sp.dma_start(wqkv[:, :, :], w_in).then_inc(w_loaded, 16)
            sp.dma_start(keep["O_b"][:, :], ins["O_b"]).then_inc(bias_loaded, 16)
            sp.dma_start(dst[:, :], ins["dst"]).then_inc(dst_loaded, 16)

            def store(t, slot, n):
                sp.wait_ge(x1_ready, t + 1)
                sp.dma_start(x1_dram[bass.ds(t * P, P), :], X1[:, bass.ds(t, 1), :].rearrange("p a d -> p (a d)")).then_inc(x1_stored, 16)
            over_tiles(sp, store)
            sp.wait_ge(x1_stored, 16 * TILES)
            sp.wait_ge(padding_cleared, 16 * TOP)

        @block.vector
        def _(dve):
            nc.vector.memset(S[:, :, :], 0.0).then_inc(s_cleared, 1)
            nc.vector.memset(keep["eps"][:, :], EPS)
            for n in range(X_LOADS):
                dve.wait_ge(x_loaded[n], 16)
                for t in range(n * X_TILES, (n + 1) * X_TILES):
                    nc.vector.bn_stats(stats[:, t, :], X[:, t, :])
            dve.drain()
            for t in range(TILES):
                nc.vector.bn_aggr(moments[:, t, :], stats[:, t, :])
            dve.drain().then_inc(var_ready, 1)
            dve.wait_ge(dst_loaded, 16)
            nc.vector.memset(edge["dst_f"][:, COLS:], 0.0)
            nc.vector.tensor_copy(edge["dst_f"][:, 0:COLS], dst[:, :])
            dve.wait_ge(std_ready, 1)
            nc.vector.reciprocal(rstd[:, :], std[:, :])
            dve.drain()

            def norm(t, slot, n):
                if n >= SLOTS:
                    dve.wait_ge(xnT_done, t - SLOTS + 1)
                    dve.wait_ge(xn_kept, t - SLOTS + 1)
                nc.vector.tensor_scalar(xn[:, slot, :], X[:, bass.ds(t, 1), :].rearrange("p a d -> p (a d)"),
                                        moments[:, bass.ds(t, 1), 0:1].rearrange("p a d -> p (a d)"), rstd[:, bass.ds(t, 1)],
                                        ALU.subtract, ALU.mult).then_inc(norm_ready, 1)

            def step(t, slot, n):
                if n + 2 < TILES:
                    norm(t + 2, (slot + 2) % SLOTS, n + 2)
                dve.wait_ge(qkv_copied, t + 1)
                q = qkv[:, slot, 0:D].rearrange("p (h d) -> p h d", h=HEADS)
                k = qkv[:, slot, D:2 * D].rearrange("p (h d) -> p h d", h=HEADS)
                shape = [P, HEADS, HEADS, DH]
                nc.vector.tensor_tensor(prod[:, :, :].rearrange("p (h g) d -> p h g d", h=HEADS),
                                        bcast(q, 2, shape), bcast(k, 1, shape), ALU.mult)
                if n:
                    normalize(t - 1, (slot + 2) % SLOTS)
                else:
                    dve.drain()
                s = score[:, slot, :, :]
                nc.vector.tensor_reduce(s.rearrange("p h g -> p (h g)"), prod[:, :, :], AX.X, ALU.add)
                dve.drain()
                nc.vector.tensor_reduce(greatest[:, :], s, AX.X, ALU.max)
                dve.drain()
                nc.vector.tensor_tensor(s, s, bcast(greatest[:, :], 2, [P, HEADS, HEADS]), ALU.subtract).then_inc(shifted, 1)

            def normalize(t, slot):
                dve.wait_ge(exped, t + 1)
                nc.vector.tensor_reduce(total[:, :], prob[:, slot, :, :], AX.X, ALU.add)
                dve.drain()
                nc.vector.reciprocal(total[:, :], total[:, :])
                dve.drain()
                nc.vector.tensor_tensor(prob[:, slot, :, :], prob[:, slot, :, :], bcast(total[:, :], 2, [P, HEADS, HEADS]),
                                        ALU.mult).then_inc(prob_ready, 1)

            norm(0, 0, 0)
            norm(1, 1, 1)
            by_group = edge["dst_f"][:, 0:COLS].rearrange("p (g j) -> p g j", j=GE)
            nc.vector.tensor_reduce(ends[:, 0, :], by_group, AX.X, ALU.max)
            nc.vector.tensor_reduce(ends[:, 1, :], by_group, AX.X, ALU.min)
            dve.drain()
            nc.vector.tensor_scalar(ends[:, 1, :], ends[:, 1, :], -1.0, None, ALU.mult).then_inc(ends_made, 1)
            over_tiles(dve, step)
            normalize(TILES - 1, (TILES - 1) % SLOTS)

        @block.scalar
        def _(act):
            act.wait_ge(s_cleared, 1)
            for c in range(TOP):
                act.dma_start(y_dram[c * NPAD + NODES:(c + 1) * NPAD, :], S[0:NPAD - NODES, 0, :]).then_inc(padding_cleared, 16)

            def copy_xnT(t, slot, n):
                act.wait_ge(xnT_done, t + 1)
                nc.scalar.activation(xnT[:, slot, :, :].rearrange("p c n -> p (c n)"), xnT_ps[:, 0:D], ACT.Copy).then_inc(xnT_copied, 1)

            def copy_qkv(t, slot, n):
                act.wait_ge(qkv_done, t + 1)
                if n >= SLOTS:
                    act.wait_ge(vprod_ready, t - SLOTS + 1)
                half = 3 * D // 2
                nc.scalar.activation(qkv[:, slot, 0:D], qkv_ps[:, slot, 0, 0:D], ACT.Copy, scale=float(DH) ** -0.5)
                nc.scalar.activation(qkv[:, slot, D:half], qkv_ps[:, slot, 0, D:half], ACT.Copy)
                nc.scalar.activation(qkv[:, slot, half:], qkv_ps[:, slot, 1, 0:half], ACT.Copy)
                act.drain().then_inc(qkv_copied, 1)

            def keep_x1(t):
                act.wait_ge(x1_summed, t + 1)
                nc.scalar.activation(X1[:, bass.ds(t, 1), :].rearrange("p a d -> p (a d)"), x1_ps[:, 0:D], ACT.Copy).then_inc(x1_ready, 1)

            def step(t, slot, n):
                if n + 2 < TILES:
                    copy_xnT(t + 2, (slot + 2) % SLOTS, n + 2)
                if n + 1 < TILES:
                    copy_qkv(t + 1, (slot + 1) % SLOTS, n + 1)
                act.wait_ge(shifted, t + 1)
                nc.scalar.activation(prob[:, slot, :, :].rearrange("p h g -> p (h g)"),
                                     score[:, slot, :, :].rearrange("p h g -> p (h g)"), ACT.Exp).then_inc(exped, 1)
                if n > 1:
                    keep_x1(t - 2)

            act.wait_ge(var_ready, 1)
            nc.scalar.activation(std[:, :], moments[:, :, 1:2].rearrange("p t a -> p (t a)"), ACT.Sqrt, bias=keep["eps"][:, 0:1]).then_inc(std_ready, 1)
            copy_xnT(0, 0, 0)
            copy_xnT(1, 1, 1)
            copy_qkv(0, 0, 0)
            over_tiles(act, step)
            keep_x1(TILES - 2)
            keep_x1(TILES - 1)

        @block.tensor
        def _(pe):
            pe.wait_ge(id_loaded, 16)
            pe.wait_ge(w_loaded, 16)

            def transpose_xn(t, slot, n):
                pe.wait_ge(norm_ready, t + 1)
                if n:
                    pe.wait_ge(xnT_copied, t)
                for c in range(KC):
                    mm = nc.tensor.transpose(xnT_ps[:, c * P:(c + 1) * P], xn[:, slot, c * P:(c + 1) * P], ident[:, :])
                mm.then_inc(xnT_done, 1)

            def project(t, slot, n):
                pe.wait_ge(xnT_copied, t + 1)
                if n >= SLOTS:
                    pe.wait_ge(qkv_copied, t - SLOTS + 1)
                for half in range(2):
                    for c in range(KC):
                        mm = nc.tensor.matmul(qkv_ps[:, slot, half, 0:3 * D // 2], xnT[:, slot, c, :],
                                              wqkv[:, c, half * 3 * D // 2:(half + 1) * 3 * D // 2],
                                              start=(c == 0), stop=(c == KC - 1))
                mm.then_inc(qkv_done, 1)

            def sum_values(t, slot, n):
                pe.wait_ge(vprod_ready, t + 1)
                if n:
                    pe.wait_ge(x1_ready, t)
                for g in range(HEADS):
                    mm = nc.tensor.matmul(x1_ps[:, 0:D], ident[:, :], vprod[:, slot, g, :], start=(g == 0), stop=(g == HEADS - 1))
                mm.then_inc(x1_summed, 1)

            def step(t, slot, n):
                if n + 1 < TILES:
                    project(t + 1, (slot + 1) % SLOTS, n + 1)
                if n + 2 < TILES:
                    transpose_xn(t + 2, (slot + 2) % SLOTS, n + 2)
                if n > 1:
                    sum_values(t - 2, (slot + 1) % SLOTS, n - 2)

            transpose_xn(0, 0, 0)
            transpose_xn(1, 1, 1)
            project(0, 0, 0)
            over_tiles(pe, step)
            for t in (TILES - 2, TILES - 1):
                sum_values(t, t % SLOTS, t)

        @block.gpsimd
        def _(pool):
            def keep_xn(t, slot, n):
                pool.wait_ge(norm_ready, t + 1)
                nc.gpsimd.tensor_tensor(tile_of(XN, t), xn[:, slot, :], keep["O_b"][:, :], ALU.add).then_inc(xn_kept, 1)

            nc.gpsimd.iota(edge["iota_w"][:, :], [[1, WINDOW]], base=0, channel_multiplier=0, allow_small_or_imprecise_dtypes=True)
            nc.gpsimd.iota(edge["iota_more"][:, :], [[WINDOW, 1 + TILES // 2]], base=0, channel_multiplier=0, allow_small_or_imprecise_dtypes=True)
            pool.wait_ge(bias_loaded, 16)
            keep_xn(0, 0, 0)
            keep_xn(1, 1, 1)
            pool.wait_ge(ends_made, 1)
            nc.gpsimd.partition_all_reduce(edge["ends"][:, :, :].rearrange("p a g -> p (a g)"), ends[:, :, :].rearrange("p a g -> p (a g)"),
                                           P, bass.bass_isa.ReduceOp.max)

            def step(t, slot, n):
                if n + 2 < TILES:
                    keep_xn(t + 2, (slot + 2) % SLOTS, n + 2)
                pool.wait_ge(prob_ready, t + 1)
                if n >= SLOTS:
                    pool.wait_ge(x1_summed, t - SLOTS + 1)
                shape = [P, HEADS, HEADS, DH]
                v = qkv[:, slot, 2 * D:3 * D].rearrange("p (g d) -> p g d", g=HEADS)
                nc.gpsimd.tensor_tensor(vprod[:, slot, :, :].rearrange("p g (h d) -> p g h d", h=HEADS),
                                        bcast(prob[:, slot, :, :].rearrange("p h g -> p g h"), 3, shape),
                                        bcast(v, 2, shape), ALU.mult).then_inc(vprod_ready, 1)
            over_tiles(pool, step)


GNN_KEPT = dict(O_w=[P, KC, D], f1_w=[P, KC, 2 * D], f2_w=[P, 2 * KC, D], w_ih=[P, KC, 3 * D], w_hh=[P, KC, 3 * D],
                f1_b=[P, 2 * KC], b_ih=[P, 3 * KC], b_hh=[P, 3 * KC],
                ln1_w=[P, D], ln1_b=[P, D], ln2_w=[P, D], ln2_b=[P, D], f2_b=[P, D])


def load_kept(eng, names, ins, keep, loaded):
    for name, shape in names.items():
        whole = tuple(slice(None) for _ in shape)
        eng.dma_start(keep[name][whole], ins[name]).then_inc(loaded, 16)
    eng.wait_ge(loaded, 16 * len(names))


def pipeline(eng, count, slots, stages, warmup=0):
    span = max(lag for _, lag in stages)
    start = -(-(span + warmup + slots) // slots) * slots
    loops = (count - 1 - warmup - start) // slots

    def step(i, n):
        for work, lag in stages:
            if 0 <= n - lag < count:
                work(i - lag, (n - lag) % slots, n - lag)

    for i in range(start):
        step(i, i)
    with eng.Fori(0, loops) as k:
        for h in range(slots):
            step(k * slots + start + h, start + h)
    for i in range(start + loops * slots, count + span):
        step(i, i)


def tile_of(array, t):
    return array[:, bass.ds(t, 1), :].rearrange("p a d -> p (a d)")


def graph_phase(nc, X, XN, X1, S, x1_dram, edge, ins, keep):
    FC = 2 * D // P
    with ExitStack() as ctx:
        sb = lambda name, shape, dt=F32: ctx.enter_context(nc.sbuf_tensor("graph_" + name, shape, dt))
        sem = lambda name: ctx.enter_context(nc.semaphore("graph_" + name))
        psum = lambda name, shape: ctx.enter_context(nc.psum_tensor("graph_" + name, shape, F32))
        ident = keep["ident"]
        src = sb("src", [P, COLS], I32)
        dst_more = sb("dst_more", [P, GE])
        iota_w, iota_more = edge["iota_w"], edge["iota_more"]
        dst_f, ends_all = edge["dst_f"], edge["ends"]
        ends_i = sb("ends_i", [P, 2, GROUPS], I32)
        least = sb("least", [P, GROUPS])
        extra_f = sb("extra_f", [P, GROUPS])
        extra_i = sb("extra_i", [P, GROUPS], I32)
        scan = sb("scan", [P, 2, GROUPS])
        table = sb("table", [P, GROUPS + 1], I32)
        words = sb("words", [P, BATCHES], I32)
        word = sb("word", [P, BATCHES])
        has_more = sb("has_more", [P, BATCHES])
        batch_least = sb("batch_least", [P, BATCHES])
        upto = sb("upto", [P, 1 + TILES])
        turns = sb("turns", [P, TILES], I32)
        number = sb("number", [P, TILES])
        last = sb("last", [P, TILES])
        index = sb("index", [P, SLOTS, GE], I32)
        rows = sb("rows", [P, SLOTS, GE, D])
        onehot = sb("onehot", [P, SLOTS, GE, WINDOW])
        part_ps = psum("part_ps", [P, SLOTS, 512])
        attn = sb("attn", [P, SLOTS, D])
        attnT = sb("attnT", [P, KC, P])
        h0 = sb("h0", [P, SLOTS, D])
        h1 = sb("h1", [P, D])
        h1T = sb("h1T", [P, SLOTS, KC, P])
        fT = sb("fT", [P, SLOTS, FC, P])
        scratch = fT[:, :, :, :].rearrange("p s k n -> p (s k n)")
        reaches = scratch[:, 0:TILES * BATCHES].rearrange("p (t b) -> p t b", b=BATCHES)
        r = sb("r", [P, SLOTS, D])
        h2 = sb("h2", [P, D])
        h2T = sb("h2T", [P, SLOTS, KC, P])
        rz = sb("rz", [P, SLOTS, 2 * KC, P])
        rn = sb("rn", [P, KC, P])
        new = rn
        diff = sb("diff", [P, SLOTS, KC, P])
        yT = diff
        stats = sb("stats", [P, 2, SLOTS, 6])
        moments = sb("moments", [P, 2, SLOTS, 2])
        std = sb("std", [P, 2, SLOTS])
        rstd = sb("rstd", [P, 2, SLOTS])
        w_rz = sb("w_rz", [P, KC, 2 * D])
        b_rz = sb("b_rz", [P, 2 * KC])
        ln1_b_f2_b = sb("ln1_b_f2_b", [P, D])
        turned_ps = psum("turned_ps", [P, 512])
        out_ps = psum("out_ps", [P, 2, D])
        f_ps = psum("f_ps", [P, FC, P])
        rz_ps = psum("rz_ps", [P, 2 * KC, P])
        n_ps = psum("n_ps", [P, 2, KC, P])

        src_loaded, kept_loaded = sem("src_loaded"), sem("kept_loaded")
        table_made, sums_made = sem("table_made"), sem("sums_made")
        index_made, index_seen = sem("index_made"), sem("index_seen")
        rows_loaded = [sem(f"rows_loaded_{s}") for s in range(SLOTS)]
        first_onehot, first_summed = sem("first_onehot"), sem("first_summed")
        more_onehot, more_summed = sem("more_onehot"), sem("more_summed")
        group_summed = sem("group_summed")
        attn_made, attnT_done, attnT_copied = sem("attn_made"), sem("attnT_done"), sem("attnT_copied")
        attn_out_done, var1_made, std1_made = sem("attn_out_done"), sem("var1_made"), sem("std1_made")
        h1_made, h1T_done, h1T_copied = sem("h1_made"), sem("h1T_done"), sem("h1T_copied")
        f_done, fT_made, f_out_done = sem("f_done"), sem("fT_made"), sem("f_out_done")
        var2_made, std2_made = sem("var2_made"), sem("std2_made")
        h2_made, h2T_done, h2T_copied = sem("h2_made"), sem("h2T_done"), sem("h2T_copied")
        rz_done, n_done, rz_made, rn_made, n_made = sem("rz_done"), sem("n_done"), sem("rz_made"), sem("rn_made"), sem("n_made")
        yT_made, y_done, y_added = sem("yT_made"), sem("y_done"), sem("y_added")
        block = ctx.enter_context(nc.Block())

        def within(value, greatest, why):
            return nc.s_assert_within(value, 0, greatest, skip_runtime_bounds_check_because=why)

        def unpack(eng, g):
            packed = eng.value_load(table[0:1, bass.ds(g, 1)], min_val=0, max_val=(1 << 31) - 1)
            tile = eng.snap(within(packed & (TILE_MAX - 1), TILES - 1, "a tile of nodes"))
            more = eng.snap((packed >> TILE_BITS) & (TILE_MAX - 1), min_val=0, max_val=TILES // 2)
            before = eng.snap(packed >> (2 * TILE_BITS), min_val=0, max_val=GROUPS * TILES)
            return tile, more, before

        def tile_in(eng, packed, at):
            return eng.snap(within((packed >> at) & (TILE_MAX - 1), TILES - 1, "a tile of nodes"))

        def over_steps(eng, plain, general, parts):
            def batch(b, after):
                packed = eng.value_load(words[0:1, bass.ds(b, 1)], min_val=0, max_val=(2 << AT_MORE) - 1)
                with eng.If(packed < (1 << AT_MORE)):
                    for slot in range(SLOTS):
                        plain(b * SLOTS + slot, slot, b, packed)
                        after(slot)
                with eng.Else():
                    for slot in range(SLOTS):
                        general(b * SLOTS + slot, slot, b)
                        after(slot)

            def step(i, slot, n):
                def part(k):
                    for work, lag in parts[k]:
                        if 0 <= n - lag < TILES:
                            work(i - lag, (n - lag) % SLOTS, n - lag)
                if n >= TILES:
                    for k in range(SLOTS):
                        part(k)
                    return
                turn = eng.value_load(turns[0:1, bass.ds(i, 1)], min_val=0, max_val=(1 << 3 * BATCH_BITS) - 1)
                mask = (1 << BATCH_BITS) - 1
                first = eng.snap(turn & mask, min_val=0, max_val=BATCHES)
                count = eng.snap((turn >> BATCH_BITS) & mask, min_val=0, max_val=BATCHES)
                last = eng.snap(within(turn >> (2 * BATCH_BITS), BATCHES - 1, "a batch"))
                with eng.If(count > 1):
                    with eng.Fori(0, count - 1) as k:
                        batch(eng.snap(within(first + k, BATCHES - 1, "a batch of the step")), lambda slot: None)
                with eng.Else():
                    eng.nop()
                with eng.If(count > 0):
                    batch(last, part)
                with eng.Else():
                    for k in range(SLOTS):
                        part(k)
            span = max(lag for stages in parts for _, lag in stages)
            pipeline(eng, TILES + span, SLOTS, [(step, 0)], span)

        @block.sync
        def _(sp):
            sp.dma_start(src[:, :], ins["src"]).then_inc(src_loaded, 16)
            load_kept(sp, GNN_KEPT, ins, keep, kept_loaded)

        @block.gpsimd
        def _(pool):
            pool.wait_ge(src_loaded, 16)

            def gather(g, slot, n):
                if n >= SLOTS:
                    pool.wait_ge(group_summed, g - SLOTS + 1)
                nc.gpsimd.tensor_copy(index[:, slot, :], src[:, bass.ds(g * GE, GE)]).then_inc(index_made, 1)
                pool.wait_ge(index_made, g + 1)
                pool.sem_inc(index_seen, 1)
                for j in range(GE):
                    nc.gpsimd.indirect_dma_start(out=rows[:, slot, j, :], out_offset=None, in_=x1_dram,
                                                 in_offset=bass.IndirectOffsetOnAxis(ap=index[:, slot, j:j + 1].bitcast(U32), axis=0)).then_inc(rows_loaded[slot], 16)
            pipeline(pool, GROUPS, SLOTS, [(gather, 0)])

        @block.vector
        def _(dve):
            by_group = dst_f[:, 0:COLS].rearrange("p (g j) -> p g j", j=GE)
            nc.vector.tensor_scalar(ends_all[:, 1, :], ends_all[:, 1, :], -1.0, None, ALU.mult)
            dve.drain()
            nc.vector.tensor_copy(ends_i[:, :, :], ends_all[:, :, :])
            dve.drain()
            nc.vector.tensor_scalar(ends_i[:, :, :], ends_i[:, :, :], P.bit_length() - 1, None, ALU.arith_shift_right)
            nc.vector.memset(table[:, :], 0)
            nc.vector.memset(upto[:, 0:1], 0.0)
            dve.drain()
            nc.vector.tensor_tensor(extra_i[:, :], ends_i[:, 0, :], ends_i[:, 1, :], ALU.subtract)
            nc.vector.tensor_copy(least[:, :], ends_i[:, 1, :])
            dve.drain()
            nc.vector.tensor_scalar(extra_i[:, :], extra_i[:, :], 1, None, ALU.arith_shift_right)
            dve.drain()
            nc.vector.tensor_copy(extra_f[:, :], extra_i[:, :])
            nc.vector.tensor_copy(scan[:, 0, :], extra_i[:, :])
            nc.vector.tensor_reduce(batch_least[:, :], least[:, :].rearrange("p (b s) -> p b s", s=SLOTS), AX.X, ALU.min)
            dve.drain()
            shape = [P, TILES, BATCHES]
            nc.vector.tensor_tensor(reaches[:, :, :], bcast(iota_w[:, 0:TILES], 2, shape), bcast(batch_least[:, :], 1, shape), ALU.is_ge)
            dve.drain()
            nc.vector.tensor_tensor(reaches[:, :, :], reaches[:, :, :], bcast(iota_w[:, 1:1 + BATCHES], 1, shape), ALU.mult)
            dve.drain()
            nc.vector.tensor_reduce(upto[:, 1:], reaches[:, :, :], AX.X, ALU.max)
            dve.drain()
            nc.vector.tensor_tensor(number[:, :], upto[:, 1:], upto[:, 0:TILES], ALU.subtract)
            nc.vector.tensor_scalar(last[:, :], upto[:, 1:], -1.0, 0.0, ALU.add, ALU.max)
            dve.drain()
            nc.vector.scalar_tensor_tensor(number[:, :], last[:, :], float(1 << BATCH_BITS), number[:, :], ALU.mult, ALU.add)
            dve.drain()
            nc.vector.scalar_tensor_tensor(turns[:, :], number[:, :], float(1 << BATCH_BITS), upto[:, 0:TILES], ALU.mult, ALU.add)
            by_batch = least[:, :].rearrange("p (b s) -> p b s", s=SLOTS)
            nc.vector.tensor_reduce(has_more[:, :], extra_f[:, :].rearrange("p (b s) -> p b s", s=SLOTS), AX.X, ALU.max)
            dve.drain()
            nc.vector.tensor_scalar(word[:, :], has_more[:, :], 0.0, None, ALU.is_gt)
            nc.vector.scalar_tensor_tensor(by_group, bcast(least[:, :], 2, [P, GROUPS, GE]), -float(P), by_group, ALU.mult, ALU.add)
            dve.drain()
            for slot in reversed(range(SLOTS)):
                nc.vector.scalar_tensor_tensor(word[:, :], word[:, :], float(TILE_MAX), by_batch[:, :, slot], ALU.mult, ALU.add)
                dve.drain()
            nc.vector.tensor_copy(words[:, :], word[:, :])
            now, reach = 0, 1
            while reach < GROUPS:
                nc.vector.tensor_copy(scan[:, 1 - now, 0:reach], scan[:, now, 0:reach])
                nc.vector.tensor_tensor(scan[:, 1 - now, reach:], scan[:, now, reach:], scan[:, now, 0:GROUPS - reach], ALU.add)
                dve.drain()
                now, reach = 1 - now, 2 * reach
            nc.vector.tensor_tensor(scan[:, now, :], scan[:, now, :], extra_f[:, :], ALU.subtract)
            dve.drain()
            nc.vector.scalar_tensor_tensor(extra_f[:, :], scan[:, now, :], float(TILE_MAX), extra_f[:, :], ALU.mult, ALU.add)
            dve.drain()
            nc.vector.scalar_tensor_tensor(table[:, 0:GROUPS], extra_f[:, :], float(TILE_MAX), ends_i[:, 1, :], ALU.mult, ALU.add)
            dve.drain().then_inc(table_made, 1)
            dve.wait_ge(table_made, 1)

            def make_onehot(slot, nodes, made):
                nc.vector.tensor_tensor(onehot[:, slot, :, :], bcast(iota_w[:, :], 1, [P, GE, WINDOW]),
                                        bcast(nodes, 2, [P, GE, WINDOW]), ALU.is_equal).then_inc(made, 1)

            def make_first(g, slot):
                make_onehot(slot, dst_f[:, bass.ds(g * GE, GE)], first_onehot)

            def add_part(tile, slot):
                s = S[:, bass.ds(tile, WINDOW // P), :]
                return nc.vector.tensor_tensor(s, s, part_ps[:, slot, :].rearrange("p (w d) -> p w d", d=D), ALU.add)

            def general(g, slot, b):
                tile, more, before = unpack(dve, g)
                make_first(g + AHEAD, (slot + AHEAD) % SLOTS)
                dve.wait_ge(first_summed, g + 1)
                add_part(tile, slot)
                with dve.If(more > 0):
                    with dve.Fori(0, more) as j:
                        to = within(tile + 2 * j + 2, TILES - 1, "a tile of nodes up to that of the group's greatest dst")
                        nc.vector.tensor_scalar(dst_more[:, :], dst_f[:, bass.ds(g * GE, GE)], iota_more[:, bass.ds(within(j + 1, TILES // 2, "a window"), 1)], None, ALU.subtract)
                        dve.drain()
                        make_onehot(slot, dst_more[:, :], more_onehot)
                        dve.wait_ge(more_summed, before + j + 1)
                        add_part(to, slot)
                with dve.Else():
                    dve.nop()
                dve.drain().then_inc(group_summed, 1)

            def plain(g, slot, b, packed):
                make_first(g + AHEAD, (slot + AHEAD) % SLOTS)
                dve.wait_ge(first_summed, g + 1)
                add_part(tile_in(dve, packed, TILE_BITS * slot), slot)
                dve.drain().then_inc(group_summed, 1)

            def gate(t, slot, n):
                if n >= SLOTS:
                    dve.wait_ge(attnT_done, t - SLOTS + 1)
                nc.vector.tensor_tensor(attn[:, slot, :], tile_of(X1, t), tile_of(S, t), ALU.mult).then_inc(attn_made, 1)

            def variance(which, values, slot, made):
                dve.drain()
                nc.vector.bn_stats(stats[:, which, slot, :], values[:, slot, :])
                dve.drain()
                nc.vector.bn_aggr(moments[:, which, slot, :], stats[:, which, slot, :]).then_inc(made, 1)

            def center(which, values, w, slot):
                nc.vector.reciprocal(rstd[:, which, slot:slot + 1], std[:, which, slot:slot + 1])
                nc.vector.scalar_tensor_tensor(values[:, slot, :], values[:, slot, :], moments[:, which, slot, 0:1], w[:, :], ALU.subtract, ALU.mult)
                dve.drain()

            def add_attn(t, slot, n):
                dve.wait_ge(attn_out_done, t + 1)
                nc.vector.tensor_tensor(h0[:, slot, :], out_ps[:, 0, :], tile_of(XN, t), ALU.add)
                variance(0, h0, slot, var1_made)

            def norm1(t, slot, n):
                dve.wait_ge(std1_made, t + 1)
                if n:
                    dve.wait_ge(h1T_done, t)
                center(0, h0, keep["ln1_w"], slot)
                nc.vector.scalar_tensor_tensor(h1[:, :], h0[:, slot, :], rstd[:, 0, slot:slot + 1], keep["ln1_b"][:, :], ALU.mult, ALU.add).then_inc(h1_made, 1)
                nc.vector.scalar_tensor_tensor(tile_of(XN, t), h0[:, slot, :], rstd[:, 0, slot:slot + 1], ln1_b_f2_b[:, :], ALU.mult, ALU.add)

            def add_ffn(t, slot, n):
                dve.wait_ge(f_out_done, t + 1)
                nc.vector.tensor_tensor(r[:, slot, :], out_ps[:, 1, :], tile_of(XN, t), ALU.add)
                variance(1, r, slot, var2_made)

            def norm2(t, slot, n):
                dve.wait_ge(std2_made, t + 1)
                if n:
                    dve.wait_ge(h2T_done, t)
                center(1, r, keep["ln2_w"], slot)
                nc.vector.scalar_tensor_tensor(h2[:, :], r[:, slot, :], rstd[:, 1, slot:slot + 1], keep["ln2_b"][:, :], ALU.mult, ALU.add).then_inc(h2_made, 1)

            def reset(t, slot, n):
                dve.wait_ge(n_done, t + 1)
                dve.wait_ge(rz_made, t + 1)
                if n:
                    dve.wait_ge(yT_made, t)
                for k in range(KC):
                    nc.vector.scalar_tensor_tensor(rn[:, k, :], n_ps[:, 1, k, :], keep["b_hh"][:, 2 * KC + k:2 * KC + k + 1],
                                                   rz[:, slot, k, :], ALU.add, ALU.mult)
                dve.drain()
                nc.vector.tensor_tensor(rn[:, :, :], rn[:, :, :], n_ps[:, 0, :, :], ALU.add).then_inc(rn_made, 1)

            def blend(t, slot, n):
                dve.wait_ge(n_made, t + 1)
                if n >= SLOTS:
                    dve.wait_ge(y_done, t - SLOTS + 1)
                nc.vector.tensor_tensor(diff[:, slot, :, :], h2T[:, slot, :, :], new[:, :, :], ALU.subtract)
                dve.drain()
                nc.vector.tensor_tensor(diff[:, slot, :, :], diff[:, slot, :, :], rz[:, slot, KC:2 * KC, :], ALU.mult)
                dve.drain()
                nc.vector.tensor_tensor(yT[:, slot, :, :], diff[:, slot, :, :], new[:, :, :], ALU.add).then_inc(yT_made, 1)

            def add_y(t, slot, n):
                dve.wait_ge(y_done, t + 1)
                nc.vector.tensor_tensor(tile_of(X, t), tile_of(X, t), turned_ps[:, 0:D], ALU.add).then_inc(y_added, 1)

            for g in range(AHEAD):
                make_first(g, g)
            dve.wait_ge(kept_loaded, 16 * len(GNN_KEPT))
            nc.vector.tensor_tensor(w_rz[:, :, :], keep["w_ih"][:, :, 0:2 * D], keep["w_hh"][:, :, 0:2 * D], ALU.add)
            nc.vector.tensor_tensor(b_rz[:, :], keep["b_ih"][:, 0:2 * KC], keep["b_hh"][:, 0:2 * KC], ALU.add)
            nc.vector.tensor_tensor(ln1_b_f2_b[:, :], keep["ln1_b"][:, :], keep["f2_b"][:, :], ALU.add)
            dve.drain().then_inc(sums_made, 1)
            over_steps(dve, plain, general, [[(norm1, 2), (reset, 7)], [(add_y, 8), (add_attn, 1), (norm2, 5), (blend, 7)], [(gate, 0), (add_ffn, 4)]])

        @block.scalar
        def _(act):
            def copy_attnT(t, slot, n):
                act.wait_ge(attnT_done, t + 1)
                if n:
                    act.wait_ge(attn_out_done, t)
                nc.scalar.activation(attnT[:, :, :].rearrange("p c n -> p (c n)"), turned_ps[:, 0:D], ACT.Copy).then_inc(attnT_copied, 1)

            def root1(t, slot, n):
                act.wait_ge(var1_made, t + 1)
                nc.scalar.activation(std[:, 0, slot:slot + 1], moments[:, 0, slot, 1:2], ACT.Sqrt, bias=keep["eps"][:, 0:1]).then_inc(std1_made, 1)

            def copy_h1T(t, slot, n):
                act.wait_ge(h1T_done, t + 1)
                if n >= SLOTS:
                    act.wait_ge(f_done, t - SLOTS + 1)
                nc.scalar.activation(h1T[:, slot, :, :].rearrange("p c n -> p (c n)"), turned_ps[:, 0:D], ACT.Copy).then_inc(h1T_copied, 1)

            def relu(t, slot, n):
                act.wait_ge(f_done, t + 1)
                if n >= SLOTS:
                    act.wait_ge(f_out_done, t - SLOTS + 1)
                for k in range(FC):
                    nc.scalar.activation(fT[:, slot, k, :], f_ps[:, k, :], ACT.Relu, bias=keep["f1_b"][:, k:k + 1])
                act.drain().then_inc(fT_made, 1)

            def root2(t, slot, n):
                act.wait_ge(var2_made, t + 1)
                nc.scalar.activation(std[:, 1, slot:slot + 1], moments[:, 1, slot, 1:2], ACT.Sqrt, bias=keep["eps"][:, 0:1]).then_inc(std2_made, 1)

            def copy_h2T(t, slot, n):
                act.wait_ge(h2T_done, t + 1)
                if n >= SLOTS:
                    act.wait_ge(yT_made, t - SLOTS + 1)
                nc.scalar.activation(h2T[:, slot, :, :].rearrange("p c n -> p (c n)"), turned_ps[:, 0:D], ACT.Copy).then_inc(h2T_copied, 1)

            def sigmoid(t, slot, n):
                act.wait_ge(rz_done, t + 1)
                if n >= SLOTS:
                    act.wait_ge(yT_made, t - SLOTS + 1)
                for k in range(2 * KC):
                    nc.scalar.activation(rz[:, slot, k, :], rz_ps[:, k, :], ACT.Sigmoid, bias=b_rz[:, k:k + 1])
                act.drain().then_inc(rz_made, 1)

            def tanh(t, slot, n):
                act.wait_ge(rn_made, t + 1)
                for k in range(KC):
                    nc.scalar.activation(new[:, k, :], rn[:, k, :], ACT.Tanh, bias=keep["b_ih"][:, 2 * KC + k:2 * KC + k + 1])
                act.drain().then_inc(n_made, 1)

            act.wait_ge(sums_made, 1)
            pipeline(act, TILES, SLOTS, [(copy_attnT, 1), (relu, 3), (copy_h1T, 2), (tanh, 7), (copy_h2T, 5), (root1, 1), (root2, 4), (sigmoid, 6)])

        @block.tensor
        def _(pe):
            def sum_window(slot, done):
                for w in range(WINDOW // P):
                    for e in range(GE):
                        mm = nc.tensor.matmul(part_ps[:, slot, w * D:(w + 1) * D], onehot[:, slot, e, w * P:(w + 1) * P],
                                              rows[:, slot, e, :], start=(e == 0), stop=(e == GE - 1))
                mm.then_inc(done, 1)

            def first_window(g, slot, b):
                pe.wait_ge(rows_loaded[slot], b * (GE * 16) + GE * 16)
                pe.wait_ge(first_onehot, g + 1)
                sum_window(slot, first_summed)

            def general(g, slot, b):
                _, more, before = unpack(pe, g)
                first_window(g, slot, b)
                with pe.If(more > 0):
                    with pe.Fori(0, more) as j:
                        pe.wait_ge(more_onehot, before + j + 1)
                        sum_window(slot, more_summed)
                with pe.Else():
                    pe.nop()

            def plain(g, slot, b, packed):
                first_window(g, slot, b)

            TURNED = ((attnT_copied, 1), (y_added, 8), (h1T_copied, 2), (h2T_copied, 5))

            def turned_free(t, n, user):
                lag = TURNED[user][1]
                for back in range(1, len(TURNED) + 1):
                    emptied, other = TURNED[(user - back) % len(TURNED)]
                    behind = other - lag + (1 if back > user else 0)
                    if 0 <= n - behind < TILES:
                        pe.wait_ge(emptied, t - behind + 1)
                        return

            def transpose(source, made, done, user):
                def stage(t, slot, n):
                    whole = source[:, slot, :] if len(source.shape) == 3 else source
                    pe.wait_ge(made, t + 1)
                    turned_free(t, n, user)
                    for c in range(KC):
                        mm = nc.tensor.transpose(turned_ps[:, c * P:(c + 1) * P], whole[:, c * P:(c + 1) * P], ident[:, :])
                    mm.then_inc(done, 1)
                return stage
            transpose_attn = transpose(attn, attn_made, attnT_done, 0)
            transpose_h1 = transpose(h1, h1_made, h1T_done, 2)
            transpose_h2 = transpose(h2, h2_made, h2T_done, 3)
            by_row = yT[:, :, :, :].rearrange("p s c n -> p s (c n)")
            transpose_y = transpose(by_row, yT_made, y_done, 1)

            def project(t, slot, n):
                if n == 0:
                    pe.wait_ge(sums_made, 1)
                pe.wait_ge(attnT_copied, t + 1)
                if n:
                    pe.wait_ge(var1_made, t)
                if n >= 4:
                    pe.wait_ge(var2_made, t - 3)
                for c in range(KC):
                    mm = nc.tensor.matmul(out_ps[:, 0, :], attnT[:, c, :], keep["O_w"][:, c, :], start=(c == 0), stop=(c == KC - 1))
                mm.then_inc(attn_out_done, 1)

            def by_feature(ps, weights, chunks, first, hT, slot):
                for k in range(chunks):
                    for c in range(KC):
                        mm = nc.tensor.matmul(ps[:, k, :], weights[:, c, first + k * P:first + (k + 1) * P], hT[:, slot, c, :],
                                              start=(c == 0), stop=(c == KC - 1))
                return mm

            def up(t, slot, n):
                pe.wait_ge(h1T_copied, t + 1)
                if n:
                    pe.wait_ge(fT_made, t)
                by_feature(f_ps, keep["f1_w"], FC, 0, h1T, slot).then_inc(f_done, 1)

            def down(t, slot, n):
                pe.wait_ge(fT_made, t + 1)
                if n:
                    pe.wait_ge(var2_made, t)
                if n + 3 < TILES:
                    pe.wait_ge(var1_made, t + 4)
                for k in range(FC):
                    mm = nc.tensor.matmul(out_ps[:, 1, :], fT[:, slot, k, :], keep["f2_w"][:, k, :], start=(k == 0), stop=(k == FC - 1))
                mm.then_inc(f_out_done, 1)

            def gates(t, slot, n):
                pe.wait_ge(h2T_copied, t + 1)
                if n:
                    pe.wait_ge(rz_made, t)
                by_feature(rz_ps, w_rz, 2 * KC, 0, h2T, slot).then_inc(rz_done, 1)
                if n:
                    pe.wait_ge(rn_made, t)
                by_feature(n_ps[:, 1], keep["w_hh"], KC, 2 * D, h2T, slot)
                by_feature(n_ps[:, 0], keep["w_ih"], KC, 2 * D, h2T, slot).then_inc(n_done, 1)

            pe.wait_ge(table_made, 1)
            over_steps(pe, plain, general, [[(transpose_attn, 1), (up, 3)], [(transpose_y, 8), (project, 1), (transpose_h1, 2)],
                                            [(transpose_h2, 5), (down, 4), (gates, 6)]])


EXPERTS, HIDDEN, TOP = 8, 1024, 2
HC = HIDDEN // P
SG = 2
SROWS = SG * P
MAX_SG = (TOP * NODES + EXPERTS * SROWS) // SROWS
SLOT_TILES = MAX_SG * SG
FAR = -3e38
MOE_KEPT = dict(wg=[P, KC, EXPERTS], bg=[P, EXPERTS], b1=[P, EXPERTS * HC], b2=[P, EXPERTS, D])


class Weights:
    def __init__(self, nc, ctx, w1_in, w2_in):
        sb = lambda name, shape: ctx.enter_context(nc.sbuf_tensor(name, shape, F32))
        self.nc, self.w1_in, self.w2_in = nc, w1_in, w2_in
        self.w1_whole, self.w2_whole = sb("w1_whole", [P, KC, HIDDEN]), sb("w2_whole", [P, HC, D])
        self.w1, self.w2 = sb("w1", [P, 2, PARTS, KC, HIDDEN]), sb("w2", [P, 2, PARTS, HC, D])
        self.loaded, self.high_made, self.split_made = [
            ctx.enter_context(nc.semaphore(f"weights_{name}")) for name in ("loaded", "high_made", "split_made")]

    def load(self, sp, e):
        sp.dma_start(self.w1_whole[:, :, :], self.w1_in[bass.ds(e, 1), :, :, :].rearrange("a p c h -> p (a c) h")).then_inc(self.loaded, 16)
        sp.dma_start(self.w2_whole[:, :, :], self.w2_in[bass.ds(e, 1), :, :, :].rearrange("a p c h -> p (a c) h")).then_inc(self.loaded, 16)

    def make_high(self, act, e, slot):
        act.wait_ge(self.loaded, e * 32 + 32)
        self.nc.scalar.activation(self.w1[:, slot, 0, :, :].bitcast(F32R), self.w1_whole[:, :, :], ACT.Copy).then_inc(self.high_made, 1)

    def make_rest(self, dve, e, slot):
        dve.wait_ge(self.loaded, e * 32 + 32)
        self.nc.vector.tensor_copy(self.w2[:, slot, 0, :, :].bitcast(F32R), self.w2_whole[:, :, :])
        dve.wait_ge(self.high_made, e + 1)
        self.nc.vector.tensor_tensor(self.w1[:, slot, 1, :, :].bitcast(F32R), self.w1_whole[:, :, :], self.w1[:, slot, 0, :, :], ALU.subtract)
        dve.drain()
        self.nc.vector.tensor_tensor(self.w2[:, slot, 1, :, :].bitcast(F32R), self.w2_whole[:, :, :], self.w2[:, slot, 0, :, :], ALU.subtract)
        dve.drain().then_inc(self.split_made, 1)


def route_phase(nc, X, XN, xn_dram, prob, take, put, groups, weights, ins, keep):
    with ExitStack() as ctx:
        sb = lambda name, shape, dt=F32: ctx.enter_context(nc.sbuf_tensor("route_" + name, shape, dt))
        sem = lambda name: ctx.enter_context(nc.semaphore("route_" + name))
        psum = lambda name, shape: ctx.enter_context(nc.psum_tensor("route_" + name, shape, F32))
        ident, wg, bg = keep["ident"], keep["wg"], keep["bg"]
        stats = sb("stats", [P, TILES, 6])
        moments = sb("moments", [P, TILES, 2])
        std = sb("std", [P, TILES])
        rstd = sb("rstd", [P, TILES])
        xn = sb("xn", [P, SLOTS, D])
        xnT = sb("xnT", [P, SLOTS, KC, P])
        gate = sb("gate", [P, TILES, EXPERTS])
        cand = sb("cand", [P, TILES, EXPERTS])
        chosen = sb("chosen", [P, TOP, TILES, EXPERTS])
        either = sb("either", [P, TILES, EXPERTS])
        best = sb("best", [P, TOP, TILES])
        top = sb("top", [P, TILES])
        ratio = sb("ratio", [P, TILES])
        scan = sb("scan", [P, 2, TILES, EXPERTS])
        rank = sb("rank", [P, TILES, EXPERTS])
        node = sb("node", [P, TILES])
        valid = sb("valid", [P, TILES])
        spare = sb("spare", [P, SLOT_TILES])
        column = sb("column", [P, P])
        place_i = sb("place_i", [P, TOP, TILES], I32)
        slot_tile = sb("slot_tile", [P, TOP, TILES])
        slot_row = sb("slot_row", [P, TOP, TILES])
        token = sb("token", [P, TOP, TILES])
        row_onehot = sb("row_onehot", [P, TOP, TILES, P])
        token_at = sb("token_at", [P, TOP, TILES, SLOT_TILES])
        used = sb("used", [P, SLOT_TILES])
        from_row = sb("from_row", [P, SLOT_TILES])
        to_row = sb("to_row", [P, SLOT_TILES])
        order = sb("order", [P, EXPERTS])
        below = sb("below", [P, P])
        ones = sb("ones", [P, P])
        number = sb("number", [P, EXPERTS])
        number_i = sb("number_i", [P, EXPERTS], I32)
        starts = sb("starts", [P, 2, EXPERTS])
        place_f = sb("place_f", [P, TOP, TILES])
        xnT_ps = psum("xnT_ps", [P, SLOTS, 512])
        gate_ps = psum("gate_ps", [P, 512])
        prefix_ps = psum("prefix_ps", [P, 512])
        count_ps = psum("count_ps", [P, 512])
        slots_ps = psum("slots_ps", [P, 512])
        var_made, xn_kept = sem("var_made"), sem("xn_kept")
        std_made, norm_made = sem("std_made"), sem("norm_made")
        xnT_done, xnT_copied, gate_done = sem("xnT_done"), sem("xnT_copied"), sem("gate_done")
        iotas_made, either_made, counted = sem("iotas_made"), sem("either_made"), sem("counted")
        margin_made, ratio_made = sem("margin_made"), sem("ratio_made")
        onehots_made, slots_done, xn_stored = sem("onehots_made"), sem("slots_done"), sem("xn_stored")
        kept_loaded = sem("kept_loaded")
        block = ctx.enter_context(nc.Block())

        @block.sync
        def _(sp):
            load_kept(sp, MOE_KEPT, ins, keep, kept_loaded)
            weights.load(sp, 0)
            rows = xn_dram.rearrange("(t p) d -> p t d", p=P)
            for n in range(X_LOADS):
                part = slice(n * X_TILES, (n + 1) * X_TILES)
                sp.wait_ge(xn_kept, (n + 1) * X_TILES)
                sp.dma_start(rows[:, part, :], XN[:, part, :]).then_inc(xn_stored, 16)
            sp.wait_ge(weights.split_made, 1)
            weights.load(sp, 1)
            sp.wait_ge(xn_stored, 16 * X_LOADS)

        @block.vector
        def _(dve):
            def moments_of(n):
                for t in range(n * X_TILES, (n + 1) * X_TILES):
                    nc.vector.bn_stats(stats[:, t, :], X[:, t, :])
                dve.drain()
                for t in range(n * X_TILES, (n + 1) * X_TILES):
                    nc.vector.bn_aggr(moments[:, t, :], stats[:, t, :])
                dve.drain().then_inc(var_made, 1)

            moments_of(0)
            for n in range(X_LOADS):
                if n + 1 < X_LOADS:
                    moments_of(n + 1)
                dve.wait_ge(std_made, n + 1)
                nc.vector.reciprocal(rstd[:, n * X_TILES:(n + 1) * X_TILES], std[:, n * X_TILES:(n + 1) * X_TILES])
                dve.drain()
                for t in range(n * X_TILES, (n + 1) * X_TILES):
                    if t >= SLOTS:
                        dve.wait_ge(xnT_done, t - SLOTS + 1)
                        dve.wait_ge(xn_kept, t - SLOTS + 1)
                    nc.vector.tensor_scalar(xn[:, t % SLOTS, :], X[:, t, :], moments[:, t, 0:1], rstd[:, t:t + 1],
                                            ALU.subtract, ALU.mult).then_inc(norm_made, 1)

            full = [P, TILES, EXPERTS]
            dve.wait_ge(gate_done, TILES)
            dve.wait_ge(iotas_made, 1)
            nc.vector.tensor_tensor(gate[:, :, :], gate_ps[:, 0:TILES * EXPERTS].rearrange("p (t e) -> p t e", e=EXPERTS), bcast(bg[:, :], 1, full), ALU.add)
            nc.vector.tensor_scalar(valid[:, :], node[:, :], float(NODES), None, ALU.is_lt)
            nc.vector.tensor_scalar(below[:, :], below[:, :], 0.0, None, ALU.is_gt)
            nc.vector.memset(ones[:, :], 1.0)
            dve.drain()
            for c in range(TOP):
                nc.vector.tensor_reduce(best[:, c, :], gate[:, :, :], AX.X, ALU.max)
                dve.drain()
                nc.vector.tensor_tensor(cand[:, :, :], gate[:, :, :], bcast(best[:, c, :], 2, full), ALU.is_equal)
                dve.drain()
                nc.vector.tensor_tensor(cand[:, :, :], cand[:, :, :], bcast(order[:, :], 1, full), ALU.mult)
                dve.drain()
                nc.vector.tensor_reduce(top[:, :], cand[:, :, :], AX.X, ALU.max)
                dve.drain()
                nc.vector.tensor_tensor(chosen[:, c, :, :], cand[:, :, :], bcast(top[:, :], 2, full), ALU.is_equal)
                dve.drain()
                if c + 1 < TOP:
                    nc.vector.scalar_tensor_tensor(gate[:, :, :], chosen[:, c, :, :], FAR, gate[:, :, :], ALU.mult, ALU.add)
                nc.vector.tensor_tensor(chosen[:, c, :, :], chosen[:, c, :, :], bcast(valid[:, :], 2, full), ALU.mult)
                dve.drain()
            nc.vector.tensor_tensor(either[:, :, :], chosen[:, 0, :, :], chosen[:, 1, :, :], ALU.add).then_inc(either_made, 1)
            nc.vector.tensor_tensor(ratio[:, :], best[:, 1, :], best[:, 0, :], ALU.subtract).then_inc(margin_made, 1)

            dve.wait_ge(counted, 1)
            tile_counts = count_ps[:, 0:TILES * EXPERTS].rearrange("p (t e) -> p t e", e=EXPERTS)
            nc.vector.tensor_copy(scan[:, 0, :, :], tile_counts)
            dve.drain()
            now, reach = 0, 1
            while reach < TILES:
                nc.vector.tensor_copy(scan[:, 1 - now, 0:reach, :], scan[:, now, 0:reach, :])
                nc.vector.tensor_tensor(scan[:, 1 - now, reach:, :], scan[:, now, reach:, :], scan[:, now, 0:TILES - reach, :], ALU.add)
                dve.drain()
                now, reach = 1 - now, 2 * reach
            nc.vector.tensor_tensor(rank[:, :, :], scan[:, now, :, :], tile_counts, ALU.subtract)
            nc.vector.tensor_scalar(number[:, :], scan[:, now, TILES - 1, :], float(SROWS - 1), None, ALU.add)
            dve.drain()
            nc.vector.tensor_tensor(rank[:, :, :], rank[:, :, :], prefix_ps[:, 0:TILES * EXPERTS].rearrange("p (t e) -> p t e", e=EXPERTS), ALU.add)
            nc.vector.tensor_copy(number_i[:, :], number[:, :])
            dve.drain()
            nc.vector.tensor_scalar(number_i[:, :], number_i[:, :], SROWS.bit_length() - 1, None, ALU.arith_shift_right)
            dve.drain()
            nc.vector.tensor_scalar(number[:, :], number_i[:, :], 1.0, None, ALU.max)
            dve.drain()
            nc.vector.tensor_copy(starts[:, 0, :], number[:, :])
            dve.drain()
            now, reach = 0, 1
            while reach < EXPERTS:
                nc.vector.tensor_copy(starts[:, 1 - now, 0:reach], starts[:, now, 0:reach])
                nc.vector.tensor_tensor(starts[:, 1 - now, reach:], starts[:, now, reach:], starts[:, now, 0:EXPERTS - reach], ALU.add)
                dve.drain()
                now, reach = 1 - now, 2 * reach
            nc.vector.tensor_tensor(starts[:, now, :], starts[:, now, :], number[:, :], ALU.subtract)
            dve.drain()
            nc.vector.tensor_copy(groups[:, 0:EXPERTS], number[:, :])
            nc.vector.tensor_copy(groups[:, EXPERTS:2 * EXPERTS], starts[:, now, :])
            nc.vector.tensor_scalar(starts[:, now, :], starts[:, now, :], float(SROWS), None, ALU.mult)
            dve.drain()
            nc.vector.tensor_tensor(rank[:, :, :], rank[:, :, :], bcast(starts[:, now, :], 1, full), ALU.add)
            dve.drain()
            for c in range(TOP):
                nc.vector.tensor_tensor(cand[:, :, :], rank[:, :, :], chosen[:, c, :, :], ALU.mult)
                dve.drain()
                nc.vector.tensor_reduce(place_f[:, c, :], cand[:, :, :], AX.X, ALU.add)
                dve.drain()
            nc.vector.tensor_copy(place_i[:, :, :], place_f[:, :, :])
            dve.drain()
            nc.vector.tensor_scalar(place_i[:, :, :], place_i[:, :, :], P.bit_length() - 1, None, ALU.arith_shift_right)
            dve.drain()
            nc.vector.tensor_copy(slot_tile[:, :, :], place_i[:, :, :])
            for c in range(TOP):
                nc.vector.scalar_tensor_tensor(token[:, c, :], node[:, :], float(c * NPAD + 1), valid[:, :], ALU.add, ALU.mult)
            dve.drain()
            nc.vector.scalar_tensor_tensor(slot_row[:, :, :], slot_tile[:, :, :], -float(P), place_f[:, :, :], ALU.mult, ALU.add)
            dve.drain()
            for c in range(TOP):
                nc.vector.tensor_tensor(row_onehot[:, c, :, :], bcast(column[:, :], 1, [P, TILES, P]), bcast(slot_row[:, c, :], 2, [P, TILES, P]), ALU.is_equal)
                shape = [P, TILES, SLOT_TILES]
                nc.vector.tensor_tensor(token_at[:, c, :, :], bcast(column[:, 0:SLOT_TILES], 1, shape), bcast(slot_tile[:, c, :], 2, shape), ALU.is_equal)
                dve.drain()
                nc.vector.tensor_tensor(token_at[:, c, :, :], token_at[:, c, :, :], bcast(token[:, c, :], 2, shape), ALU.mult)
                dve.drain().then_inc(onehots_made, 1)
            dve.wait_ge(ratio_made, 1)
            nc.vector.tensor_scalar(top[:, :], ratio[:, :], 1.0, None, ALU.add)
            dve.drain()
            nc.vector.reciprocal(top[:, :], top[:, :])
            dve.drain()
            nc.vector.tensor_copy(prob[:, :, 0], top[:, :])
            nc.vector.tensor_tensor(prob[:, :, 1], top[:, :], ratio[:, :], ALU.mult)
            weights.make_rest(dve, 0, 0)
            dve.wait_ge(slots_done, 1)
            nc.vector.tensor_scalar(used[:, :], slots_ps[:, 0:SLOT_TILES], 0.0, None, ALU.is_gt)
            nc.vector.scalar_tensor_tensor(to_row[:, :], slots_ps[:, 0:SLOT_TILES], -1.0, spare[:, :], ALU.add, ALU.subtract)
            nc.vector.tensor_scalar(from_row[:, :], slots_ps[:, 0:SLOT_TILES], float(NPAD), -float(NPAD), ALU.is_gt, ALU.mult)
            nc.vector.memset(take[:, SLOT_TILES:], 0)
            dve.drain()
            nc.vector.tensor_tensor(from_row[:, :], from_row[:, :], slots_ps[:, 0:SLOT_TILES], ALU.add)
            nc.vector.tensor_tensor(to_row[:, :], to_row[:, :], used[:, :], ALU.mult)
            dve.drain()
            nc.vector.tensor_scalar(take[:, 0:SLOT_TILES], from_row[:, :], -1.0, 0.0, ALU.add, ALU.max)
            nc.vector.tensor_tensor(put[:, :], to_row[:, :], spare[:, :], ALU.add)

        @block.scalar
        def _(act):
            def copy(t, slot, n):
                act.wait_ge(xnT_done, t + 1)
                if n >= SLOTS:
                    act.wait_ge(gate_done, t - SLOTS + 1)
                nc.scalar.activation(xnT[:, slot, :, :].rearrange("p c n -> p (c n)"), xnT_ps[:, slot, 0:D], ACT.Copy).then_inc(xnT_copied, 1)
            for n in range(X_LOADS):
                part = slice(n * X_TILES, (n + 1) * X_TILES)
                act.wait_ge(var_made, n + 1)
                nc.scalar.activation(std[:, part], moments[:, part, 1:2].rearrange("p t a -> p (t a)"), ACT.Sqrt, bias=keep["eps"][:, 0:1]).then_inc(std_made, 1)
                for t in range(n * X_TILES, (n + 1) * X_TILES):
                    copy(t, t % SLOTS, t)

            act.wait_ge(margin_made, 1)
            nc.scalar.activation(ratio[:, :], ratio[:, :], ACT.Exp).then_inc(ratio_made, 1)
            weights.make_high(act, 0, 0)

        @block.tensor
        def _(pe):
            def transpose(t, slot, n):
                pe.wait_ge(norm_made, t + 1)
                if n >= SLOTS:
                    pe.wait_ge(xnT_copied, t - SLOTS + 1)
                for c in range(KC):
                    mm = nc.tensor.transpose(xnT_ps[:, slot, c * P:(c + 1) * P], xn[:, slot, c * P:(c + 1) * P], ident[:, :])
                mm.then_inc(xnT_done, 1)

            def score(t, slot, n):
                pe.wait_ge(xnT_copied, t + 1)
                for c in range(KC):
                    mm = nc.tensor.matmul(gate_ps[:, bass.ds(t * EXPERTS, EXPERTS)], xnT[:, slot, c, :], wg[:, c, :], start=(c == 0), stop=(c == KC - 1))
                mm.then_inc(gate_done, 1)
            pe.wait_ge(kept_loaded, 16 * len(MOE_KEPT))
            pipeline(pe, TILES, SLOTS, [(transpose, 0), (score, 1)])
            pe.wait_ge(either_made, 1)
            flat = either[:, :, :].rearrange("p t e -> p (t e)")
            nc.tensor.matmul(prefix_ps[:, 0:TILES * EXPERTS], below[:, :], flat, start=True, stop=True)
            nc.tensor.matmul(count_ps[:, 0:TILES * EXPERTS], ones[:, :], flat, start=True, stop=True).then_inc(counted, 1)
            for c in range(TOP):
                pe.wait_ge(onehots_made, c + 1)
                for t in range(TILES):
                    mm = nc.tensor.matmul(slots_ps[:, 0:SLOT_TILES], row_onehot[:, c, t, :], token_at[:, c, t, :],
                                          start=(c == 0 and t == 0), stop=(c == TOP - 1 and t == TILES - 1))
            mm.then_inc(slots_done, 1)

        @block.gpsimd
        def _(pool):
            f = dict(allow_small_or_imprecise_dtypes=True)
            nc.gpsimd.iota(node[:, :], [[P, TILES]], base=0, channel_multiplier=1, **f)
            nc.gpsimd.iota(spare[:, :], [[0, MAX_SG], [P, SG]], base=TOP * NPAD, channel_multiplier=1, **f)
            nc.gpsimd.iota(order[:, :], [[-1, EXPERTS]], base=EXPERTS, channel_multiplier=0, **f)
            nc.gpsimd.iota(column[:, :], [[1, P]], base=0, channel_multiplier=0, **f)
            nc.gpsimd.iota(below[:, :], [[1, P]], base=0, channel_multiplier=-1, **f).then_inc(iotas_made, 1)

            def keep_xn(t, slot, n):
                pool.wait_ge(norm_made, t + 1)
                nc.gpsimd.tensor_copy(tile_of(XN, t), xn[:, slot, :]).then_inc(xn_kept, 1)
            pipeline(pool, TILES, SLOTS, [(keep_xn, 0)])


def expert_phase(nc, xn_dram, y_dram, weights, take, put, groups, keep):
    with ExitStack() as ctx:
        sb = lambda name, shape, dt=F32: ctx.enter_context(nc.sbuf_tensor("moe_" + name, shape, dt))
        sem = lambda name: ctx.enter_context(nc.semaphore("moe_" + name))
        psum = lambda name, shape: ctx.enter_context(nc.psum_tensor("moe_" + name, shape, F32))
        ident, b1, b2 = keep["ident"], keep["b1"], keep["b2"]
        w1, w2 = weights.w1, weights.w2
        x = sb("x", [P, SG, D])
        xT = sb("xT", [P, PARTS, KC, SROWS])
        hT_whole = sb("hT_whole", [P, HC, SROWS])
        hT = sb("hT", [P, PARTS, HC, SROWS])
        y = sb("y", [P, SG, D])
        HB = 4
        h_ps = psum("h_ps", [P, HB, 512])
        xT_ps = psum("xT_ps", [P, KC, SROWS])
        y_ps = psum("y_ps", [P, SG, D])
        h_split, xT_high = sem("h_split"), sem("xT_high")
        x_loaded, xT_done, xT_copied = sem("x_loaded"), sem("xT_done"), sem("xT_copied")
        h_done, h_made, y_done, y_made, y_stored = sem("h_done"), sem("h_made"), sem("y_done"), sem("y_made"), sem("y_stored")
        expert_done, take_made, put_made, y_free = sem("expert_done"), sem("take_made"), sem("put_made"), sem("y_free")
        take_index = sb("take_index", [P, SG], I32)
        put_index = sb("put_index", [P, SG], I32)
        weights_seen, ends_seen = sem("weights_seen"), sem("ends_seen")
        block = ctx.enter_context(nc.Block())

        def span(eng, e):
            count = eng.value_load(groups[0:1, bass.ds(e, 1)], min_val=1, max_val=MAX_SG)
            before = eng.value_load(groups[0:1, bass.ds(e + EXPERTS, 1)], min_val=0, max_val=MAX_SG - 1)
            return count, before

        def over_experts(eng, body):
            with eng.Fori(0, EXPERTS // 2 - 1) as k:
                body(2 * k, 0, True)
                body(2 * k + 1, 1, True)
            body(EXPERTS - 2, 0, True)
            body(EXPERTS - 1, 1, False)

        @block.sync
        def _(sp):
            with sp.Fori(2, EXPERTS) as e:
                sp.wait_ge(weights.split_made, e)
                weights.load(sp, e)

        @block.gpsimd
        def _(pool):
            def fetch(q):
                nc.gpsimd.tensor_copy(take_index[:, :], take[:, bass.ds(q * SG, SG)]).then_inc(take_made, 1)
                pool.wait_ge(take_made, q + 1)
                pool.sem_inc(ends_seen, 1)
                for i in range(SG):
                    nc.gpsimd.indirect_dma_start(out=x[:, i, :], out_offset=None, in_=xn_dram,
                                                 in_offset=bass.IndirectOffsetOnAxis(ap=take_index[:, i:i + 1].bitcast(U32), axis=0)).then_inc(x_loaded, 16)

            def give(q):
                nc.gpsimd.tensor_copy(put_index[:, :], put[:, bass.ds(q * SG, SG)]).then_inc(put_made, 1)
                pool.wait_ge(put_made, q + 1)
                pool.sem_inc(ends_seen, 1)
                for i in range(SG):
                    nc.gpsimd.indirect_dma_start(out=y_dram, out_offset=bass.IndirectOffsetOnAxis(ap=put_index[:, i:i + 1].bitcast(U32), axis=0),
                                                 in_=y[:, i, :], in_offset=None).then_inc(y_stored, 16)

            pool.sem_inc(y_free, 1)
            count, before = span(pool, EXPERTS - 1)
            fetch(0)
            pool.wait_ge(xT_done, 1)
            fetch(1)
            with pool.Fori(0, before + count) as i:
                q = nc.s_assert_within(i, 0, MAX_SG - 1, skip_runtime_bounds_check_because="no routing fills more groups")
                pool.wait_ge(xT_done, q + 2)
                fetch(q + 2)
                pool.wait_ge(y_made, q + 1)
                give(q)
                pool.wait_ge(y_stored, q * (16 * SG) + 16 * SG)
                pool.sem_inc(y_free, 1)
            pool.wait_ge(x_loaded, (before + count) * (16 * SG) + 2 * 16 * SG)
            pool.sem_inc(ends_seen, 1)

        @block.tensor
        def _(pe):
            def transpose(q):
                pe.wait_ge(x_loaded, q * (16 * SG) + 16 * SG)
                for c in range(KC):
                    for i in range(SG):
                        mm = nc.tensor.transpose(xT_ps[:, c, i * P:(i + 1) * P], x[:, i, c * P:(c + 1) * P], ident[:, :])
                mm.then_inc(xT_done, 1)

            def expert(e, slot, more):
                count, before = span(pe, e)
                pe.wait_ge(weights.split_made, e + 1)
                pe.sem_inc(weights_seen, 1)
                with pe.Fori(0, count) as j:
                    q = before + j
                    pe.wait_ge(xT_copied, q + 1)
                    for k in range(HC):
                        if k >= HB:
                            pe.wait_ge(h_made, q * HC + k - HB + 1)
                        for c in range(KC):
                            for a, b in PRODUCTS:
                                mm = nc.tensor.matmul(h_ps[:, k % HB, 0:SROWS], w1[:, slot, a, c, k * P:(k + 1) * P].bitcast(F32R), xT[:, b, c, :].bitcast(F32R),
                                                      start=(c == 0 and (a, b) == PRODUCTS[0]), stop=(c == KC - 1 and (a, b) == PRODUCTS[-1]))
                        mm.then_inc(h_done, 1)
                    transpose(q + 1)
                    for i in range(SG):
                        for k in range(HC):
                            if i == 0:
                                pe.wait_ge(h_split, q * HC + k + 1)
                            for a, b in PRODUCTS:
                                mm = nc.tensor.matmul(y_ps[:, i, :], hT[:, a, k, i * P:(i + 1) * P].bitcast(F32R), w2[:, slot, b, k, :].bitcast(F32R),
                                                      start=(k == 0 and (a, b) == PRODUCTS[0]), stop=(k == HC - 1 and (a, b) == PRODUCTS[-1]))
                    mm.then_inc(y_done, 1)
                pe.drain().then_inc(expert_done, 1)
            pe.sem_inc(expert_done, 1)
            transpose(0)
            over_experts(pe, expert)

        @block.scalar
        def _(act):
            def copy_xT(q):
                act.wait_ge(xT_done, q + 1)
                nc.scalar.activation(xT[:, 0, :, :].bitcast(F32R), xT_ps[:, :, :], ACT.Copy).then_inc(xT_high, 1)

            def expert(e, slot, more):
                if more:
                    act.wait_ge(expert_done, e + 1)
                    act.sem_inc(weights_seen, 1)
                    weights.make_high(act, e + 1, 1 - slot)
                count, before = span(act, e)
                with act.Fori(0, count) as j:
                    q = before + j
                    for k in range(HC):
                        act.wait_ge(h_done, q * HC + k + 1)
                        nc.scalar.activation(hT_whole[:, k, :], h_ps[:, k % HB, 0:SROWS], ACT.Relu, bias=b1[:, bass.ds(e * HC + k, 1)]).then_inc(h_made, 1)
                    copy_xT(q + 1)
                    act.wait_ge(h_split, q * HC + HC)
            copy_xT(0)
            over_experts(act, expert)

        @block.vector
        def _(dve):
            def split_xT(q):
                dve.wait_ge(xT_high, q + 1)
                nc.vector.tensor_tensor(xT[:, 1, :, :].bitcast(F32R), xT_ps[:, :, :], xT[:, 0, :, :], ALU.subtract).then_inc(xT_copied, 1)

            def expert(e, slot, more):
                if more:
                    dve.wait_ge(expert_done, e + 1)
                    dve.sem_inc(weights_seen, 1)
                    weights.make_rest(dve, e + 1, 1 - slot)
                count, before = span(dve, e)
                with dve.Fori(0, count) as j:
                    q = before + j
                    for k in range(HC):
                        dve.wait_ge(h_made, q * HC + k + 1)
                        nc.vector.tensor_copy(hT[:, 0, k, :].bitcast(F32R), hT_whole[:, k, :])
                        dve.drain()
                        nc.vector.tensor_tensor(hT[:, 1, k, :].bitcast(F32R), hT_whole[:, k, :], hT[:, 0, k, :], ALU.subtract).then_inc(h_split, 1)
                    split_xT(q + 1)
                    dve.wait_ge(y_done, q + 1)
                    dve.wait_ge(y_free, q + 1)
                    nc.vector.tensor_tensor(y[:, :, :], y_ps[:, :, :],
                                            b2[:, bass.ds(e, 1), :].broadcast_to([P, SG, D]), ALU.add).then_inc(y_made, 1)
            split_xT(0)
            over_experts(dve, expert)


def combine_phase(nc, X, y_dram, prob, out):
    with ExitStack() as ctx:
        sb = lambda name, shape, dt=F32: ctx.enter_context(nc.sbuf_tensor("sum_" + name, shape, dt))
        sem = lambda name: ctx.enter_context(nc.semaphore("sum_" + name))
        y = sb("y", [P, TOP, TILES, D])
        y_loaded = [sem(f"y_loaded_{n}") for n in range(X_LOADS)]
        result_made, stored = sem("result_made"), sem("stored")
        block = ctx.enter_context(nc.Block())
        part = lambda n: slice(n * X_TILES, (n + 1) * X_TILES)

        def load(eng, c):
            rows = y_dram[c * NPAD:(c + 1) * NPAD, :].rearrange("(t p) d -> p t d", p=P)
            for n in range(X_LOADS):
                eng.dma_start(y[:, c, part(n), :], rows[:, part(n), :]).then_inc(y_loaded[n], 16)

        @block.sync
        def _(sp):
            load(sp, 0)
            rows = out.rearrange("(t p) d -> p t d", p=P)
            for n in range(X_LOADS):
                sp.wait_ge(result_made, n + 1)
                sp.dma_start(rows[:, part(n), :], X[:, part(n), :]).then_inc(stored, 16)
            sp.wait_ge(stored, 16 * X_LOADS)

        @block.scalar
        def _(act):
            load(act, 1)

        @block.vector
        def _(dve):
            for n in range(X_LOADS):
                dve.wait_ge(y_loaded[n], 16 * TOP)
                for c in range(TOP):
                    for t in range(n * X_TILES, (n + 1) * X_TILES):
                        nc.vector.scalar_tensor_tensor(X[:, t, :], y[:, c, t, :], prob[:, t, c:c + 1], X[:, t, :], ALU.mult, ALU.add)
                    dve.drain()
                dve.drain().then_inc(result_made, 1)


def build_program(nc, ins, out):
    x1_dram = nc.dram_tensor("x1_rows", [NPAD, D], F32).ap()
    xn_dram = nc.dram_tensor("xn_rows", [NPAD, D], F32).ap()
    y_dram = nc.dram_tensor("y_rows", [TOP * NPAD + SG * P, D], F32).ap()
    with ExitStack() as ctx:
        sb = lambda name, shape, dt=F32: ctx.enter_context(nc.sbuf_tensor(name, shape, dt))
        X, XN = sb("X", [P, TILES, D]), sb("XN", [P, TILES, D])
        prob = sb("prob", [P, TILES, TOP])
        take = sb("take", [P, SLOT_TILES + 2 * SG], I32)
        put = sb("put", [P, SLOT_TILES], I32)
        groups = sb("groups", [P, 2 * EXPERTS], I32)
        keep = dict(ident=sb("ident", [P, P]), eps=sb("eps", [P, 1]), O_b=sb("O_b", [P, D]))
        with ExitStack() as gnn:
            X1 = gnn.enter_context(nc.sbuf_tensor("X1", [P, TILES, D], F32))
            S = gnn.enter_context(nc.sbuf_tensor("S", [P, TILES + 1, D], F32))
            edge = {name: gnn.enter_context(nc.sbuf_tensor(name, shape, F32)) for name, shape in dict(
                dst_f=[P, COLS + AHEAD * GE],
                ends=[P, 2, GROUPS],
                iota_w=[P, WINDOW], iota_more=[P, 1 + TILES // 2]).items()}
            attention_phase(nc, X, XN, X1, S, ins["x"], ins["w_qkv"], x1_dram, y_dram, edge, ins, keep)
            for name, shape in GNN_KEPT.items():
                keep[name] = gnn.enter_context(nc.sbuf_tensor(name, shape, F32))
            graph_phase(nc, X, XN, X1, S, x1_dram, edge, ins, keep)
        for name, shape in MOE_KEPT.items():
            keep[name] = sb(name, shape)
        with ExitStack() as moe:
            weights = Weights(nc, moe, ins["w1"], ins["w2"])
            route_phase(nc, X, XN, xn_dram, prob, take, put, groups, weights, ins, keep)
            expert_phase(nc, xn_dram, y_dram, weights, take, put, groups, keep)
        combine_phase(nc, X, y_dram, prob, out)


def kernel(x, src, dst, L0_gnn_Wq, L0_gnn_Wk, L0_gnn_Wv, L0_gnn_O_w, L0_gnn_O_b, L0_gnn_ln1_w, L0_gnn_ln1_b,
           L0_gnn_f1_w, L0_gnn_f1_b, L0_gnn_f2_w, L0_gnn_f2_b, L0_gnn_ln2_w, L0_gnn_ln2_b, L0_gnn_gru_w_ih,
           L0_gnn_gru_w_hh, L0_gnn_gru_b_ih, L0_gnn_gru_b_hh, L0_ffn_Wg, L0_ffn_bg, L0_ffn_W1, L0_ffn_b1,
           L0_ffn_W2, L0_ffn_b2):
    import numpy as np
    import concourse.bacc as bacc
    from concourse.bass_utils import run_bass_kernel_spmd as run

    def by_tile(a):
        return np.asarray(a).reshape(-1, P, a.shape[-1]).transpose(1, 0, 2)

    def by_chunk(a):
        return np.asarray(a).reshape(-1, P).T

    def repeated(a):
        return np.broadcast_to(np.asarray(a), (P,) + a.shape)

    def edges(a, fill):
        return np.concatenate([np.asarray(a), np.full(COLS * P - EDGES, fill, np.int32)]).reshape(COLS, P).T

    x_padded = np.concatenate([np.asarray(x), np.zeros((NPAD - NODES, D), np.float32)])
    qkv = np.concatenate([np.asarray(L0_gnn_Wq), np.asarray(L0_gnn_Wk), np.asarray(L0_gnn_Wv)], 1)
    arrays = dict(
        x=by_tile(x_padded), w_qkv=by_tile(qkv), ident=np.eye(P, dtype=np.float32),
        src=edges(src, 0), dst=edges(dst, NPAD - 1),
        O_w=by_tile(L0_gnn_O_w), O_b=repeated(L0_gnn_O_b), f1_w=by_tile(L0_gnn_f1_w), f1_b=by_chunk(L0_gnn_f1_b),
        f2_w=by_tile(L0_gnn_f2_w), f2_b=repeated(L0_gnn_f2_b),
        ln1_w=repeated(L0_gnn_ln1_w), ln1_b=repeated(L0_gnn_ln1_b), ln2_w=repeated(L0_gnn_ln2_w), ln2_b=repeated(L0_gnn_ln2_b),
        w_ih=by_tile(L0_gnn_gru_w_ih), w_hh=by_tile(L0_gnn_gru_w_hh), b_ih=by_chunk(L0_gnn_gru_b_ih), b_hh=by_chunk(L0_gnn_gru_b_hh),
        wg=by_tile(np.asarray(L0_ffn_Wg).T), bg=repeated(L0_ffn_bg),
        b1=by_chunk(np.asarray(L0_ffn_b1).reshape(-1)), b2=repeated(L0_ffn_b2),
        w1=np.asarray(L0_ffn_W1).transpose(0, 2, 1).reshape(EXPERTS, KC, P, HIDDEN).transpose(0, 2, 1, 3),
        w2=np.asarray(L0_ffn_W2).transpose(0, 2, 1).reshape(EXPERTS, HC, P, D).transpose(0, 2, 1, 3),
    )
    arrays = {f"in_{name}": np.ascontiguousarray(a) for name, a in arrays.items()}
    nc = bacc.Bacc("TRN2", target_bir_lowering=False, num_devices=1)
    ins = {name[3:]: nc.dram_tensor(name, a.shape, mybir.dt.from_np(a.dtype), kind="ExternalInput").ap() for name, a in arrays.items()}
    out = nc.dram_tensor("out", [NPAD, D], F32, kind="ExternalOutput").ap()
    build_program(nc, ins, out)
    result = run(nc, [arrays], core_ids=[0])
    return result.results[0]["out"][:NODES]
```
